# Optimizing a Trainium2 kernel written in Bass

```python
import numpy as np
import jax
import jax.numpy as jnp

def _softmax(x, axis=-1):
    return jax.nn.softmax(x, axis=axis)

def _gelu(x):
    return jax.nn.gelu(x, approximate=True)

def _silu(x):
    return jax.nn.silu(x)

def _sigmoid(x):
    return jax.nn.sigmoid(x)

def _layernorm(x, axis=-1, eps=1e-05):
    m = jnp.mean(x, axis=axis, keepdims=True)
    v = jnp.var(x, axis=axis, keepdims=True)
    return (x - m) / jnp.sqrt(v + eps)

def _scatter_add(tgt, idx, src, axis=0):
    return tgt.at[idx].add(src)

def _segment_sum(src, seg, n):
    return jax.ops.segment_sum(src, seg, n)
kernel_name = 'mk_xattn_ffn_d2_seqx_r4_b40b0f'

def setup_inputs(seed: int=0):
    np.random.seed(seed)
    _w = jnp.asarray

    def _rec_inputs():
        import jax
        import jax.numpy as jnp
        _rk = jax.random.key(seed)
        x = -0.0002928 + 1 * jax.random.normal(jax.random.fold_in(_rk, 1), (2, 1024, 256), jnp.float32)
        _lenS = 1024 - jax.random.randint(jax.random.fold_in(_rk, 7), (2,), 0, max(1, 1024 // 4) + 1, jnp.int32)
        _lenS2 = 77 - jax.random.randint(jax.random.fold_in(_rk, 8), (2,), 0, max(1, 77 // 4) + 1, jnp.int32)
        _ctx_1024P = jax.random.normal(jax.random.fold_in(_rk, 11), (2, 16, 256), jnp.float32)
        _ctx_1024c = jax.random.dirichlet(jax.random.fold_in(_rk, 511), 0.3 * jnp.ones((16,), jnp.float32), (2, 77))
        _ctx_1024t = jnp.einsum('bsk,bkd->bsd', _ctx_1024c, _ctx_1024P)
        _ctx_1024t = _ctx_1024t * jax.lax.rsqrt(jnp.mean(jnp.square(_ctx_1024t)) + 1e-12) * 0.953939
        ctx_1024 = -1.39393e-06 + 0.999914 * (_ctx_1024t + 0.3 * jax.random.normal(jax.random.fold_in(_rk, 611), (2, 77, 256), jnp.float32))
        _validS = jnp.arange(1024)[None, :] < _lenS[:, None]
        _validS2 = jnp.arange(77)[None, :] < _lenS2[:, None]
        _causal = jnp.tril(jnp.ones((1024, 1024), dtype=bool))
        mask_BxS2_bf1 = jnp.ones((2, 77), dtype=bool)
        return (x, ctx_1024, mask_BxS2_bf1)
    x, ctx_1024, mask_BxS2_bf1 = _rec_inputs()

    def _L0_xattn_setup():
        import jax, jax.numpy as jnp
        import numpy as np
        N_HEADS = 16

        def _rel_emb(table, len_q, len_k):
            P = (table.shape[0] - 1) // 2
            rel = jnp.arange(len_k)[None, :] - jnp.arange(len_q)[:, None]
            idx = jnp.clip(rel, -P, P) + P
            return table[idx]
        key = jax.random.key(seed)
        ks = jax.random.split(key, 13)
        B, S, E = (2, 512, 256)
        P = 128
        d = E // N_HEADS
        s = 0.02
        return {'q': jax.random.normal(ks[0], (B, S, E), jnp.float32), 'k': jax.random.normal(ks[1], (B, S, E), jnp.float32), 'v': jax.random.normal(ks[2], (B, S, E), jnp.float32), 'Wq': jax.random.normal(ks[3], (E, E), jnp.float32) * s, 'bq': jnp.zeros((E,), jnp.float32), 'Wk': jax.random.normal(ks[4], (E, E), jnp.float32) * s, 'bk': jnp.zeros((E,), jnp.float32), 'Wv': jax.random.normal(ks[5], (E, E), jnp.float32) * s, 'bv': jnp.zeros((E,), jnp.float32), 'Wo': jax.random.normal(ks[6], (E, E), jnp.float32) * s, 'bo': jnp.zeros((E,), jnp.float32), 'rk_table': jax.random.normal(ks[7], (2 * P + 1, d), jnp.float32) * s, 'rv_table': jax.random.normal(ks[8], (2 * P + 1, d), jnp.float32) * s}
    _L0_xattn_all = _L0_xattn_setup()
    _L0_xattn_in = {k: v for k, v in _L0_xattn_all.items() if k in ('Wq', 'bq', 'Wk', 'bk', 'Wv', 'bv', 'Wo', 'bo', 'rk_table', 'rv_table')}
    del _L0_xattn_all

    def _L0_ffn_setup():
        import jax, jax.numpy as jnp
        import numpy as np
        ALPHA = 1.702
        LIMIT = 7.0
        TOP_K = 2
        key = jax.random.key(seed)
        ks = jax.random.split(key, 4)
        B, S, H, E, I = (2, 256, 256, 8, 512)
        return {'hidden_states': jax.random.normal(ks[0], (B, S, H), jnp.float32), 'router_weight': jax.random.normal(ks[1], (E, H), jnp.float32), 'router_bias': jnp.zeros((E,), jnp.float32), 'gate_up_proj': jax.random.normal(ks[2], (E, H, 2 * I), jnp.float32) * 0.02, 'gate_up_bias': jnp.zeros((E, 2 * I), jnp.float32), 'down_proj': jax.random.normal(ks[3], (E, I, H), jnp.float32) * 0.02, 'down_bias': jnp.zeros((E, H), jnp.float32)}
    _L0_ffn_all = _L0_ffn_setup()
    _L0_ffn_in = {k: v for k, v in _L0_ffn_all.items() if k in ('router_weight', 'router_bias', 'gate_up_proj', 'gate_up_bias', 'down_proj', 'down_bias')}
    del _L0_ffn_all

    def _L1_xattn_setup():
        import jax, jax.numpy as jnp
        import numpy as np
        DIM = 256
        DIM_LATENT = 256
        DIM_HEAD = 64
        HEADS = 16
        INNER = HEADS * DIM_HEAD

        def layernorm(x, g, b, eps=1e-05):
            m = jnp.mean(x, axis=-1, keepdims=True)
            v = jnp.mean((x - m) ** 2, axis=-1, keepdims=True)
            return (x - m) / jnp.sqrt(v + eps) * g + b

        def rmsnorm(x, gamma, eps=1e-08):
            n = jnp.linalg.norm(x, axis=-1, keepdims=True) * x.shape[-1] ** (-0.5)
            return x / jnp.maximum(n, eps) * gamma
        key = jax.random.key(seed)
        ks = jax.random.split(key, 8)
        b, n, m = (4, 1024, 128)
        x = jax.random.normal(ks[0], (b, n, DIM), dtype=jnp.float32)
        latents = jax.random.normal(ks[1], (b, m, DIM_LATENT), dtype=jnp.float32)
        mask = jnp.ones((b, n), dtype=bool)
        s = 0.02
        return {'x': x, 'latents': latents, 'mask': mask, 'ln_x_g': jnp.ones((DIM,), jnp.float32), 'ln_x_b': jnp.zeros((DIM,), jnp.float32), 'ln_l_g': jnp.ones((DIM_LATENT,), jnp.float32), 'ln_l_b': jnp.zeros((DIM_LATENT,), jnp.float32), 'qn_g': jnp.ones((DIM_HEAD,), jnp.float32), 'kn_g': jnp.ones((DIM_HEAD,), jnp.float32), 'Wq': jax.random.normal(ks[2], (DIM_LATENT, INNER), jnp.float32) * s, 'Wkv': jax.random.normal(ks[3], (DIM, 2 * INNER), jnp.float32) * s, 'Wout': jax.random.normal(ks[4], (INNER, DIM_LATENT), jnp.float32) * s, 'bout': jnp.zeros((DIM_LATENT,), jnp.float32)}
    _L1_xattn_all = _L1_xattn_setup()
    _L1_xattn_in = {k: v for k, v in _L1_xattn_all.items() if k in ('ln_x_g', 'ln_x_b', 'ln_l_g', 'ln_l_b', 'qn_g', 'kn_g', 'Wq', 'Wkv', 'Wout', 'bout')}
    del _L1_xattn_all

    def _L1_ffn_setup():
        import jax, jax.numpy as jnp
        import numpy as np
        B, S, D, F, E, K = (2, 512, 256, 1024, 8, 2)
        key = jax.random.key(seed)
        ks = jax.random.split(key, 5)
        x = jax.random.normal(ks[0], (B, S, D), dtype=jnp.float32)
        Wg = jax.random.normal(ks[1], (D, E), dtype=jnp.float32) * 0.02
        W1 = jax.random.normal(ks[2], (E, D, F), dtype=jnp.float32) * 0.02
        b1 = jnp.zeros((E, F), dtype=jnp.float32)
        W2 = jax.random.normal(ks[3], (E, F, D), dtype=jnp.float32) * 0.02
        b2 = jnp.zeros((E, D), dtype=jnp.float32)
        return {'x': x, 'Wg': Wg, 'W1': W1, 'b1': b1, 'W2': W2, 'b2': b2}
    _L1_ffn_all = _L1_ffn_setup()
    _L1_ffn_in = {k: v for k, v in _L1_ffn_all.items() if k in ('Wg', 'W1', 'b1', 'W2', 'b2')}
    del _L1_ffn_all
    return {'x': x, 'ctx_1024': ctx_1024, 'mask_BxS2_bf1': mask_BxS2_bf1, 'L0_xattn_Wq': _L0_xattn_in['Wq'], 'L0_xattn_bq': _L0_xattn_in['bq'], 'L0_xattn_Wk': _L0_xattn_in['Wk'], 'L0_xattn_bk': _L0_xattn_in['bk'], 'L0_xattn_Wv': _L0_xattn_in['Wv'], 'L0_xattn_bv': _L0_xattn_in['bv'], 'L0_xattn_Wo': _L0_xattn_in['Wo'], 'L0_xattn_bo': _L0_xattn_in['bo'], 'L0_xattn_rk_table': _L0_xattn_in['rk_table'], 'L0_xattn_rv_table': _L0_xattn_in['rv_table'], 'L0_ffn_router_weight': _L0_ffn_in['router_weight'], 'L0_ffn_router_bias': _L0_ffn_in['router_bias'], 'L0_ffn_gate_up_proj': _L0_ffn_in['gate_up_proj'], 'L0_ffn_gate_up_bias': _L0_ffn_in['gate_up_bias'], 'L0_ffn_down_proj': _L0_ffn_in['down_proj'], 'L0_ffn_down_bias': _L0_ffn_in['down_bias'], 'L1_xattn_ln_x_g': _L1_xattn_in['ln_x_g'], 'L1_xattn_ln_x_b': _L1_xattn_in['ln_x_b'], 'L1_xattn_ln_l_g': _L1_xattn_in['ln_l_g'], 'L1_xattn_ln_l_b': _L1_xattn_in['ln_l_b'], 'L1_xattn_qn_g': _L1_xattn_in['qn_g'], 'L1_xattn_kn_g': _L1_xattn_in['kn_g'], 'L1_xattn_Wq': _L1_xattn_in['Wq'], 'L1_xattn_Wkv': _L1_xattn_in['Wkv'], 'L1_xattn_Wout': _L1_xattn_in['Wout'], 'L1_xattn_bout': _L1_xattn_in['bout'], 'L1_ffn_Wg': _L1_ffn_in['Wg'], 'L1_ffn_W1': _L1_ffn_in['W1'], 'L1_ffn_b1': _L1_ffn_in['b1'], 'L1_ffn_W2': _L1_ffn_in['W2'], 'L1_ffn_b2': _L1_ffn_in['b2']}

def reference(x, ctx_1024, mask_BxS2_bf1, L0_xattn_Wq, L0_xattn_bq, L0_xattn_Wk, L0_xattn_bk, L0_xattn_Wv, L0_xattn_bv, L0_xattn_Wo, L0_xattn_bo, L0_xattn_rk_table, L0_xattn_rv_table, L0_ffn_router_weight, L0_ffn_router_bias, L0_ffn_gate_up_proj, L0_ffn_gate_up_bias, L0_ffn_down_proj, L0_ffn_down_bias, L1_xattn_ln_x_g, L1_xattn_ln_x_b, L1_xattn_ln_l_g, L1_xattn_ln_l_b, L1_xattn_qn_g, L1_xattn_kn_g, L1_xattn_Wq, L1_xattn_Wkv, L1_xattn_Wout, L1_xattn_bout, L1_ffn_Wg, L1_ffn_W1, L1_ffn_b1, L1_ffn_W2, L1_ffn_b2):
    import jax
    import jax.numpy as jnp

    def _L0_xattn_ref(q, k, v, Wq, bq, Wk, bk, Wv, bv, Wo, bo, rk_table, rv_table):
        import jax, jax.numpy as jnp
        import numpy as np
        N_HEADS = 16

        def _rel_emb(table, len_q, len_k):
            P = (table.shape[0] - 1) // 2
            rel = jnp.arange(len_k)[None, :] - jnp.arange(len_q)[:, None]
            idx = jnp.clip(rel, -P, P) + P
            return table[idx]
        B, Sq, E = q.shape
        Sk = k.shape[1]
        H = N_HEADS
        d = E // H
        scale = jnp.sqrt(jnp.asarray(d, q.dtype))
        qh = (q @ Wq.T + bq).reshape(B, Sq, H, d).transpose(0, 2, 1, 3)
        kh = (k @ Wk.T + bk).reshape(B, Sk, H, d).transpose(0, 2, 1, 3)
        vh = (v @ Wv.T + bv).reshape(B, Sk, H, d).transpose(0, 2, 1, 3)
        qk = jnp.einsum('bhqd,bhkd->bhqk', qh, kh)
        r_k = _rel_emb(rk_table, Sq, Sk)
        q_rk = jnp.einsum('bhqd,qkd->bhqk', qh, r_k)
        attn = jax.nn.softmax((qk + q_rk) / scale, axis=-1)
        w1 = jnp.einsum('bhqk,bhkd->bhqd', attn, vh)
        r_v = _rel_emb(rv_table, Sq, Sk)
        w2 = jnp.einsum('bhqk,qkd->bhqd', attn, r_v)
        out = (w1 + w2).transpose(0, 2, 1, 3).reshape(B, Sq, E)
        return out @ Wo.T + bo

    def _L0_ffn_ref(hidden_states, router_weight, router_bias, gate_up_proj, gate_up_bias, down_proj, down_bias):
        import jax, jax.numpy as jnp
        import numpy as np
        ALPHA = 1.702
        LIMIT = 7.0
        TOP_K = 2
        B, S, H = hidden_states.shape
        E, _, two_I = gate_up_proj.shape
        I = two_I // 2
        flat = hidden_states.reshape(B * S, H)
        logits = flat @ router_weight.T + router_bias
        scores = jax.nn.softmax(logits, axis=-1)
        topk_w, topk_idx = jax.lax.top_k(scores, TOP_K)
        gu = jnp.einsum('th,ehn->ten', flat, gate_up_proj) + gate_up_bias
        gate = jnp.minimum(gu[..., :I], LIMIT)
        up = jnp.clip(gu[..., I:], -LIMIT, LIMIT)
        glu = gate * jax.nn.sigmoid(gate * ALPHA)
        act = (up + 1.0) * glu
        down = jnp.einsum('tei,eih->teh', act, down_proj) + down_bias
        gathered = jnp.take_along_axis(down, topk_idx[:, :, None], axis=1)
        out = (gathered * topk_w[:, :, None]).sum(axis=1)
        return out.reshape(B, S, H)

    def _L1_xattn_ref(x, latents, mask, ln_x_g, ln_x_b, ln_l_g, ln_l_b, qn_g, kn_g, Wq, Wkv, Wout, bout):
        import jax, jax.numpy as jnp
        import numpy as np
        DIM = 256
        DIM_LATENT = 256
        DIM_HEAD = 64
        HEADS = 16
        INNER = HEADS * DIM_HEAD

        def layernorm(x, g, b, eps=1e-05):
            m = jnp.mean(x, axis=-1, keepdims=True)
            v = jnp.mean((x - m) ** 2, axis=-1, keepdims=True)
            return (x - m) / jnp.sqrt(v + eps) * g + b

        def rmsnorm(x, gamma, eps=1e-08):
            n = jnp.linalg.norm(x, axis=-1, keepdims=True) * x.shape[-1] ** (-0.5)
            return x / jnp.maximum(n, eps) * gamma
        b, n, _ = x.shape
        m = latents.shape[1]
        h, d = (HEADS, DIM_HEAD)
        scale = d ** (-0.5)
        xn = layernorm(x, ln_x_g, ln_x_b)
        ln = layernorm(latents, ln_l_g, ln_l_b)
        q = (ln @ Wq).reshape(b, m, h, d).transpose(0, 2, 1, 3)
        kv = jnp.concatenate([xn @ Wkv, ln @ Wkv], axis=1)
        kv = kv.reshape(b, n + m, 2, h, d)
        k = kv[:, :, 0].transpose(0, 2, 1, 3)
        v = kv[:, :, 1].transpose(0, 2, 1, 3)
        qn = rmsnorm(q, qn_g) * scale
        kn = rmsnorm(k, kn_g)
        sim = jnp.einsum('bhid,bhjd->bhij', qn, kn)
        max_neg = -jnp.finfo(sim.dtype).max
        padded_mask = jnp.concatenate([mask, jnp.ones((b, m), bool)], axis=1)
        sim = jnp.where(padded_mask[:, None, None, :], sim, max_neg)
        attn = jax.nn.softmax(sim.astype(jnp.float32), axis=-1).astype(sim.dtype)
        out = jnp.einsum('bhij,bhjd->bhid', attn, v)
        out = out.transpose(0, 2, 1, 3).reshape(b, m, h * d)
        return out @ Wout + bout

    def _L1_ffn_ref(x, Wg, W1, b1, W2, b2):
        import jax, jax.numpy as jnp
        import numpy as np
        B, S, D, F, E, K = (2, 512, 256, 1024, 8, 2)
        b, s, d = x.shape
        e = Wg.shape[1]
        T = b * s
        C = 2 * K * T // e
        xt = x.reshape(T, d)
        logits = xt.astype(jnp.float32) @ Wg.astype(jnp.float32)
        gates = jax.nn.softmax(logits, axis=-1)
        idx1 = jnp.argmax(gates, axis=-1)
        mask1 = jax.nn.one_hot(idx1, e, dtype=gates.dtype)
        gate1 = jnp.sum(gates * mask1, axis=-1)
        logits2 = jnp.where(mask1 > 0, -jnp.inf, logits)
        idx2 = jnp.argmax(logits2, axis=-1)
        mask2 = jax.nn.one_hot(idx2, e, dtype=gates.dtype)
        gate2 = jnp.sum(gates * mask2, axis=-1)
        denom = gate1 + gate2 + 1e-09
        w1 = gate1 / denom
        w2 = gate2 / denom
        p1 = jnp.cumsum(mask1, axis=0) - mask1
        pos1 = jnp.sum(p1 * mask1, axis=-1).astype(jnp.int32)
        off = jnp.sum(mask1, axis=0)
        p2 = jnp.cumsum(mask2, axis=0) - mask2 + off[None, :]
        pos2 = jnp.sum(p2 * mask2, axis=-1).astype(jnp.int32)
        keep1 = (pos1 < C).astype(xt.dtype)
        keep2 = (pos2 < C).astype(xt.dtype)
        pos1 = jnp.clip(pos1, 0, C - 1)
        pos2 = jnp.clip(pos2, 0, C - 1)
        xe = jnp.zeros((e, C, d), dtype=xt.dtype)
        xe = xe.at[idx1, pos1].add(xt * keep1[:, None])
        xe = xe.at[idx2, pos2].add(xt * keep2[:, None])
        h = jax.nn.gelu(jnp.einsum('ecd,edf->ecf', xe, W1) + b1[:, None, :], approximate=False)
        ye = jnp.einsum('ecf,efd->ecd', h, W2) + b2[:, None, :]
        out = ye[idx1, pos1] * (w1 * keep1)[:, None] + ye[idx2, pos2] * (w2 * keep2)[:, None]
        return out.reshape(b, s, d)
    x = x + _L0_xattn_ref(_layernorm(x, axis=-1), ctx_1024, ctx_1024, L0_xattn_Wq, L0_xattn_bq, L0_xattn_Wk, L0_xattn_bk, L0_xattn_Wv, L0_xattn_bv, L0_xattn_Wo, L0_xattn_bo, L0_xattn_rk_table, L0_xattn_rv_table)
    x = x + _L0_ffn_ref(_layernorm(x, axis=-1), L0_ffn_router_weight, L0_ffn_router_bias, L0_ffn_gate_up_proj, L0_ffn_gate_up_bias, L0_ffn_down_proj, L0_ffn_down_bias)
    x = x + _L1_xattn_ref(ctx_1024, _layernorm(x, axis=-1), mask_BxS2_bf1, L1_xattn_ln_x_g, L1_xattn_ln_x_b, L1_xattn_ln_l_g, L1_xattn_ln_l_b, L1_xattn_qn_g, L1_xattn_kn_g, L1_xattn_Wq, L1_xattn_Wkv, L1_xattn_Wout, L1_xattn_bout)
    x = x + _L1_ffn_ref(_layernorm(x, axis=-1), L1_ffn_Wg, L1_ffn_W1, L1_ffn_b1, L1_ffn_W2, L1_ffn_b2)
    return x

_drawn_inputs = setup_inputs


def setup_inputs(seed=0):
    import zlib

    import numpy as np

    out = dict(_drawn_inputs(seed))
    spreads = {'L0_xattn_bq': (0.0, 0.8),
     'L0_xattn_bk': (0.0, 2.0),
     'L0_xattn_bv': (0.0, 0.1),
     'L0_xattn_bo': (0.0, 0.1),
     'L0_ffn_router_bias': (0.0, 2.0),
     'L0_ffn_gate_up_bias': (0.0, 0.1),
     'L0_ffn_down_bias': (0.0, 0.1),
     'L1_xattn_ln_x_g': (1.0, 0.6),
     'L1_xattn_ln_x_b': (0.0, 0.8),
     'L1_xattn_ln_l_g': (1.0, 0.6),
     'L1_xattn_ln_l_b': (0.0, 0.374),
     'L1_xattn_qn_g': (1.0, 0.6),
     'L1_xattn_kn_g': (1.0, 0.6),
     'L1_xattn_bout': (0.0, 0.1),
     'L1_ffn_b1': (0.0, 0.323),
     'L1_ffn_b2': (0.0, 0.1)}
    factors = {'L0_xattn_Wq': 8.0,
     'L0_xattn_Wk': 8.0,
     'L0_xattn_rk_table': 64.0,
     'L0_xattn_rv_table': 5.303}
    for name, (base, spread) in spreads.items():
        noise = np.random.default_rng([zlib.crc32(name.encode()), seed]).standard_normal(out[name].shape)
        drawn = base * np.exp(spread * noise) if base else spread * noise
        out[name] = jnp.asarray(drawn.astype(out[name].dtype))
    for name, factor in factors.items():
        out[name] = (out[name] * factor).astype(out[name].dtype)
    return out
```

```python
from contextlib import ExitStack, contextmanager

import concourse.bass as bass
from concourse import mybir
import numpy as np

F32 = mybir.dt.float32
F32R = mybir.dt.float32r
BF16 = mybir.dt.bfloat16
I32 = mybir.dt.int32
U32 = mybir.dt.uint32
U8 = mybir.dt.uint8
ALU = mybir.AluOpType
ACT = mybir.ActivationFunctionType
AX = mybir.AxisListType

P = 128
BATCH, SEQ, E = 2, 1024, 256
CTX = 77
TOKENS = BATCH * SEQ
TILES = TOKENS // P
EC = E // P
LN_EPS = 1e-5

H0 = 16
D0 = E // H0
REACH = 128
GROUP = P // D0
HEAD_GROUPS = H0 // GROUP
BAND = CTX + P - 1
V0 = D0 + 1
NEAR = 2
BANK = 512

NE = 8
TOPK = 2
SLOT_COLS = TOPK * TILES
BLOCKS = TOPK * TOKENS // P + NE
DUMP = TOPK * TOKENS

H1, D1 = 16, 64
KEYS = SEQ + CTX
KT_TILES = SEQ // P + 1
PAIRS = H1 // 2
CAPACITY = 2 * TOPK * TOKENS // NE


@contextmanager
def phase(nc):
    with nc.cleanup_on_exit(), ExitStack() as ctx:
        yield ctx


class Steps:

    def __init__(self, engine, sem):
        self.engine, self.sem, self.n = engine, sem, 0

    def mark(self, ins):
        self.n += 1
        return ins.then_inc(self.sem, 1)

    def after(self, ins):
        self.mark(ins)
        self.engine.wait_ge(self.sem, self.n)


def layer_norm(nc, name, src, dst, ident, dstT=None, gain=None, shift=None, store=None):
    with phase(nc) as ctx:
        sb = lambda n, s, d=F32: ctx.enter_context(nc.sbuf_tensor(f"{name}_{n}", s, d))
        sem = lambda n: nc.alloc_semaphore(f"{name}_{n}")
        stats = sb("stats", [P, TILES, 6])
        moments = sb("moments", [P, TILES, 2])
        variance = sb("variance", [P, TILES])
        exponent = sb("exponent", [P, TILES])
        rstd = sb("rstd", [P, TILES])
        turned = [ctx.enter_context(nc.psum_tensor(f"{name}_turned{i}", [P, EC, P], F32)) for i in range(4)]
        stats_done, moments_done, variance_done = sem("stats_done"), sem("moments_done"), sem("variance_done")
        exponent_set, rstd_done, dst_done = sem("exponent_set"), sem("rstd_done"), sem("dst_done")
        turned_done, copied, stored = sem("turned_done"), sem("copied"), sem("stored")
        block = ctx.enter_context(nc.Block())

        @block.vector
        def _(dve):
            for t in range(TILES):
                nc.vector.bn_stats(stats[:, t, :], src[:, t, :]).then_inc(stats_done, 1)
            for t in range(TILES):
                dve.wait_ge(stats_done, t + 1)
                nc.vector.bn_aggr(moments[:, t, :], stats[:, t, :]).then_inc(moments_done, 1)
            dve.wait_ge(moments_done, TILES)
            nc.vector.tensor_scalar(variance[:, :], moments[:, :, 1], LN_EPS, None, ALU.add).then_inc(variance_done, 1)
            dve.wait_ge(rstd_done, 1)
            for t in range(TILES):
                nc.vector.tensor_scalar(dst[:, t, :], src[:, t, :], moments[:, t, 0:1], rstd[:, t:t + 1],
                                        ALU.subtract, ALU.mult).then_inc(dst_done, 1)

        @block.gpsimd
        def _(pool):
            nc.gpsimd.memset(exponent[:, :], -0.5).then_inc(exponent_set, 1)
            pool.wait_ge(exponent_set, 1)
            pool.wait_ge(variance_done, 1)
            nc.gpsimd.tensor_tensor(rstd[:, :], variance[:, :], exponent[:, :], ALU.pow).then_inc(rstd_done, 1)

        @block.tensor
        def _(pe):
            for t in range(TILES if dstT is not None else 0):
                pe.wait_ge(dst_done, t + 1)
                if t >= 4:
                    pe.wait_ge(copied, t - 3)
                for c in range(EC):
                    ins = nc.tensor.transpose(turned[t % 4][:, c, :], dst[:, t, c * P:(c + 1) * P], ident[:, :])
                ins.then_inc(turned_done, 1)

        @block.scalar
        def _(act):
            for t in range(TILES if dstT is not None else 0):
                act.wait_ge(turned_done, t + 1)
                cols = slice(t * P, (t + 1) * P)
                if gain is None:
                    nc.scalar.activation(dstT[:, :, cols], turned[t % 4][:, :, :], ACT.Copy).then_inc(copied, 1)
                else:
                    for c in range(EC):
                        ins = nc.scalar.activation(dstT[:, c, cols], turned[t % 4][:, c, :], ACT.Identity,
                                                   bias=shift[:, c:c + 1], scale=gain[:, c:c + 1])
                    ins.then_inc(copied, 1)

        @block.sync
        def _(sp):
            if store is not None:
                for t in range(TILES):
                    sp.wait_ge(dst_done, t + 1)
                    sp.dma_start(store[t * P:(t + 1) * P, :], dst[:, t, :]).then_inc(stored, 16)
                sp.wait_ge(stored, 16 * TILES)


def load_residual(nc, x, ident_in, xres, ident):
    with phase(nc) as ctx:
        x_loaded = nc.alloc_semaphore("x_loaded")
        block = ctx.enter_context(nc.Block())

        @block.sync
        def _(sp):
            sp.dma_start(xres[:, :, :], x.rearrange("b (t p) e -> p (b t) e", p=P)).then_inc(x_loaded, 16)
            sp.dma_start(ident[:, :], ident_in).then_inc(x_loaded, 16)
            sp.wait_ge(x_loaded, 32)


def store_residual(nc, xres, out):
    with phase(nc) as ctx:
        out_stored = nc.alloc_semaphore("out_stored")
        block = ctx.enter_context(nc.Block())

        @block.sync
        def _(sp):
            sp.dma_start(out.rearrange("b (t p) e -> p (b t) e", p=P), xres[:, :, :]).then_inc(out_stored, 16)
            sp.wait_ge(out_stored, 16)


def layer0_attention(nc, I, xres, ident):
    with phase(nc) as ctx:
        sb = lambda n, s, d=F32: ctx.enter_context(nc.sbuf_tensor(f"a0_{n}", s, d))
        sem = lambda n: nc.alloc_semaphore(f"a0_{n}")
        XW = BAND + 1
        near_tiles = [b * (SEQ // P) + i for b in range(BATCH) for i in range(NEAR)]
        far_tiles = [t for t in range(TILES) if t not in near_tiles]
        NN = len(near_tiles)

        QT = sb("QT", [P, EC, TOKENS])
        dist_d = nc.dram_tensor("a0_dist_dram", [NN, P, BAND, H0], F32)
        prob_d = nc.dram_tensor("a0_prob_dram", [NN, P, BAND, H0], F32)
        Wo = sb("Wo", [P, EC, E])
        bo = sb("bo", [P, E])
        kblock = sb("kblock", [P, 2, BATCH, HEAD_GROUPS, GROUP, CTX])
        rblock = sb("rblock", [P, NEAR, GROUP, BAND])
        vones = sb("vones", [CTX, 2, BATCH, H0, V0])
        rv = sb("rv", [BAND // 2, NEAR, 2, V0])

        with ExitStack() as c2:
            sb2 = lambda n, s, d=F32: c2.enter_context(nc.sbuf_tensor(f"a0p_{n}", s, d))
            sem2 = lambda n: nc.alloc_semaphore(f"a0p_{n}")
            xn = sb2("xn", [P, TILES, E])
            xnT = sb2("xnT", [P, EC, TOKENS])
            layer_norm(nc, "a0ln", xres, xn, ident, xnT)
            W = {n: sb2(n, [P, EC, E]) for n in ("Wq", "Wk", "Wv")}
            ctxT = sb2("ctxT", [P, EC, BATCH * CTX])
            bq, bqs, bk = sb2("bq", [P, EC]), sb2("bqs", [P, EC]), sb2("bk", [P, EC])
            bv, rv0 = sb2("bv", [CTX, E]), sb2("rv0", [CTX, E])
            mask = sb2("mask", [P, GROUP])
            relk = sb2("relk", [P, NEAR, BAND])
            kT = sb2("kT", [P, 2, EC, BATCH * CTX])
            vnear = sb2("vnear", [CTX, BATCH, E])
            zeros = sb2("zeros", [P, BAND * H0])
            pq = [c2.enter_context(nc.psum_tensor(f"a0_pq{i}", [P, BANK], F32)) for i in range(4)]
            pk = c2.enter_context(nc.psum_tensor("a0_pk", [P, EC, BATCH * CTX], F32))
            pv = c2.enter_context(nc.psum_tensor("a0_pv", [CTX, BATCH, E], F32))
            loaded, zeroed, cleared = sem2("loaded"), sem2("zeroed"), sem2("cleared")
            q_done, q_out, k_done, k_out, v_done = (sem2(n) for n in ("q_done", "q_out", "k_done", "k_out", "v_done"))
            step, bias_ready, tails = sem2("step"), sem2("bias_ready"), sem2("tails")
            NLOAD = 13
            block = c2.enter_context(nc.Block())

            @block.sync
            def _(sp):
                for n, dst in (("Wq", W["Wq"]), ("Wk", W["Wk"]), ("Wv", W["Wv"]), ("Wo", Wo)):
                    sp.dma_start(dst[:, :, :], I["L0_xattn_" + n + "T"].rearrange("(c p) n -> p c n", p=P)).then_inc(loaded, 16)
                sp.dma_start(ctxT[:, :, :], I["ctxT"].rearrange("(c p) n -> p c n", p=P)).then_inc(loaded, 16)
                sp.dma_start(bq[:, :], I["L0_xattn_bq"]).then_inc(loaded, 16)
                sp.dma_start(bk[:, :], I["L0_xattn_bk"]).then_inc(loaded, 16)
                sp.dma_start(bv[:, :], I["L0_xattn_bv"].to_broadcast([CTX, E])).then_inc(loaded, 16)
                sp.dma_start(rv0[:, :], I["rv_far"].to_broadcast([CTX, E])).then_inc(loaded, 16)
                sp.dma_start(bo[:, :], I["L0_xattn_bo"].to_broadcast([P, E])).then_inc(loaded, 16)
                sp.dma_start(mask[:, :], I["head_mask"]).then_inc(loaded, 16)
                sp.dma_start(relk[:, :, :], I["rel_k"]).then_inc(loaded, 16)
                sp.wait_ge(tails, 1)
                sp.dma_start(rv[:, :, :, 0:D0], I["rel_v"]).then_inc(loaded, 16)
                sp.wait_ge(zeroed, 1)
                for n in range(NN):
                    sp.dma_start(prob_d[n].rearrange("p j h -> p (j h)"), zeros[:, :]).then_inc(cleared, 16)
                sp.wait_ge(cleared, 16 * NN)
                sp.wait_ge(loaded, 16 * NLOAD)

            @block.gpsimd
            def _(pool):
                nc.gpsimd.memset(zeros[:, :], 0.0).then_inc(zeroed, 1)

            @block.tensor
            def _(pe):
                pe.wait_ge(loaded, 16 * NLOAD)
                for g in range(EC):
                    for c in range(EC):
                        ins = nc.tensor.matmul(pk[:, g, :], W["Wk"][:, c, g * P:(g + 1) * P], ctxT[:, c, :],
                                               start=c == 0, stop=c == EC - 1)
                ins.then_inc(k_done, 1)
                for b in range(BATCH):
                    for c in range(EC):
                        ins = nc.tensor.matmul(pv[:, b, :], ctxT[:, c, b * CTX:(b + 1) * CTX], W["Wv"][:, c, :],
                                               start=c == 0, stop=c == EC - 1)
                ins.then_inc(v_done, 1)
                for g in range(EC):
                    for n in range(TOKENS // BANK):
                        i = g * (TOKENS // BANK) + n
                        if i >= 4:
                            pe.wait_ge(q_out, i - 3)
                        for c in range(EC):
                            ins = nc.tensor.matmul(pq[i % 4][:, :], W["Wq"][:, c, g * P:(g + 1) * P],
                                                   xnT[:, c, n * BANK:(n + 1) * BANK], start=c == 0, stop=c == EC - 1)
                        ins.then_inc(q_done, 1)

            @block.scalar
            def _(act):
                act.wait_ge(bias_ready, 1)
                act.wait_ge(k_done, 1)
                for g in range(EC):
                    ins = nc.scalar.activation(kT[:, 0, g, :], pk[:, g, :], ACT.Identity, bias=bk[:, g:g + 1])
                ins.then_inc(k_out, 1)
                for g in range(EC):
                    for n in range(TOKENS // BANK):
                        i = g * (TOKENS // BANK) + n
                        act.wait_ge(q_done, i + 1)
                        nc.scalar.activation(QT[:, g, n * BANK:(n + 1) * BANK], pq[i % 4][:, :], ACT.Identity,
                                             bias=bqs[:, g:g + 1], scale=D0 ** -0.5).then_inc(q_out, 1)

            @block.vector
            def _(dve):
                s = Steps(dve, step)
                s.mark(nc.vector.memset(vones[:, :, :, :, D0:V0], 1.0))
                nc.vector.memset(rv[:, :, :, D0:V0], 0.0).then_inc(tails, 1)
                dve.wait_ge(loaded, 16 * NLOAD)
                nc.vector.tensor_scalar(bqs[:, :], bq[:, :], D0 ** -0.5, None, ALU.mult).then_inc(bias_ready, 1)
                for i in range(NEAR):
                    s.mark(nc.vector.tensor_tensor(
                        rblock[:, i, :, :], relk[:, i, :].unsqueeze(1).to_broadcast([P, GROUP, BAND]),
                        mask[:, :].unsqueeze(2).to_broadcast([P, GROUP, BAND]), ALU.mult))
                dve.wait_ge(v_done, 1)
                for b in range(BATCH):
                    s.mark(nc.vector.tensor_tensor(vnear[:, b, :], pv[:, b, :], bv[:, :], ALU.add))
                dve.wait_ge(step, s.n)
                for b in range(BATCH):
                    v = vnear[:, b, :].rearrange("p (h d) -> p h d", h=H0)
                    s.mark(nc.vector.tensor_copy(vones[:, 0, b, :, 0:D0], v))
                    s.mark(nc.vector.tensor_tensor(vones[:, 1, b, :, 0:D0], v,
                                                   rv0[:, :].rearrange("p (h d) -> p h d", h=H0), ALU.add))
                dve.wait_ge(k_out, 1)
                for g in range(EC):
                    s.mark(nc.vector.tensor_scalar(kT[:, 1, g, :], kT[:, 0, g, :], relk[:, 1, 0:1], None, ALU.add))
                dve.wait_ge(step, s.n)
                for far in range(2):
                    for b in range(BATCH):
                        for g in range(HEAD_GROUPS):
                            nc.vector.tensor_tensor(
                                kblock[:, far, b, g, :, :],
                                kT[:, far, g, b * CTX:(b + 1) * CTX].unsqueeze(1).to_broadcast([P, GROUP, CTX]),
                                mask[:, :].unsqueeze(2).to_broadcast([P, GROUP, CTX]), ALU.mult)

        GB = GROUP // 2
        SB = H0 // GB
        soft_order = far_tiles[:6] + near_tiles + far_tiles[6:]
        value_order = far_tiles[:6] + far_tiles[6:] + near_tiles
        dist = sb("dist", [P, BAND, H0])
        near_scores = sb("near_scores", [P, NN, CTX, H0])
        shifted = sb("shifted", [P, H0, CTX])
        biased = sb("biased", [P, H0, CTX])
        peak = sb("peak", [P, 2, H0])
        prob = sb("prob", [P, 3, CTX, H0])
        near_prob = sb("near_prob", [P, NN, CTX, H0])
        band_prob = sb("band_prob", [P, 2, BAND, H0])
        probT = sb("probT", [P, 2, GROUP, P])
        rsum = sb("rsum", [P, H0])
        O = sb("O", [P, H0, D0])
        OT = sb("OT", [P, EC, P])
        yb = sb("yb", [P, E])
        ps = ctx.enter_context(nc.psum_tensor("a0_ps", [P, SB, BANK], F32))
        pt = ctx.enter_context(nc.psum_tensor("a0_pt", [P, GROUP, P], F32))
        po = ctx.enter_context(nc.psum_tensor("a0_po", [P, H0, V0], F32))
        py = ctx.enter_context(nc.psum_tensor("a0_py", [P, BANK], F32))
        d_done, d_out, d_stored = (sem(n) for n in ("d_done", "d_out", "d_stored"))
        d_back = [sem(f"d_back{n}") for n in range(NN)]
        p_back = [sem(f"p_back{n}") for n in range(NN)]
        s_done, s_shift, p_done = (sem(n) for n in ("s_done", "s_shift", "p_done"))
        p_stored, t_done, t_out, pt_used = (sem(n) for n in ("p_stored", "t_done", "t_out", "pt_used"))
        o_out, ot_done, ot_out, y_done, y_out = (sem(n) for n in ("o_out", "ot_done", "ot_out", "y_done", "y_out"))
        step = sem("step")
        DHEADS = 2
        DGROUPS = H0 // DHEADS

        def rounds(t):
            blocks = [(h, None) for h in range(H0)]
            if t in near_tiles:
                blocks += [(h, c) for h in range(H0) for c in range(2)]
            return [blocks[i:i + GROUP] for i in range(0, len(blocks), GROUP)]

        ROUNDS = [(t, r, blocks) for t in value_order for r, blocks in enumerate(rounds(t))]
        until = [min(TILES, max(soft_order.index(t) + 1 for t in value_order[:i + 1]) + 1) for i in range(TILES)]
        ahead = [range(until[i - 1] if i else 1, until[i]) for i in range(TILES)]
        prob_slot = {t: i % 3 for i, t in enumerate(far_tiles)}
        round_ends = {}
        for n, (t, r, blocks) in enumerate(ROUNDS):
            round_ends[t] = n + 1

        def prob_of(t):
            return near_prob[:, near_tiles.index(t)] if t in near_tiles else prob[:, prob_slot[t]]

        block = ctx.enter_context(nc.Block())

        @block.sync
        def _(sp):
            for n in range(NN):
                sp.wait_ge(d_out, DGROUPS * (n + 1))
                sp.dma_start(dist_d[n].rearrange("p j h -> p (j h)"),
                             dist[:, :, :].rearrange("p j h -> p (j h)")).then_inc(d_stored, 16)
                sp.wait_ge(d_stored, 16 * (n + 1))
                sheared = bass.AP(dist_d, n * P * BAND * H0 + (P - 1) * H0, [[(BAND - 1) * H0, P], [1, CTX * H0]])
                sp.dma_start(near_scores[:, n].rearrange("p j h -> p (j h)"), sheared).then_inc(d_back[n], 16)
            for n, t in enumerate(near_tiles):
                sp.wait_ge(p_done, soft_order.index(t) + 1)
                sheared = bass.AP(prob_d, n * P * BAND * H0 + (P - 1) * H0, [[(BAND - 1) * H0, P], [1, CTX * H0]])
                sp.dma_start(sheared, near_prob[:, n].rearrange("p j h -> p (j h)")).then_inc(p_stored, 16)
            for n, t in enumerate(near_tiles):
                sp.wait_ge(p_stored, 16 * NN)
                if n >= 2:
                    sp.wait_ge(t_done, round_ends[near_tiles[n - 2]])
                sp.dma_start(band_prob[:, n % 2].rearrange("p j h -> p (j h)"),
                             prob_d[n].rearrange("p j h -> p (j h)")).then_inc(p_back[n], 16)

        @block.tensor
        def _(pe):
            for n, t in enumerate(near_tiles):
                for i in range(DGROUPS):
                    k = n * DGROUPS + i
                    if k >= SB:
                        pe.wait_ge(d_out, k - SB + 1)
                    g, h = divmod(i * DHEADS, GROUP)
                    nc.tensor.matmul(ps[:, k % SB, 0:DHEADS * BAND], QT[:, g, t * P:(t + 1) * P],
                                     rblock[:, n % NEAR, h:h + DHEADS, :],
                                     start=True, stop=True).then_inc(d_done, 1)
            pe.wait_ge(d_out, NN * DGROUPS)

            def scores(i):
                t = soft_order[i]
                far, b = int(t not in near_tiles), t // (SEQ // P)
                if i:
                    pe.wait_ge(s_shift, i)
                for j in range(SB):
                    g, h = divmod(j * GB, GROUP)
                    ins = nc.tensor.matmul(ps[:, j, 0:GB * CTX], QT[:, g, t * P:(t + 1) * P],
                                           kblock[:, far, b, g, h:h + GB, :], start=True, stop=True)
                ins.then_inc(s_done, 1)

            n = 0
            scores(0)
            for i, t in enumerate(value_order):
                for j in ahead[i]:
                    scores(j)
                far, b = int(t not in near_tiles), t // (SEQ // P)
                pe.wait_ge(p_done, soft_order.index(t) + 1)
                for r, blocks in enumerate(rounds(t)):
                    if n >= 1:
                        pe.wait_ge(t_out, n)
                    if blocks[0][1] is not None and r == 2:
                        pe.wait_ge(p_back[near_tiles.index(t)], 16)
                    for j, (h, c) in enumerate(blocks):
                        if c is None:
                            ins = nc.tensor.transpose(pt[0:CTX, j, :], prob_of(t)[:, :, h], ident[:, :])
                        else:
                            rows = slice(c * (BAND // 2), (c + 1) * (BAND // 2))
                            ins = nc.tensor.transpose(pt[0:BAND // 2, j, :],
                                                      band_prob[:, near_tiles.index(t) % 2, rows, h], ident[:, :])
                    ins.then_inc(t_done, 1)
                    n += 1
                    pe.wait_ge(t_out, n)
                    if r == 0 and i:
                        pe.wait_ge(o_out, i)
                    for j, (h, c) in enumerate(blocks):
                        rhs = vones[:, far, b, h, :] if c is None else rv[:, near_tiles.index(t) % NEAR, c, :]
                        rows = CTX if c is None else BAND // 2
                        ins = nc.tensor.matmul(po[:, h, :], probT[0:rows, (n - 1) % 2, j, :], rhs,
                                               start=r == 0 and j == 0, stop=True, skip_group_check=True)
                    ins.then_inc(pt_used, 1)
                pe.wait_ge(o_out, i + 1)
                if i:
                    pe.wait_ge(y_out, i)
                for c in range(EC):
                    ins = nc.tensor.transpose(py[:, c * P:(c + 1) * P],
                                              O[:, c * GROUP:(c + 1) * GROUP, :].rearrange("p h d -> p (h d)"), ident[:, :])
                ins.then_inc(ot_done, 1)
                pe.wait_ge(ot_out, i + 1)
                for c in range(EC):
                    ins = nc.tensor.matmul(py[:, E:2 * E], OT[:, c, :], Wo[:, c, :], start=c == 0, stop=c == EC - 1)
                ins.then_inc(y_done, 1)

        @block.scalar
        def _(act):
            for k in range(NN * DGROUPS):
                act.wait_ge(d_done, k + 1)
                if k % DGROUPS == 0 and k:
                    act.wait_ge(d_stored, 16 * (k // DGROUPS))
                h = k % DGROUPS * DHEADS
                nc.scalar.activation(dist[:, :, h:h + DHEADS].rearrange("p j h -> p h j"),
                                     ps[:, k % SB, 0:DHEADS * BAND].rearrange("p (h j) -> p h j", h=DHEADS),
                                     ACT.Copy).then_inc(d_out, 1)

            def soft(i):
                t = soft_order[i]
                act.wait_ge(s_shift, i + 1)
                if t not in near_tiles and far_tiles.index(t) >= 3:
                    act.wait_ge(pt_used, round_ends[far_tiles[far_tiles.index(t) - 3]])
                nc.scalar.activation(prob_of(t).rearrange("p k h -> p h k"), shifted[:, :, :], ACT.Exp).then_inc(p_done, 1)

            n = 0
            soft(0)
            for i, t in enumerate(value_order):
                for j in ahead[i]:
                    soft(j)
                for r, blocks in enumerate(rounds(t)):
                    act.wait_ge(t_done, n + 1)
                    if n >= 2:
                        act.wait_ge(pt_used, n - 1)
                    rows = CTX if blocks[0][1] is None else BAND // 2
                    nc.scalar.activation(probT[0:rows, n % 2, :, :], pt[0:rows, :, :], ACT.Copy).then_inc(t_out, 1)
                    n += 1
                act.wait_ge(ot_done, i + 1)
                nc.scalar.activation(OT[:, :, :], py[:, 0:E].rearrange("p (c n) -> p c n", c=EC), ACT.Copy).then_inc(ot_out, 1)

        @block.vector
        def _(dve):
            s = Steps(dve, step)

            def shift(i):
                t = soft_order[i]
                dve.wait_ge(s_done, i + 1)
                src = ps[:, :, 0:GB * CTX].rearrange("p b (h k) -> p b h k", h=GB)
                if t in near_tiles:
                    dve.wait_ge(d_back[near_tiles.index(t)], 16)
                    for j in range(SB):
                        ins = nc.vector.tensor_tensor(
                            biased[:, j * GB:(j + 1) * GB, :], src[:, j],
                            near_scores[:, near_tiles.index(t), :, j * GB:(j + 1) * GB].rearrange("p k h -> p h k"), ALU.add)
                    s.after(ins)
                    src = biased[:, :, :].rearrange("p (b h) k -> p b h k", b=SB)
                s.after(nc.vector.tensor_reduce(peak[:, i % 2, :].rearrange("p (b h) -> p b h", b=SB), src, AX.X, ALU.max))
                if i:
                    dve.wait_ge(p_done, i)
                nc.vector.tensor_tensor(
                    shifted[:, :, :].rearrange("p (b h) k -> p b h k", b=SB), src,
                    peak[:, i % 2, :].rearrange("p (b h) -> p b h", b=SB).unsqueeze(3).to_broadcast([P, SB, GB, CTX]),
                    ALU.subtract).then_inc(s_shift, 1)

            shift(0)
            for i, t in enumerate(value_order):
                for j in ahead[i]:
                    shift(j)
                dve.wait_ge(pt_used, round_ends[t])
                if i:
                    dve.wait_ge(ot_done, i)
                s.after(nc.vector.reciprocal(rsum[:, :], po[:, :, D0]))
                nc.vector.tensor_tensor(O[:, :, :], po[:, :, 0:D0],
                                        rsum[:, :].unsqueeze(2).to_broadcast([P, H0, D0]), ALU.mult).then_inc(o_out, 1)
                dve.wait_ge(y_done, i + 1)
                ins = nc.vector.tensor_tensor(yb[:, :], py[:, E:2 * E], bo[:, :], ALU.add)
                ins.then_inc(y_out, 1)
                dve.wait_ge(y_out, i + 1)
                s.after(nc.vector.tensor_tensor(xres[:, t, :], xres[:, t, :], yb[:, :], ALU.add))


def route(nc, name, I, layer, xnT, lists):
    with phase(nc) as ctx:
        sb = lambda n, s, d=F32: ctx.enter_context(nc.sbuf_tensor(f"{name}_{n}", s, d))
        sem = lambda n: nc.alloc_semaphore(f"{name}_{n}")
        Wr = sb("Wr", [P, EC, NE])
        br = sb("br", [P, NE])
        iota = sb("iota", [P, P])
        lane = sb("lane", [P, 2])
        before = sb("before", [P, P])
        ones = sb("ones", [P, P])
        logits = sb("logits", [P, TILES, NE])
        top = sb("top", [P, TILES, 8])
        topi = sb("topi", [P, TILES, 8], U32)
        pick = sb("pick", [P, TOPK, TILES])
        less = sb("less", [P, TILES, NE])
        ex = sb("ex", [P, TILES, NE])
        gap = sb("gap", [P, TILES])
        second = sb("second", [P, TILES])
        total = sb("total", [P, TILES])
        first = sb("first", [P, TILES])
        M = sb("M", [P, SLOT_COLS, NE])
        scan = [sb(f"scan{i}", [P, SLOT_COLS + 1, NE]) for i in range(2)]
        rank = sb("rank", [P, SLOT_COLS, NE])
        work = sb("work", [P, SLOT_COLS, NE])
        need = sb("need", [P, NE], I32)
        needb = sb("needb", [P, NE], I32)
        base = [sb(f"base{i}", [P, NE + 1]) for i in range(2)]
        pos = sb("pos", [P, SLOT_COLS])
        posi = sb("posi", [P, SLOT_COLS], I32)
        part = sb("part", [P, 2, SLOT_COLS], I32)
        partf = sb("partf", [P, 2, SLOT_COLS])
        row1h = sb("row1h", [P, SLOT_COLS, P], BF16)
        blk1h = sb("blk1h", [P, SLOT_COLS, 3, BLOCKS], BF16)
        code = sb("code", [P, BLOCKS])
        free = sb("free", [P, BLOCKS])
        wrap = sb("wrap", [P, BLOCKS])
        cmp = sb("cmp", [P, BLOCKS, NE])
        own = sb("own", [P, BLOCKS])
        low = sb("low", [P, BLOCKS])
        unused = sb("unused", [P, BLOCKS])
        rk = sb("rk", [P, SLOT_COLS])
        keep = sb("keep", [P, SLOT_COLS])
        pl = ctx.enter_context(nc.psum_tensor(f"{name}_pl", [P, TILES, NE], F32))
        pp = ctx.enter_context(nc.psum_tensor(f"{name}_pp", [P, 2, SLOT_COLS * NE], F32))
        pinv = ctx.enter_context(nc.psum_tensor(f"{name}_pinv", [P, 3, BLOCKS], F32))
        loaded, step, shifted, exps = sem("loaded"), sem("step"), sem("shifted"), sem("exps")
        logits_done, masks_done, counts_done, hot_done, inverse_done = (
            sem(n) for n in ("logits_done", "masks_done", "counts_done", "hot_done", "inverse_done"))
        block = ctx.enter_context(nc.Block())

        @block.sync
        def _(sp):
            sp.dma_start(Wr[:, :, :], I[f"L{layer}_router"].rearrange("(c p) n -> p c n", p=P)).then_inc(loaded, 16)
            sp.dma_start(iota[:, :], I["iota"].to_broadcast([P, P])).then_inc(loaded, 16)
            sp.dma_start(lane[:, :], I["lane"]).then_inc(loaded, 16)
            sp.dma_start(before[:, :], I["before"]).then_inc(loaded, 16)
            if layer == 0:
                sp.dma_start(br[:, :], I["L0_ffn_router_bias"].to_broadcast([P, NE])).then_inc(loaded, 16)
        nload = 16 * (5 if layer == 0 else 4)

        @block.tensor
        def _(pe):
            pe.wait_ge(loaded, nload)
            for t in range(TILES):
                for c in range(EC):
                    ins = nc.tensor.matmul(pl[:, t, :], xnT[:, c, t * P:(t + 1) * P], Wr[:, c, :],
                                           start=c == 0, stop=c == EC - 1)
            ins.then_inc(logits_done, 1)
            pe.wait_ge(masks_done, 1)
            m = M[:, :, :].rearrange("p s e -> p (s e)")
            nc.tensor.matmul(pp[:, 0, :], before[:, :], m, start=True, stop=True)
            nc.tensor.matmul(pp[:, 1, :], ones[:, :], m, start=True, stop=True).then_inc(counts_done, 1)
            pe.wait_ge(hot_done, 1)
            for s in range(SLOT_COLS):
                ins = nc.tensor.matmul(pinv[:, :, :], row1h[:, s, :], blk1h[:, s, :, :],
                                       start=s == 0, stop=s == SLOT_COLS - 1)
            ins.then_inc(inverse_done, 1)

        @block.scalar
        def _(act):
            act.wait_ge(shifted, 2)
            nc.scalar.activation(ex[:, :, :], less[:, :, :], ACT.Exp).then_inc(exps, 1)
            nc.scalar.activation(second[:, :], gap[:, :], ACT.Exp).then_inc(exps, 1)

        @block.vector
        def _(dve):
            s = Steps(dve, step)
            v = nc.vector
            s.mark(v.memset(ones[:, :], 1.0))
            for i in range(2):
                s.mark(v.memset(scan[i][:, 0, :], 0.0))
                s.mark(v.memset(base[i][:, 0:1], 0.0))
            dve.wait_ge(loaded, nload)
            dve.wait_ge(logits_done, 1)
            if layer == 0:
                s.after(v.tensor_tensor(logits[:, :, :], pl[:, :, :], br[:, :].unsqueeze(1).to_broadcast([P, TILES, NE]), ALU.add))
            else:
                s.after(v.tensor_copy(logits[:, :, :], pl[:, :, :]))
            for t in range(TILES):
                s.mark(v.max(top[:, t, :], logits[:, t, :]))
            dve.wait_ge(step, s.n)
            v.tensor_tensor(less[:, :, :], logits[:, :, :], top[:, :, 0:1].to_broadcast([P, TILES, NE]),
                            ALU.subtract).then_inc(shifted, 1)
            v.tensor_tensor(gap[:, :], top[:, :, 1], top[:, :, 0], ALU.subtract).then_inc(shifted, 1)
            for t in range(TILES):
                s.mark(v.max_index(topi[:, t, :], top[:, t, :], logits[:, t, :]))
            dve.wait_ge(step, s.n)
            s.after(v.tensor_copy(pick[:, :, :], topi[:, :, 0:TOPK].rearrange("p t k -> p k t")))
            v.tensor_tensor(M[:, :, :], iota[:, 0:NE].unsqueeze(1).to_broadcast([P, SLOT_COLS, NE]),
                            pick[:, :, :].rearrange("p k t -> p (k t)").unsqueeze(2).to_broadcast([P, SLOT_COLS, NE]),
                            ALU.is_equal).then_inc(masks_done, 1)
            dve.wait_ge(exps, 2)
            s.after(v.tensor_reduce(total[:, :], ex[:, :, :], AX.X, ALU.add))
            s.after(v.reciprocal(first[:, :], total[:, :]))
            if layer == 0:
                s.mark(v.tensor_copy(lists["gates"][:, 0, :], first[:, :]))
                s.mark(v.tensor_tensor(lists["gates"][:, 1, :], second[:, :], first[:, :], ALU.mult))
            else:
                s.after(v.tensor_tensor(second[:, :], second[:, :], first[:, :], ALU.mult))
                s.after(v.scalar_tensor_tensor(total[:, :], first[:, :], 1e-9, second[:, :], ALU.add, ALU.add))
                s.after(v.reciprocal(total[:, :], total[:, :]))
                s.mark(v.tensor_tensor(lists["gates"][:, 0, :], first[:, :], total[:, :], ALU.mult))
                s.mark(v.tensor_tensor(lists["gates"][:, 1, :], second[:, :], total[:, :], ALU.mult))
            dve.wait_ge(counts_done, 1)
            s.after(v.tensor_copy(scan[0][:, 1:, :], pp[:, 1, :].rearrange("p (s e) -> p s e", e=NE)))
            src, k = 0, 1
            while k < SLOT_COLS:
                a, b = scan[src], scan[1 - src]
                s.mark(v.tensor_copy(b[:, 1:1 + k, :], a[:, 1:1 + k, :]))
                s.after(v.tensor_tensor(b[:, 1 + k:, :], a[:, 1 + k:, :], a[:, 1:SLOT_COLS + 1 - k, :], ALU.add))
                src, k = 1 - src, 2 * k
            counted = scan[src]
            s.mark(v.tensor_tensor(rank[:, :, :], pp[:, 0, :].rearrange("p (s e) -> p s e", e=NE),
                                   counted[:, 0:SLOT_COLS, :], ALU.add))
            s.after(v.tensor_scalar(need[:, :], counted[:, SLOT_COLS, :], float(P - 1), None, ALU.add))
            s.after(v.tensor_scalar(needb[:, :], need[:, :], 7, None, ALU.arith_shift_right))
            s.after(v.tensor_copy(base[0][:, 1:], needb[:, :]))
            src, k = 0, 1
            while k < NE:
                a, b = base[src], base[1 - src]
                s.mark(v.tensor_copy(b[:, 1:1 + k], a[:, 1:1 + k]))
                s.after(v.tensor_tensor(b[:, 1 + k:], a[:, 1 + k:], a[:, 1:NE + 1 - k], ALU.add))
                src, k = 1 - src, 2 * k
            start = base[src][:, 0:NE]
            if layer == 1:
                s.after(v.tensor_tensor(work[:, :, :], rank[:, :, :], M[:, :, :], ALU.mult))
                s.after(v.tensor_reduce(rk[:, :], work[:, :, :], AX.X, ALU.add))
                s.after(v.tensor_scalar(keep[:, :], rk[:, :], float(CAPACITY), None, ALU.is_lt))
                g = lists["gates"][:, :, :].rearrange("p k t -> p (k t)")
                s.after(v.tensor_tensor(g, g, keep[:, :], ALU.mult))
            s.after(v.scalar_tensor_tensor(rank[:, :, :], start.unsqueeze(1).to_broadcast([P, SLOT_COLS, NE]), float(P),
                                           rank[:, :, :], ALU.mult, ALU.add))
            s.after(v.tensor_tensor(work[:, :, :], rank[:, :, :], M[:, :, :], ALU.mult))
            s.after(v.tensor_reduce(pos[:, :], work[:, :, :], AX.X, ALU.add))
            s.after(v.tensor_copy(posi[:, :], pos[:, :]))
            s.mark(v.tensor_scalar(part[:, 0, :], posi[:, :], P - 1, None, ALU.bitwise_and))
            s.after(v.tensor_scalar(part[:, 1, :], posi[:, :], 7, None, ALU.arith_shift_right))
            s.after(v.tensor_copy(partf[:, :, :], part[:, :, :]))
            s.mark(v.tensor_tensor(row1h[:, :, :], iota[:, :].unsqueeze(1).to_broadcast([P, SLOT_COLS, P]),
                                   partf[:, 0, :].unsqueeze(2).to_broadcast([P, SLOT_COLS, P]), ALU.is_equal))
            s.after(v.tensor_tensor(blk1h[:, :, 2, :], iota[:, 0:BLOCKS].unsqueeze(1).to_broadcast([P, SLOT_COLS, BLOCKS]),
                                    partf[:, 1, :].unsqueeze(2).to_broadcast([P, SLOT_COLS, BLOCKS]), ALU.is_equal))
            s.mark(v.tensor_scalar(blk1h[:, :, 1, :], blk1h[:, :, 2, :], lane[:, 0:1], None, ALU.mult))
            s.after(v.tensor_tensor(blk1h[:, :, 0, :], blk1h[:, :, 2, :],
                                    iota[:, 0:SLOT_COLS].unsqueeze(2).to_broadcast([P, SLOT_COLS, BLOCKS]), ALU.mult))
            s.engine.sem_inc(hot_done, 1)
            s.after(v.tensor_tensor(cmp[:, :, :], iota[:, 0:BLOCKS].unsqueeze(2).to_broadcast([P, BLOCKS, NE]),
                                    start.unsqueeze(1).to_broadcast([P, BLOCKS, NE]), ALU.is_ge))
            s.after(v.tensor_reduce(own[:, :], cmp[:, :, :], AX.X, ALU.add))
            s.mark(v.tensor_scalar(lists["expert"][:, :], own[:, :], -1.0, None, ALU.add))
            dve.wait_ge(inverse_done, 1)
            s.mark(v.tensor_scalar(unused[:, :], iota[:, 0:BLOCKS], float(P), lane[:, 1:2], ALU.mult, ALU.add))
            s.mark(v.tensor_scalar(free[:, :], pinv[:, 2, :], -1.0, 1.0, ALU.mult, ALU.add))
            s.after(v.tensor_copy(low[:, :], pinv[:, 1, :]))
            s.after(v.scalar_tensor_tensor(code[:, :], pinv[:, 0, :], float(P), low[:, :], ALU.mult, ALU.add))
            s.after(v.tensor_tensor(free[:, :], free[:, :], unused[:, :], ALU.mult))
            s.mark(v.tensor_tensor(lists["scatter"][:, :], free[:, :], code[:, :], ALU.add))
            s.after(v.tensor_scalar(wrap[:, :], code[:, :], float(TOKENS), -float(TOKENS), ALU.is_ge, ALU.mult))
            s.after(v.tensor_tensor(lists["gather"][:, :], code[:, :], wrap[:, :], ALU.add))


def experts(nc, name, layer, ident, lists, xn_rows, y_rows, up, down, bup, bdown, weights_ready, ff):
    FC = ff // P
    UP = E * 4

    def reached(engine, sem, value):
        if not isinstance(value, int) or value > 0:
            engine.wait_ge(sem, value)

    with phase(nc) as ctx:
        sb = lambda n, s, d=F32: ctx.enter_context(nc.sbuf_tensor(f"{name}_{n}", s, d))
        sem = lambda n: nc.alloc_semaphore(f"{name}_{n}")
        ps = lambda n, s: ctx.enter_context(nc.psum_tensor(f"{name}_{n}", s, F32))
        xg = sb("xg", [P, 2, E])
        xT = sb("xT", [P, 2, EC, P])
        h = sb("h", [P, 2, UP])
        a = sb("a", [P, 2, ff]) if layer == 0 else h
        aT = sb("aT", [P, FC, P])
        y = sb("y", [P, 2, E])
        sig = sb("sig", [P, ff]) if layer == 0 else None
        pxT = ps("pxT", [P, BANK])
        ph = ps("ph", [P, 2, UP])
        paT = ps("paT", [P, max(FC, 4), P])
        py = ps("py", [P, BANK])
        gathered = [sem(f"gathered{q}") for q in range(2)]
        scattered = [sem(f"scattered{q}") for q in range(2)]
        xT_done, xT_out, h_done, h_out, a_done, aT_done, aT_out, y_done, y_out = (
            sem(n) for n in ("xT_done", "xT_out", "h_done", "h_out", "a_done", "aT_done", "aT_out", "y_done", "y_out"))
        step, gate_ready, sig_ready = sem("step"), sem("gate_ready"), sem("sig_ready")
        block = ctx.enter_context(nc.Block())

        def steps(engine, body):
            for s in range(3):
                body(s, s % 2, s == 0, False)
            with engine.Fori(1, (BLOCKS - 2) // 2) as i:
                for k in (1, 2):
                    body(i * 2 + k, k % 2, False, False)
            body(BLOCKS - 1, (BLOCKS - 1) % 2, False, True)
            body(BLOCKS, BLOCKS % 2, False, True)

        @block.gpsimd
        def _(pool):
            def gather(b):
                if b >= 2:
                    pool.wait_ge(xT_done, b - 1)
                nc.gpsimd.indirect_dma_start(xg[:, b % 2, :], None, xn_rows,
                                             bass.IndirectOffsetOnAxis(ap=lists["gather"][:, b:b + 1], axis=0)
                                             ).then_inc(gathered[b % 2], 16)

            gather(0)
            gather(1)
            for b in range(BLOCKS):
                if b + 2 < BLOCKS:
                    gather(b + 2)
                pool.wait_ge(y_out, b + 1)
                nc.gpsimd.indirect_dma_start(y_rows, bass.IndirectOffsetOnAxis(ap=lists["scatter"][:, b:b + 1], axis=0),
                                             y[:, b % 2, :], None).then_inc(scattered[b % 2], 16)
            for q in range(2):
                pool.wait_ge(scattered[q], 16 * (BLOCKS // 2))

        @block.tensor
        def _(pe):
            def turn_x(b, q, rounds):
                pe.wait_ge(gathered[q], rounds)
                for c in range(EC):
                    ins = nc.tensor.transpose(pxT[:, c * P:(c + 1) * P], xg[:, q, c * P:(c + 1) * P], ident[:, :])
                ins.then_inc(xT_done, 1)

            def body(s, q, first, last):
                if first:
                    turn_x(0, 0, 16)
                    pe.wait_ge(weights_ready[0], weights_ready[1])
                if not isinstance(s, int) or s < BLOCKS:
                    e = pe.value_load(lists["expert"][0:1, bass.ds(s, 1)], min_val=0, max_val=NE - 1)
                    pe.wait_ge(xT_out, s + 1)
                    if not first:
                        reached(pe, h_out, s - 1)
                    for half in range(UP // BANK):
                        for c in range(EC):
                            cols = slice(half * BANK, (half + 1) * BANK)
                            ins = nc.tensor.matmul(ph[:, q, cols], xT[:, q, c, :],
                                                   up[:, bass.ds(e, 1), c, cols].rearrange("p a n -> p (a n)"),
                                                   start=c == 0, stop=c == EC - 1)
                    ins.then_inc(h_done, 1)
                if not first:
                    pe.wait_ge(a_done, s)
                    for f in range(FC):
                        ins = nc.tensor.transpose(paT[:, f, :], a[:, 1 - q, f * P:(f + 1) * P], ident[:, :])
                    ins.then_inc(aT_done, 1)
                if not isinstance(s, int) or s + 1 < BLOCKS:
                    turn_x(s + 1, 1 - q, 8 * (s + 1 - (1 - q)) + 16)
                if not first:
                    e = pe.value_load(lists["expert"][0:1, bass.ds(s - 1, 1)], min_val=0, max_val=NE - 1)
                    pe.wait_ge(aT_out, s)
                    reached(pe, y_out, s - 1)
                    for f in range(FC):
                        ins = nc.tensor.matmul(py[:, 0:E], aT[:, f, :],
                                               down[:, bass.ds(e, 1), f, :].rearrange("p a n -> p (a n)"),
                                               start=f == 0, stop=f == FC - 1)
                    ins.then_inc(y_done, 1)

            steps(pe, body)

        @block.scalar
        def _(act):
            def copy_x(b, q, first):
                act.wait_ge(xT_done, b + 1)
                if not first:
                    reached(act, h_done, b - 1)
                nc.scalar.activation(xT[:, q, :, :], pxT[:, 0:E].rearrange("p (c n) -> p c n", c=EC), ACT.Copy).then_inc(xT_out, 1)

            def body(s, q, first, last):
                if first:
                    copy_x(0, 0, True)
                else:
                    act.wait_ge(aT_done, s)
                    reached(act, y_done, s - 1)
                    nc.scalar.activation(aT[:, :, :], paT[:, 0:FC, :], ACT.Copy).then_inc(aT_out, 1)
                if not isinstance(s, int) or s + 1 < BLOCKS:
                    copy_x(s + 1, 1 - q, first)
                if not isinstance(s, int) or s < BLOCKS:
                    if layer == 1:
                        act.wait_ge(h_out, s + 1)
                        nc.scalar.activation(a[:, q, :], h[:, q, :], ACT.Gelu).then_inc(a_done, 1)
                    else:
                        act.wait_ge(gate_ready, s + 1)
                        if not first:
                            act.wait_ge(a_done, s)
                        nc.scalar.activation(sig[:, :], h[:, q, 0:ff], ACT.Sigmoid, scale=1.702).then_inc(sig_ready, 1)

            steps(act, body)

        @block.vector
        def _(dve):
            v = nc.vector
            dve.wait_ge(weights_ready[0], weights_ready[1])

            def body(s, q, first, last):
                if not isinstance(s, int) or s < BLOCKS:
                    e = dve.value_load(lists["expert"][0:1, bass.ds(s, 1)], min_val=0, max_val=NE - 1)
                    dve.wait_ge(h_done, s + 1)
                    if not first:
                        reached(dve, a_done if layer == 0 else aT_done, s - 1)
                    v.tensor_tensor(h[:, q, :], ph[:, q, :], bup[:, bass.ds(e, 1), :].rearrange("p a n -> p (a n)"),
                                    ALU.add).then_inc(h_out, 1)
                    if layer == 0:
                        dve.wait_ge(h_out, s + 1)
                        v.tensor_scalar(h[:, q, 0:ff], h[:, q, 0:ff], 7.0, None, ALU.min).then_inc(gate_ready, 1)
                        v.tensor_scalar(h[:, q, ff:], h[:, q, ff:], 7.0, -7.0, ALU.min, ALU.max).then_inc(step, 1)
                if not first:
                    e = dve.value_load(lists["expert"][0:1, bass.ds(s - 1, 1)], min_val=0, max_val=NE - 1)
                    dve.wait_ge(y_done, s)
                    reached(dve, scattered[1 - q], 8 * (s - 1 - (1 - q)))
                    v.tensor_tensor(y[:, 1 - q, :], py[:, 0:E], bdown[:, bass.ds(e, 1), :].rearrange("p a n -> p (a n)"),
                                    ALU.add).then_inc(y_out, 1)
                if layer == 0 and (not isinstance(s, int) or s < BLOCKS):
                    dve.wait_ge(sig_ready, s + 1)
                    if not first:
                        reached(dve, aT_done, s - 1)
                    v.tensor_tensor(a[:, q, :], h[:, q, 0:ff], sig[:, :], ALU.mult).then_inc(step, 1)
                    dve.wait_ge(step, s * 2 + 2)
                    v.scalar_tensor_tensor(a[:, q, :], h[:, q, ff:], 1.0, a[:, q, :], ALU.add, ALU.mult).then_inc(a_done, 1)

            steps(dve, body)


def combine(nc, name, gates, y_rows, xres):
    with phase(nc) as ctx:
        got = [ctx.enter_context(nc.sbuf_tensor(f"{name}_got{i}", [P, TOPK, E], F32)) for i in range(4)]
        loaded = [nc.alloc_semaphore(f"{name}_loaded{i}") for i in range(4)]
        added, half = nc.alloc_semaphore(f"{name}_added"), nc.alloc_semaphore(f"{name}_half")
        rows = y_rows[0:DUMP, :].rearrange("(k t p) e -> t p k e", k=TOPK, p=P)
        block = ctx.enter_context(nc.Block())

        @block.sync
        def _(sp):
            for t in range(TILES):
                if t >= 4:
                    sp.wait_ge(added, t - 3)
                sp.dma_start(got[t % 4][:, :, :], rows[t]).then_inc(loaded[t % 4], 16)

        @block.vector
        def _(dve):
            for t in range(TILES):
                dve.wait_ge(loaded[t % 4], 16 * (t // 4 + 1))
                nc.vector.scalar_tensor_tensor(xres[:, t, :], got[t % 4][:, 0, :], gates[:, 0, t:t + 1], xres[:, t, :],
                                               ALU.mult, ALU.add).then_inc(half, 1)
                dve.wait_ge(half, t + 1)
                nc.vector.scalar_tensor_tensor(xres[:, t, :], got[t % 4][:, 1, :], gates[:, 1, t:t + 1], xres[:, t, :],
                                               ALU.mult, ALU.add).then_inc(added, 1)


def mixture(nc, I, xres, ident, layer):
    name = f"m{layer}"
    ff = 512 if layer == 0 else 1024
    FC = ff // P
    wup, wbup, wdown, wbdown = (
        ("L0_ffn_gate_up_proj", "L0_ffn_gate_up_bias", "L0_ffn_down_proj", "L0_ffn_down_bias") if layer == 0 else
        ("L1_ffn_W1", "L1_ffn_b1", "L1_ffn_W2", "L1_ffn_b2"))
    xn_rows = nc.dram_tensor(f"{name}_xn_rows", [TOKENS, E], F32).ap()
    y_rows = nc.dram_tensor(f"{name}_y_rows", [DUMP + BLOCKS * P, E], F32).ap()
    with phase(nc) as ctx:
        gates = ctx.enter_context(nc.sbuf_tensor(f"{name}_gates", [P, TOPK, TILES], F32))
        with ExitStack() as c2:
            sb = lambda n, s, d=F32: c2.enter_context(nc.sbuf_tensor(f"{name}_{n}", s, d))
            lists = {"gates": gates, "gather": sb("gather", [P, BLOCKS], U32), "scatter": sb("scatter", [P, BLOCKS], U32),
                     "expert": sb("expert", [P, BLOCKS], I32)}
            weights_loaded = nc.alloc_semaphore(f"{name}_weights_loaded")
            up = sb("up", [P, NE, EC, E * 4])
            bup, bdown = sb("bup", [P, NE, E * 4]), sb("bdown", [P, NE, E])
            with nc.Block() as block:
                @block.sync
                def _(sp):
                    for e in range(NE):
                        sp.dma_start(up[:, e], I[wup][e].rearrange("(c p) n -> p c n", p=P)).then_inc(weights_loaded, 16)
                    sp.dma_start(bup[:, :, :].rearrange("p e n -> p (e n)"),
                                 I[wbup].to_broadcast([P, NE * E * 4])).then_inc(weights_loaded, 16)
                    sp.dma_start(bdown[:, :, :].rearrange("p e n -> p (e n)"),
                                 I[wbdown].to_broadcast([P, NE * E])).then_inc(weights_loaded, 16)
            with ExitStack() as c3:
                xn = c3.enter_context(nc.sbuf_tensor(f"{name}_xn", [P, TILES, E], F32))
                xnT = c3.enter_context(nc.sbuf_tensor(f"{name}_xnT", [P, EC, TOKENS], F32))
                layer_norm(nc, f"{name}ln", xres, xn, ident, xnT, store=xn_rows)
                route(nc, f"{name}r", I, layer, xnT, lists)
            down = sb("down", [P, NE, FC, E])
            with nc.Block() as block:
                @block.sync
                def _(sp):
                    for e in range(NE):
                        sp.dma_start(down[:, e], I[wdown][e].rearrange("(c p) n -> p c n", p=P)).then_inc(weights_loaded, 16)
            experts(nc, f"{name}e", layer, ident, lists, xn_rows, y_rows, up, down, bup, bdown,
                    (weights_loaded, 16 * (2 * NE + 2)), ff)
        combine(nc, f"{name}c", gates, y_rows, xres)


class Pair:

    def __init__(self, g, b, hp, parity):
        self.g, self.b, self.hp, self.parity = g, b, hp, parity

    def next(self):
        if isinstance(self.g, int):
            return Pair(self.g + 1, *divmod(self.g + 1, PAIRS), 1 - self.parity) if self.g + 1 < BATCH * PAIRS else None
        return Pair(self.g + 1, self.b, self.hp + 1, 1 - self.parity)


PREPARE = ["K", "Q", "V", "K0", "K1", "Q0", "Q1"]
ORDER = ["K", 0, 1, "Q", 2, 3, "V", 4, 5, 6, 7, "K0", 8, 9, "K1", 10, 11, "Q0", 12, "Q1", 13, 14, 15]
UNITS = 2 * (SEQ // P)
BY_DVE = ("K0", "K1", "Q0", "Q1")
ACT_STEPS, DVE_STEPS = len(ORDER) - len(BY_DVE), len(BY_DVE)


def order(pair):
    last = isinstance(pair.g, int) and pair.g == BATCH * PAIRS - 1
    return [t for t in ORDER if isinstance(t, int)] if last else ORDER


def slots_before(pair):
    return pair.g * len(ORDER) + len(PREPARE)


def reads_of(pair, k):
    own = order(pair)[:k + 1]
    dve = sum(t in BY_DVE for t in own)
    return (pair.g * ACT_STEPS + len(PREPARE) - DVE_STEPS + len(own) - dve, pair.g * DVE_STEPS + DVE_STEPS + dve)


def prepared_by(pair, step):
    if isinstance(pair.g, int) and pair.g == 0:
        k = PREPARE.index(step)
        dve = sum(t in BY_DVE for t in PREPARE[:k + 1])
        return k + 1, k + 1 - dve, dve
    k = ORDER.index(step)
    dve = sum(t in BY_DVE for t in ORDER[:k + 1])
    g = pair.g - 1
    return (g * len(ORDER) + len(PREPARE) + k + 1, g * ACT_STEPS + len(PREPARE) - DVE_STEPS + k + 1 - dve,
            g * DVE_STEPS + DVE_STEPS + dve)


def all_pairs(engine, body):
    for b in range(BATCH):
        with engine.Fori(0, PAIRS // 2 - 1) as i:
            for r in range(2):
                body(Pair(i * 2 + (b * PAIRS + r), b, i * 2 + r, r))
        for hp in (PAIRS - 2, PAIRS - 1):
            body(Pair(b * PAIRS + hp, b, hp, hp % 2))


def layer1_attention(nc, I, xres, ident):
    with phase(nc) as outer:
        o_rows = nc.dram_tensor("a1_o_rows", [TOKENS, H1 * D1], F32).ap()
        attn = outer.enter_context(ExitStack())
        sb = lambda n, s, d=F32: attn.enter_context(nc.sbuf_tensor(f"a1_{n}", s, d))
        sem = lambda n: nc.alloc_semaphore(f"a1_{n}")
        latT = sb("latT", [P, EC, TOKENS])
        ctxT = sb("ctxT", [P, EC, BATCH * CTX])
        Wq = sb("Wq", [P, EC, H1 * D1])
        Wkv = sb("Wkv", [P, EC, 2 * H1 * D1])
        maskbias = sb("maskbias", [P, BATCH, CTX])
        gamma = sb("gamma", [P, 1])

        with ExitStack() as c2:
            sb2 = lambda n, s, d=F32: c2.enter_context(nc.sbuf_tensor(f"a1n_{n}", s, d))
            sem2 = lambda n: nc.alloc_semaphore(f"a1n_{n}")
            lat = sb2("lat", [P, TILES, E])
            lat2 = sb2("lat2", [P, TILES, E])
            lng, lnb = sb2("lng", [P, EC]), sb2("lnb", [P, EC])
            cng, cnb = sb2("cng", [P, EC]), sb2("cnb", [P, EC])
            qg, kg = sb2("qg", [P, 1]), sb2("kg", [P, 1])
            mask = sb2("mask", [P, BATCH, CTX], U8)
            c = sb2("c", [CTX, BATCH, E])
            stats, moments = sb2("stats", [CTX, BATCH, 6]), sb2("moments", [CTX, BATCH, 2])
            var, expo, rstd = sb2("var", [CTX, BATCH]), sb2("expo", [CTX, BATCH]), sb2("rstd", [CTX, BATCH])
            cn = sb2("cn", [CTX, BATCH, E])
            pc = c2.enter_context(nc.psum_tensor("a1_pc", [P, EC, BATCH, 128], F32))
            loaded, step, expo_set, var_done, rstd_done = (sem2(n) for n in ("loaded", "step", "expo_set", "var_done", "rstd_done"))
            cn_done, pc_done, ctxT_done, gamma_done = (sem2(n) for n in ("cn_done", "pc_done", "ctxT_done", "gamma_done"))
            with nc.Block() as block:
                @block.sync
                def _(sp):
                    for dst, src in ((lng, "ln_l_g"), (lnb, "ln_l_b"), (cng, "ln_x_g"), (cnb, "ln_x_b")):
                        sp.dma_start(dst[:, :], I[f"L1_xattn_{src}"]).then_inc(loaded, 16)
                    sp.dma_start(qg[:, :], I["L1_xattn_qn_g"]).then_inc(loaded, 16)
                    sp.dma_start(kg[:, :], I["L1_xattn_kn_g"]).then_inc(loaded, 16)
                    sp.dma_start(mask[:, :, :].rearrange("p b k -> p (b k)"),
                                 I["mask"].to_broadcast([P, BATCH * CTX])).then_inc(loaded, 16)
                    sp.dma_start(c[:, :, :], I["ctx"].rearrange("b k e -> k b e")).then_inc(loaded, 16)
                    sp.dma_start(Wq[:, :, :], I["L1_xattn_Wq"].rearrange("(c p) n -> p c n", p=P)).then_inc(loaded, 16)
                    sp.dma_start(Wkv[:, :, :], I["L1_xattn_Wkv"].rearrange("(c p) n -> p c n", p=P)).then_inc(loaded, 16)
                    sp.wait_ge(loaded, 160)

                @block.gpsimd
                def _(pool):
                    nc.gpsimd.memset(expo[:, :], -0.5).then_inc(expo_set, 1)
                    pool.wait_ge(expo_set, 1)
                    pool.wait_ge(var_done, 1)
                    nc.gpsimd.tensor_tensor(rstd[:, :], var[:, :], expo[:, :], ALU.pow).then_inc(rstd_done, 1)

                @block.vector
                def _(dve):
                    s = Steps(dve, step)
                    v = nc.vector
                    dve.wait_ge(loaded, 160)
                    s.mark(v.tensor_scalar(maskbias[:, :, :], mask[:, :, :], 3e38, -3e38, ALU.mult, ALU.add))
                    s.mark(v.scalar_tensor_tensor(gamma[:, :], qg[:, :], D1 ** -0.5, kg[:, :], ALU.mult, ALU.mult))
                    for b in range(BATCH):
                        s.after(v.bn_stats(stats[:, b, :], c[:, b, :]))
                        s.after(v.bn_aggr(moments[:, b, :], stats[:, b, :]))
                    v.tensor_scalar(var[:, :], moments[:, :, 1], LN_EPS, None, ALU.add).then_inc(var_done, 1)
                    dve.wait_ge(rstd_done, 1)
                    for b in range(BATCH):
                        v.tensor_scalar(cn[:, b, :], c[:, b, :], moments[:, b, 0:1], rstd[:, b:b + 1],
                                        ALU.subtract, ALU.mult).then_inc(cn_done, 1)

                @block.tensor
                def _(pe):
                    pe.wait_ge(cn_done, BATCH)
                    for b in range(BATCH):
                        for e in range(EC):
                            ins = nc.tensor.transpose(pc[:, e, b, 0:CTX], cn[:, b, e * P:(e + 1) * P], ident[0:CTX, 0:CTX])
                    ins.then_inc(pc_done, 1)

                @block.scalar
                def _(act):
                    act.wait_ge(loaded, 160)
                    act.wait_ge(pc_done, 1)
                    for e in range(EC):
                        nc.scalar.activation(ctxT[:, e, :].rearrange("p (b k) -> p b k", b=BATCH), pc[:, e, :, 0:CTX],
                                             ACT.Identity, bias=cnb[:, e:e + 1], scale=cng[:, e:e + 1])
            layer_norm(nc, "a1lat", xres, lat, ident)
            layer_norm(nc, "a1ln", lat, lat2, ident, latT, gain=lng, shift=lnb)

        W2 = KEYS + 1
        S = SEQ // P
        KHL = sb("KHL", [P, 2, 2, 2, W2], F32R)
        QHL = sb("QHL", [P, 2, 2, SEQ], F32R)
        V1 = sb("V1", [P, 2, KT_TILES, 2, D1 + 1])
        knat, qnat = sb("knat", [P, KT_TILES, P]), sb("qnat", [P, S, P])
        ksq, qsq = sb("ksq", [P, KT_TILES, P]), sb("qsq", [P, S, P])
        kvar, qvar = sb("kvar", [P, KT_TILES * 2]), sb("qvar", [P, S * 2])
        kinv, qinv = sb("kinv", [P, KT_TILES * 2]), sb("qinv", [P, S * 2])
        expo = sb("expo", [P, KT_TILES * 2])
        kdup = sb("kdup", [P, KT_TILES, 2, 2, D1])
        qdup = sb("qdup", [P, S, 2, 2, D1])
        qgam = sb("qgam", [P, SEQ])
        npeak = sb("npeak", [P, 2])
        prob = sb("prob", [P, 2, KEYS])
        probT = sb("probT", [P, 2, KT_TILES, P])
        rsum = sb("rsum", [P, 1])
        O = sb("O", [P, 2, S, P])
        slot = [attn.enter_context(nc.psum_tensor(f"a1_slot{i}", [P, 3 * BANK], F32)) for i in range(2)]
        pt = attn.enter_context(nc.psum_tensor("a1_pt", [P, 4, P], F32))
        po = attn.enter_context(nc.psum_tensor("a1_po", [P, BANK], F32))
        filled, act_freed, dve_freed = sem("filled"), sem("act_freed"), sem("dve_freed")
        set_up, padded, squared, meaned, powered, scaled, summed = (
            sem(n) for n in ("set_up", "padded", "squared", "meaned", "powered", "scaled", "summed"))
        khigh, qhigh, qlow, masked, peaked = (sem(n) for n in ("khigh", "qhigh", "qlow", "masked", "peaked"))
        turned, turned_act, turned_dve, weighed, rsum_done, o_out = (
            sem(n) for n in ("turned", "turned_act", "turned_dve", "weighed", "rsum_done", "o_out"))
        o_stored = [sem(f"o_stored{i}") for i in range(2)]
        NSET = 6
        block = attn.enter_context(nc.Block())

        @block.sync
        def _(sp):
            for i in range(2):
                sp.sem_inc(o_stored[i], 16)

            def body(pair):
                sp.wait_ge(o_out, pair.g * UNITS + (UNITS + 1))
                rows = o_rows[pair.b * SEQ:(pair.b + 1) * SEQ, :].rearrange("(t p) n -> p t n", p=P)
                hp = pair.hp
                cols = bass.ds(hp * P, P)
                sp.dma_start(rows[:, :, cols], O[:, pair.parity, :, :]).then_inc(o_stored[pair.parity], 16)

            all_pairs(sp, body)
            for i in range(2):
                sp.wait_ge(o_stored[i], 16 * BATCH * PAIRS // 2 + 16)

        @block.gpsimd
        def _(pool):
            g_ = nc.gpsimd
            g_.memset(expo[:, :], -0.5).then_inc(set_up, 1)
            g_.memset(knat[:, KT_TILES - 1, :], 0.0).then_inc(set_up, 1)
            for p in range(2):
                for h in range(2):
                    g_.memset(V1[:, p, :, h, D1:D1 + 1], 1.0).then_inc(set_up, 1)
            pool.wait_ge(set_up, NSET)

            def body(pair, first):
                n = pair.g
                for nat, sq, step in ((knat, ksq, "K"), (qnat, qsq, "Q")):
                    pool.wait_ge(act_freed, prepared_by(pair, step)[1])
                    if not first:
                        pool.wait_ge(meaned, n * 2)
                    g_.tensor_tensor(sq[:, :, :], nat[:, :, :], nat[:, :, :], ALU.mult).then_inc(squared, 1)
                for j, (nat, dup, var, inv, last) in enumerate(((knat, kdup, kvar, kinv, "K1"), (qnat, qdup, qvar, qinv, "Q1"))):
                    tiles = nat.shape[1]
                    pool.wait_ge(meaned, n * 2 + (j + 1))
                    g_.tensor_tensor(inv[:, :], var[:, :], expo[:, 0:2 * tiles], ALU.pow).then_inc(powered, 1)
                    pool.wait_ge(powered, n * 2 + (j + 1))
                    if not first:
                        before = Pair(pair.g - 1, 0, 0, 0)
                        pool.wait_ge(filled, prepared_by(before, last)[0] if isinstance(pair.g, int) else
                                     (pair.g - 2) * len(ORDER) + (len(PREPARE) + ORDER.index(last) + 1))
                    for h in range(2):
                        src = nat[:, :, h * D1:(h + 1) * D1]
                        scale = inv[:, :].rearrange("p (t h) -> p t h", h=2)[:, :, h:h + 1].to_broadcast([P, tiles, D1])
                        for d in range(2):
                            ins = g_.tensor_tensor(dup[:, :, h, d, :], src, scale, ALU.mult)
                    ins.then_inc(scaled, 1)

            body(Pair(0, 0, 0, 0), True)
            body(Pair(1, 0, 0, 0), False)
            with pool.Fori(2, BATCH * PAIRS) as g:
                body(Pair(g, 0, 0, 0), False)

        @block.tensor
        def _(pe):
            t_ = nc.tensor

            def fill(pair, step, sl, wait):
                if wait:
                    pe.wait_ge(*wait)
                out = slot[sl]
                b = pair.b
                if step in ("K", "V", "Q"):
                    W, off = {"K": (Wkv, 0), "V": (Wkv, H1 * D1), "Q": (Wq, 0)}[step]
                    hp = pair.hp
                    for j in range(S if step == "Q" else KT_TILES):
                        lhs = latT[:, :, b * SEQ + j * P:b * SEQ + (j + 1) * P] if j < S else ctxT[:, :, b * CTX:(b + 1) * CTX]
                        for c in range(EC):
                            ins = t_.matmul(out[0:P if j < S else CTX, j * P:(j + 1) * P], lhs[:, c, :],
                                            W[:, c, bass.ds(hp * P + off, P)], start=c == 0, stop=c == EC - 1)
                elif step in BY_DVE:
                    h = int(step[1])
                    pe.wait_ge(scaled, pair.g * 2 + (1 if step[0] == "K" else 2))
                    dup = kdup if step[0] == "K" else qdup
                    for j in range(S):
                        ins = t_.transpose(out[:, j * P:(j + 1) * P], dup[:, j, h, :, :].rearrange("p a d -> p (a d)"), ident[:, :])
                    if step[0] == "K":
                        ins = t_.transpose(out[:, SEQ:KEYS], dup[0:CTX, S, h, :, :].rearrange("p a d -> p (a d)"),
                                           ident[0:CTX, 0:CTX])
                else:
                    t, h = divmod(step, 2)
                    if step == 0:
                        pe.wait_ge(dve_freed, pair.g * DVE_STEPS + DVE_STEPS)
                        pe.wait_ge(qlow, pair.g * 2 + 2)
                    q = QHL[:, pair.parity, h, t * P:(t + 1) * P]
                    for lo, hi in ((0, BANK), (BANK, SEQ), (SEQ, W2)):
                        for part in range(2):
                            ins = t_.matmul(out[:, lo:hi], q, KHL[:, pair.parity, h, part, lo:hi],
                                            start=part == 0, stop=part == 1)
                ins.then_inc(filled, 1)

            def turn(pair, u, c):
                n = pair.g * UNITS + u
                par = u % 2
                if c == 0:
                    pe.wait_ge(turned_dve, n + 1)
                else:
                    pe.wait_ge(turned_act, n * 2 + c)
                if c < 2:
                    for j in range(4):
                        k = (4 * c + j) * P
                        ins = t_.transpose(pt[:, j, :], prob[:, par, k:k + P], ident[:, :])
                else:
                    ins = t_.transpose(pt[0:CTX, 0, :], prob[:, par, SEQ:KEYS], ident[:, :])
                ins.then_inc(turned, 1)

            def weigh(pair, u, c):
                n = pair.g * UNITS + u
                if c == 0:
                    pe.wait_ge(o_out, n + 1)
                if c < 2:
                    pe.wait_ge(turned_act, n * 2 + (c + 1))
                else:
                    pe.wait_ge(turned_dve, n + 2)
                for j in range(4 * c, min(4 * c + 4, KT_TILES)):
                    rows = P if j < S else CTX
                    ins = t_.matmul(po[:, 0:D1 + 1], probT[0:rows, u % 2, j, :], V1[0:rows, pair.parity, j, u % 2, :],
                                    start=j == 0, stop=j == S)
                if c == 2:
                    ins.then_inc(weighed, 1)

            pe.sem_inc(turned, 3 * 2)
            pe.sem_inc(weighed, 2)
            start = Pair(0, 0, 0, 0)
            for k, step in enumerate(PREPARE):
                n = k - 2
                wait = None
                if n >= 0:
                    _, a, d = prepared_by(start, PREPARE[n])
                    wait = (dve_freed, d) if PREPARE[n] in BY_DVE else (act_freed, a)
                fill(start, step, k % 2, wait)
            pe.wait_ge(padded, 8)
            for k in range(2):
                _, a, d = prepared_by(start, PREPARE[len(PREPARE) - 2 + k])
                fill(start if isinstance(ORDER[k], int) else start.next(), ORDER[k], (len(PREPARE) + k) % 2, (dve_freed, d))

            def body(pair):
                steps, after = order(pair), pair.next()
                more = steps + (order(after)[0:2] if after else [])
                for k, step in enumerate(steps):
                    nxt = None
                    if k + 2 < len(more):
                        owner = pair if k + 2 < len(steps) else after
                        target = more[k + 2]
                        who = owner if isinstance(target, int) else owner.next()
                        a, d = reads_of(pair, k)
                        wait = (dve_freed, d) if step in BY_DVE else (act_freed, a)
                        nxt = (who, target, (len(PREPARE) + pair.parity * len(ORDER) + k) % 2, wait)
                    if isinstance(step, int):
                        pe.wait_ge(act_freed, reads_of(pair, k)[0])
                        turn(pair, step, 0)
                        if nxt:
                            fill(*nxt)
                        turn(pair, step, 1)
                        weigh(pair, step, 0)
                        turn(pair, step, 2)
                        weigh(pair, step, 1)
                        weigh(pair, step, 2)
                    elif nxt:
                        fill(*nxt)

            all_pairs(pe, body)

        @block.scalar
        def _(act):
            a_ = nc.scalar

            def read(pair, step, sl, n):
                act.wait_ge(filled, n)
                src = slot[sl]
                if step in ("K", "Q", "V"):
                    tiles = S if step == "Q" else KT_TILES
                    if step == "V":
                        def dst(r, lo, hi):
                            return V1[0:r, pair.parity, lo:hi, :, 0:D1]
                    else:
                        nat = knat if step == "K" else qnat
                        if not (isinstance(pair.g, int) and pair.g == 0):
                            act.wait_ge(scaled, pair.g * 2 - (1 if step == "K" else 0))

                        def dst(r, lo, hi):
                            return nat[0:r, lo:hi, :].rearrange("p t (h d) -> p t h d", h=2)
                    view = src[:, 0:tiles * P].rearrange("p (t h d) -> p t h d", h=2, d=D1)
                    if isinstance(pair.g, int) and pair.g == 0 and step == "K":
                        act.wait_ge(set_up, NSET)
                    ins = a_.activation(dst(P, 0, S), view[:, 0:S], ACT.Copy)
                    if tiles > S:
                        ins = a_.activation(dst(CTX, S, tiles), view[0:CTX, S:tiles], ACT.Copy)
                    ins.then_inc(act_freed, 1)
                elif step in ("K0", "K1"):
                    a_.activation(KHL[:, pair.parity, int(step[1]), 0, 0:KEYS], src[:, 0:KEYS], ACT.Copy).then_inc(khigh, 1)
                elif isinstance(step, int):
                    u = pair.g * UNITS + step
                    act.wait_ge(peaked, u + 1)
                    act.wait_ge(turned, u * 3 + 3)
                    a_.activation(prob[:, step % 2, :], src[:, 0:KEYS], ACT.Exp, bias=npeak[:, step % 2:step % 2 + 1]
                                  ).then_inc(act_freed, 1)

            def copy(pair, u, c):
                n = pair.g * UNITS + u
                act.wait_ge(turned, n * 3 + (c + 7))
                if c == 0:
                    act.wait_ge(weighed, n + 1)
                a_.activation(probT[:, u % 2, 4 * c:4 * c + 4, :], pt[:, :, :], ACT.Copy).then_inc(turned_act, 1)

            start = Pair(0, 0, 0, 0)
            for k, step in enumerate(PREPARE):
                read(start, step, k % 2, k + 1)

            def first_read(pair, target_pair):
                steps = order(pair)
                step = steps[0]
                read(pair if isinstance(step, int) else target_pair, step,
                     (len(PREPARE) + pair.parity * len(ORDER)) % 2, slots_before(pair) + 1)

            first_read(start, start.next())

            def body(pair):
                steps, after = order(pair), pair.next()
                for k, step in enumerate(steps):
                    if isinstance(step, int):
                        copy(pair, step, 0)
                        copy(pair, step, 1)
                    if k + 1 < len(steps):
                        target = steps[k + 1]
                        read(pair if isinstance(target, int) else after, target,
                             (len(PREPARE) + pair.parity * len(ORDER) + k + 1) % 2, slots_before(pair) + (k + 2))
                    elif after:
                        first_read(after, after.next())

            all_pairs(act, body)

        @block.vector
        def _(dve):
            v = nc.vector
            dve.sem_inc(turned_dve, 1)
            dve.sem_inc(o_out, 1)
            for p in range(2):
                for h in range(2):
                    for part in range(2):
                        v.memset(KHL[:, p, h, part, KEYS:W2].bitcast(F32), 0.0).then_inc(padded, 1)

            def read(pair, step, sl, n):
                src = slot[sl]
                if isinstance(step, int):
                    u = pair.g * UNITS + step
                    dve.wait_ge(filled, n)
                    v.tensor_tensor(src[:, SEQ:KEYS], src[:, SEQ:KEYS], maskbias[:, pair.b, :], ALU.add).then_inc(masked, 1)
                    dve.wait_ge(masked, u + 1)
                    if step >= 2 or not (isinstance(pair.g, int) and pair.g == 0):
                        dve.wait_ge(act_freed, exp_done(pair, step - 2))
                    v.tensor_reduce(npeak[:, step % 2:step % 2 + 1], src[:, 0:KEYS], AX.X, ALU.max, negate=True).then_inc(peaked, 1)
                elif step in ("K0", "K1"):
                    h = int(step[1])
                    dve.wait_ge(khigh, pair.g * 2 + (h + 1))
                    k = KHL[:, pair.parity, h]
                    v.tensor_tensor(k[:, 1, 0:KEYS], src[:, 0:KEYS], k[:, 0, 0:KEYS], ALU.subtract).then_inc(dve_freed, 1)
                elif step in ("Q0", "Q1"):
                    h = int(step[1])
                    q = QHL[:, pair.parity, h]
                    dve.wait_ge(filled, n)
                    if h or not (isinstance(pair.g, int) and pair.g == 0):
                        dve.wait_ge(qlow, pair.g * 2 + h)
                    v.tensor_scalar(qgam[:, :], src[:, 0:SEQ], gamma[:, 0:1], None, ALU.mult).then_inc(dve_freed, 1)
                    dve.wait_ge(dve_freed, pair.g * DVE_STEPS + (3 + h))
                    v.tensor_copy(q[:, :], qgam[:, :]).then_inc(qhigh, 1)
                    dve.wait_ge(qhigh, pair.g * 2 + (h + 1))
                    v.tensor_tensor(q[D1:, :], qgam[D1:, :], q[D1:, :], ALU.subtract).then_inc(qlow, 1)

            def exp_done(pair, step):
                if step < 0:
                    g, k = pair.g - 1, ORDER.index(UNITS + step)
                else:
                    g, k = pair.g, order(pair).index(step)
                own = (order(pair) if step >= 0 else ORDER)[:k + 1]
                return g * ACT_STEPS + (len(PREPARE) - DVE_STEPS + len(own) - sum(t in BY_DVE for t in own))

            def sums(pair, j):
                sq, var = ((ksq, kvar), (qsq, qvar))[j]
                n = pair.g * 2 + (j + 1)
                dve.wait_ge(squared, n)
                v.tensor_reduce(var[:, :], sq[:, :, :].rearrange("p t (h d) -> p (t h) d", h=2), AX.X, ALU.add).then_inc(summed, 1)
                dve.wait_ge(summed, n)
                v.tensor_scalar(var[:, :], var[:, :], 1.0 / D1, 1e-16, ALU.mult, ALU.max).then_inc(meaned, 1)

            def copy(pair, u):
                n = pair.g * UNITS + u
                dve.wait_ge(turned, n * 3 + 9)
                v.tensor_copy(probT[0:CTX, u % 2, S, :], pt[0:CTX, 0, :]).then_inc(turned_dve, 1)

            def normalise(pair, u):
                n = pair.g * UNITS + u
                dve.wait_ge(weighed, n + 3)
                v.reciprocal(rsum[:, :], po[:, D1:D1 + 1]).then_inc(rsum_done, 1)
                dve.wait_ge(rsum_done, n + 1)
                if u == 0:
                    dve.wait_ge(o_stored[pair.parity], (pair.g - pair.parity) * 8 + 16)
                t, h = divmod(u, 2)
                v.tensor_scalar(O[:, pair.parity, t, h * D1:(h + 1) * D1], po[:, 0:D1], rsum[:, 0:1], None,
                                ALU.mult).then_inc(o_out, 1)

            start = Pair(0, 0, 0, 0)
            sums(start, 0)
            sums(start, 1)
            for k, step in enumerate(PREPARE):
                read(start, step, k % 2, k + 1)

            def first_read(pair):
                if isinstance(order(pair)[0], int):
                    read(pair, order(pair)[0], (len(PREPARE) + pair.parity * len(ORDER)) % 2, slots_before(pair) + 1)

            def body(pair):
                steps, after = order(pair), pair.next()
                for k, step in enumerate(steps):
                    if k + 1 < len(steps):
                        target = steps[k + 1]
                        read(pair if isinstance(target, int) else after, target,
                             (len(PREPARE) + pair.parity * len(ORDER) + k + 1) % 2, slots_before(pair) + (k + 2))
                    elif after:
                        first_read(after)
                    if isinstance(step, int):
                        copy(pair, step)
                        normalise(pair, step)
                        if after and step in (2, 7):
                            sums(after, int(step == 7))

            all_pairs(dve, body)
        attn.close()

        with ExitStack() as c3:
            sb3 = lambda n, s, d=F32: c3.enter_context(nc.sbuf_tensor(f"a1o_{n}", s, d))
            sem3 = lambda n: nc.alloc_semaphore(f"a1o_{n}")
            OC = H1 * D1 // P
            Wout, bout = sb3("Wout", [P, OC, E]), sb3("bout", [P, E])
            o = sb3("o", [P, 4, H1 * D1])
            oT = sb3("oT", [P, 2, OC, P])
            yb = sb3("yb", [P, 2, E])
            pT = [c3.enter_context(nc.psum_tensor(f"a1o_pT{i}", [P, OC, P], F32)) for i in range(2)]
            py = [c3.enter_context(nc.psum_tensor(f"a1o_py{i}", [P, BANK], F32)) for i in range(2)]
            w_loaded, t_done, t_out, y_done, y_out, added = (sem3(n) for n in ("w_loaded", "t_done", "t_out", "y_done", "y_out", "added"))
            o_loaded = [sem3(f"o_loaded{i}") for i in range(4)]
            with nc.Block() as block:
                @block.sync
                def _(sp):
                    sp.dma_start(Wout[:, :, :], I["L1_xattn_Wout"].rearrange("(c p) n -> p c n", p=P)).then_inc(w_loaded, 16)
                    sp.dma_start(bout[:, :], I["L1_xattn_bout"].to_broadcast([P, E])).then_inc(w_loaded, 16)
                    for t in range(TILES):
                        if t >= 4:
                            sp.wait_ge(t_done, t - 3)
                        sp.dma_start(o[:, t % 4, :], o_rows[t * P:(t + 1) * P, :]).then_inc(o_loaded[t % 4], 16)

                @block.tensor
                def _(pe):
                    def project(t):
                        pe.wait_ge(t_out, t + 1)
                        if t >= 2:
                            pe.wait_ge(y_out, t - 1)
                        for c in range(OC):
                            ins = nc.tensor.matmul(py[t % 2][:, 0:E], oT[:, t % 2, c, :], Wout[:, c, :],
                                                   start=c == 0, stop=c == OC - 1)
                        ins.then_inc(y_done, 1)

                    pe.wait_ge(w_loaded, 32)
                    for t in range(TILES):
                        pe.wait_ge(o_loaded[t % 4], 16 * (t // 4 + 1))
                        if t >= 2:
                            pe.wait_ge(t_out, t - 1)
                        for c in range(OC):
                            ins = nc.tensor.transpose(pT[t % 2][:, c, :], o[:, t % 4, c * P:(c + 1) * P], ident[:, :])
                        ins.then_inc(t_done, 1)
                        if t:
                            project(t - 1)
                    project(TILES - 1)

                @block.scalar
                def _(act):
                    for t in range(TILES):
                        act.wait_ge(t_done, t + 1)
                        if t >= 2:
                            act.wait_ge(y_done, t - 1)
                        nc.scalar.activation(oT[:, t % 2, :, :], pT[t % 2][:, :, :], ACT.Copy).then_inc(t_out, 1)

                @block.vector
                def _(dve):
                    dve.wait_ge(w_loaded, 32)
                    for t in range(TILES):
                        dve.wait_ge(y_done, t + 1)
                        if t >= 2:
                            dve.wait_ge(added, t - 1)
                        nc.vector.tensor_tensor(yb[:, t % 2, :], py[t % 2][:, 0:E], bout[:, :], ALU.add).then_inc(y_out, 1)
                        dve.wait_ge(y_out, t + 1)
                        nc.vector.tensor_tensor(xres[:, t, :], xres[:, t, :], yb[:, t % 2, :], ALU.add).then_inc(added, 1)
                    dve.wait_ge(added, TILES)


def layer0_mixture(nc, I, xres, ident):
    mixture(nc, I, xres, ident, 0)


def layer1_mixture(nc, I, xres, ident):
    mixture(nc, I, xres, ident, 1)


PHASES = [layer0_attention, layer0_mixture, layer1_attention, layer1_mixture]


def lay_out(inputs):
    a = {n: np.asarray(v) for n, v in inputs.items()}
    out = {"x": a["x"], "ident": np.eye(P, dtype=np.float32)}
    for n in ("Wq", "Wk", "Wv", "Wo"):
        out[f"L0_xattn_{n}T"] = a[f"L0_xattn_{n}"].T
    out["ctxT"] = a["ctx_1024"].reshape(BATCH * CTX, E).T
    for n in ("bq", "bk"):
        out[f"L0_xattn_{n}"] = a[f"L0_xattn_{n}"].reshape(EC, P).T
    for n in ("bv", "bo"):
        out[f"L0_xattn_{n}"] = a[f"L0_xattn_{n}"].reshape(1, E)
    out["head_mask"] = (np.arange(P)[:, None] // D0 == np.arange(GROUP)).astype(np.float32)
    rows = np.clip(np.arange(BAND)[None, :] - (P - 1) - P * np.arange(NEAR)[:, None], -REACH, REACH) + REACH
    out["rel_k"] = np.tile(np.moveaxis(a["L0_xattn_rk_table"][rows], 2, 0), (GROUP, 1, 1))
    out["rel_v"] = a["L0_xattn_rv_table"][rows].reshape(NEAR, 2, BAND // 2, D0).transpose(2, 0, 1, 3)
    out["rv_far"] = np.tile(a["L0_xattn_rv_table"][0], H0)[None, :]
    out["iota"] = np.arange(P, dtype=np.float32)[None, :]
    out["lane"] = np.stack([np.arange(P), DUMP + np.arange(P)], 1).astype(np.float32)
    out["before"] = np.triu(np.ones((P, P), np.float32), 1)
    out["L0_router"] = a["L0_ffn_router_weight"].T
    out["L0_ffn_router_bias"] = a["L0_ffn_router_bias"][None, :]
    out["L1_router"] = a["L1_ffn_Wg"]
    for n in ("L0_ffn_gate_up_proj", "L0_ffn_down_proj", "L1_ffn_W1", "L1_ffn_W2"):
        out[n] = a[n]
    for n in ("L0_ffn_gate_up_bias", "L0_ffn_down_bias", "L1_ffn_b1", "L1_ffn_b2"):
        out[n] = a[n].reshape(1, -1)
    for n in ("ln_x_g", "ln_x_b", "ln_l_g", "ln_l_b"):
        out[f"L1_xattn_{n}"] = a[f"L1_xattn_{n}"].reshape(EC, P).T
    for n in ("qn_g", "kn_g"):
        out[f"L1_xattn_{n}"] = np.tile(a[f"L1_xattn_{n}"], 2)[:, None]
    out["mask"] = a["mask_BxS2_bf1"].reshape(1, -1).view(np.uint8)
    out["ctx"] = a["ctx_1024"]
    for n in ("Wq", "Wkv", "Wout"):
        out[f"L1_xattn_{n}"] = a[f"L1_xattn_{n}"]
    out["L1_xattn_bout"] = a["L1_xattn_bout"][None, :]
    return {n: np.ascontiguousarray(v) for n, v in out.items()}


def program(nc, I, out):
    with ExitStack() as ctx:
        xres = ctx.enter_context(nc.sbuf_tensor("xres", [P, TILES, E], F32))
        ident = ctx.enter_context(nc.sbuf_tensor("ident", [P, P], F32))
        load_residual(nc, I["x"], I["ident"], xres, ident)
        for phase in PHASES:
            phase(nc, I, xres, ident)
        store_residual(nc, xres, out)


def kernel(**inputs):
    import concourse.bacc as bacc
    from concourse.bass_utils import run_bass_kernel_spmd

    nc = bacc.Bacc("TRN2", target_bir_lowering=False, num_devices=1)
    arrays = {f"in_{n}_dram": v for n, v in lay_out(inputs).items()}
    aps = {n[3:-5]: nc.dram_tensor(n, v.shape, mybir.dt.from_np(v.dtype), kind="ExternalInput").ap()
           for n, v in arrays.items()}
    out = nc.dram_tensor("out_0_dram", (BATCH, SEQ, E), F32, kind="ExternalOutput").ap()
    program(nc, aps, out)
    r = run_bass_kernel_spmd(nc, [arrays], core_ids=[0])
    return r.results[0]["out_0_dram"]
```

```python
from contextlib import ExitStack, contextmanager

import concourse.bass as bass
from concourse import mybir
import numpy as np

F32 = mybir.dt.float32
F32R = mybir.dt.float32r
BF16 = mybir.dt.bfloat16
I32 = mybir.dt.int32
U32 = mybir.dt.uint32
U8 = mybir.dt.uint8
ALU = mybir.AluOpType
ACT = mybir.ActivationFunctionType
AX = mybir.AxisListType

P = 128
BATCH, SEQ, E = 2, 1024, 256
CTX = 77
TOKENS = BATCH * SEQ
TILES = TOKENS // P
EC = E // P
LN_EPS = 1e-5

H0 = 16
D0 = E // H0
REACH = 128
GROUP = P // D0
GATHERS = 4
TURN = 4
HEAD_GROUPS = H0 // GROUP
BAND = CTX + P - 1
V0 = D0 + 1
NEAR = 2
BANK = 512

NE = 8
TOPK = 2
SLOT_COLS = TOPK * TILES
BLOCKS = TOPK * TOKENS // P + NE
DUMP = TOPK * TOKENS

H1, D1 = 16, 64
KEYS = SEQ + CTX
KT_TILES = SEQ // P + 1
PAIRS = H1 // 2
CAPACITY = 2 * TOPK * TOKENS // NE


@contextmanager
def phase(nc):
    with nc.cleanup_on_exit(), ExitStack() as ctx:
        yield ctx


class Steps:

    def __init__(self, engine, sem):
        self.engine, self.sem, self.n = engine, sem, 0

    def mark(self, ins):
        self.n += 1
        return ins.then_inc(self.sem, 1)

    def after(self, ins):
        self.mark(ins)
        self.engine.wait_ge(self.sem, self.n)


def layer_norm(nc, name, src, dst, ident, dstT=None, gain=None, shift=None, store=None):
    with phase(nc) as ctx:
        sb = lambda n, s, d=F32: ctx.enter_context(nc.sbuf_tensor(f"{name}_{n}", s, d))
        sem = lambda n: nc.alloc_semaphore(f"{name}_{n}")
        stats = sb("stats", [P, TILES, 6])
        moments = sb("moments", [P, TILES, 2])
        variance = sb("variance", [P, TILES])
        exponent = sb("exponent", [P, TILES])
        rstd = sb("rstd", [P, TILES])
        turned = [ctx.enter_context(nc.psum_tensor(f"{name}_turned{i}", [P, EC, P], F32)) for i in range(4)]
        stats_done, moments_done, variance_done = sem("stats_done"), sem("moments_done"), sem("variance_done")
        exponent_set, rstd_done, dst_done = sem("exponent_set"), sem("rstd_done"), sem("dst_done")
        turned_done, copied = sem("turned_done"), sem("copied")
        block = ctx.enter_context(nc.Block())

        @block.vector
        def _(dve):
            for t in range(TILES):
                nc.vector.bn_stats(stats[:, t, :], src[:, t, :]).then_inc(stats_done, 1)
            for t in range(TILES):
                dve.wait_ge(stats_done, t + 1)
                nc.vector.bn_aggr(moments[:, t, :], stats[:, t, :]).then_inc(moments_done, 1)
            dve.wait_ge(moments_done, TILES)
            nc.vector.tensor_scalar(variance[:, :], moments[:, :, 1], LN_EPS, None, ALU.add).then_inc(variance_done, 1)
            dve.wait_ge(rstd_done, 1)
            for t in range(TILES):
                nc.vector.tensor_scalar(dst[:, t, :], src[:, t, :], moments[:, t, 0:1], rstd[:, t:t + 1],
                                        ALU.subtract, ALU.mult).then_inc(dst_done, 1)

        @block.gpsimd
        def _(pool):
            nc.gpsimd.memset(exponent[:, :], -0.5).then_inc(exponent_set, 1)
            pool.wait_ge(exponent_set, 1)
            pool.wait_ge(variance_done, 1)
            nc.gpsimd.tensor_tensor(rstd[:, :], variance[:, :], exponent[:, :], ALU.pow).then_inc(rstd_done, 1)

        @block.tensor
        def _(pe):
            for t in range(TILES if dstT is not None else 0):
                pe.wait_ge(dst_done, t + 1)
                if t >= 4:
                    pe.wait_ge(copied, t - 3)
                for c in range(EC):
                    ins = nc.tensor.transpose(turned[t % 4][:, c, :], dst[:, t, c * P:(c + 1) * P], ident[:, :])
                ins.then_inc(turned_done, 1)

        @block.scalar
        def _(act):
            for t in range(TILES if dstT is not None else 0):
                act.wait_ge(turned_done, t + 1)
                cols = slice(t * P, (t + 1) * P)
                if gain is None:
                    nc.scalar.activation(dstT[:, :, cols], turned[t % 4][:, :, :], ACT.Copy).then_inc(copied, 1)
                else:
                    for c in range(EC):
                        ins = nc.scalar.activation(dstT[:, c, cols], turned[t % 4][:, c, :], ACT.Identity,
                                                   bias=shift[:, c:c + 1], scale=gain[:, c:c + 1])
                    ins.then_inc(copied, 1)

        @block.sync
        def _(sp):
            if store is not None:
                rows, stored = store
                for t in range(TILES):
                    sp.wait_ge(dst_done, t + 1)
                    sp.dma_start(rows[t * P:(t + 1) * P, :], dst[:, t, :]).then_inc(stored, 16)


def load_residual(nc, x, ident_in, xres, ident):
    with phase(nc) as ctx:
        x_loaded = nc.alloc_semaphore("x_loaded")
        block = ctx.enter_context(nc.Block())

        @block.sync
        def _(sp):
            sp.dma_start(xres[:, :, :], x.rearrange("b (t p) e -> p (b t) e", p=P)).then_inc(x_loaded, 16)
            sp.dma_start(ident[:, :], ident_in).then_inc(x_loaded, 16)
            sp.wait_ge(x_loaded, 32)


def store_residual(nc, xres, out):
    with phase(nc) as ctx:
        out_stored = nc.alloc_semaphore("out_stored")
        block = ctx.enter_context(nc.Block())

        @block.sync
        def _(sp):
            sp.dma_start(out.rearrange("b (t p) e -> p (b t) e", p=P), xres[:, :, :]).then_inc(out_stored, 16)
            sp.wait_ge(out_stored, 16)


def layer0_attention(nc, I, xres, ident):
    with phase(nc) as ctx:
        sb = lambda n, s, d=F32: ctx.enter_context(nc.sbuf_tensor(f"a0_{n}", s, d))
        sem = lambda n: nc.alloc_semaphore(f"a0_{n}")
        XW = BAND + 1
        near_tiles = [b * (SEQ // P) + i for b in range(BATCH) for i in range(NEAR)]
        far_tiles = [t for t in range(TILES) if t not in near_tiles]
        NN = len(near_tiles)

        QT = sb("QT", [P, EC, TOKENS])
        dist_d = nc.dram_tensor("a0_dist_dram", [NN, P, BAND, H0], F32)
        prob_d = nc.dram_tensor("a0_prob_dram", [NN, P, BAND, H0], F32)
        Wo = sb("Wo", [P, EC, E])
        bo = sb("bo", [P, E])
        kblock = sb("kblock", [P, 2, BATCH, HEAD_GROUPS, GROUP, CTX])
        rblock = sb("rblock", [P, NEAR, GROUP, BAND])
        vones = sb("vones", [CTX, 2, BATCH, H0, V0])
        rv = sb("rv", [BAND // 2, NEAR, 2, V0])

        with ExitStack() as c2:
            sb2 = lambda n, s, d=F32: c2.enter_context(nc.sbuf_tensor(f"a0p_{n}", s, d))
            sem2 = lambda n: nc.alloc_semaphore(f"a0p_{n}")
            xn = sb2("xn", [P, TILES, E])
            xnT = sb2("xnT", [P, EC, TOKENS])
            layer_norm(nc, "a0ln", xres, xn, ident, xnT)
            W = {n: sb2(n, [P, EC, E]) for n in ("Wq", "Wk", "Wv")}
            ctxT = sb2("ctxT", [P, EC, BATCH * CTX])
            bq, bqs, bk = sb2("bq", [P, EC]), sb2("bqs", [P, EC]), sb2("bk", [P, EC])
            bv, rv0 = sb2("bv", [CTX, E]), sb2("rv0", [CTX, E])
            mask = sb2("mask", [P, GROUP])
            relk = sb2("relk", [P, NEAR, BAND])
            kT = sb2("kT", [P, 2, EC, BATCH * CTX])
            vnear = sb2("vnear", [CTX, BATCH, E])
            zeros = sb2("zeros", [P, BAND * H0])
            pq = [c2.enter_context(nc.psum_tensor(f"a0_pq{i}", [P, BANK], F32)) for i in range(4)]
            pk = c2.enter_context(nc.psum_tensor("a0_pk", [P, EC, BATCH * CTX], F32))
            pv = c2.enter_context(nc.psum_tensor("a0_pv", [CTX, BATCH, E], F32))
            loaded, zeroed, cleared = sem2("loaded"), sem2("zeroed"), sem2("cleared")
            q_done, q_out, k_done, k_out, v_done = (sem2(n) for n in ("q_done", "q_out", "k_done", "k_out", "v_done"))
            step, bias_ready, tails = sem2("step"), sem2("bias_ready"), sem2("tails")
            NLOAD = 13
            block = c2.enter_context(nc.Block())

            @block.sync
            def _(sp):
                for n, dst in (("Wq", W["Wq"]), ("Wk", W["Wk"]), ("Wv", W["Wv"]), ("Wo", Wo)):
                    sp.dma_start(dst[:, :, :], I["L0_xattn_" + n + "T"].rearrange("(c p) n -> p c n", p=P)).then_inc(loaded, 16)
                sp.dma_start(ctxT[:, :, :], I["ctxT"].rearrange("(c p) n -> p c n", p=P)).then_inc(loaded, 16)
                sp.dma_start(bq[:, :], I["L0_xattn_bq"]).then_inc(loaded, 16)
                sp.dma_start(bk[:, :], I["L0_xattn_bk"]).then_inc(loaded, 16)
                sp.dma_start(bv[:, :], I["L0_xattn_bv"].to_broadcast([CTX, E])).then_inc(loaded, 16)
                sp.dma_start(rv0[:, :], I["rv_far"].to_broadcast([CTX, E])).then_inc(loaded, 16)
                sp.dma_start(bo[:, :], I["L0_xattn_bo"].to_broadcast([P, E])).then_inc(loaded, 16)
                sp.dma_start(mask[:, :], I["head_mask"]).then_inc(loaded, 16)
                sp.dma_start(relk[:, :, :], I["rel_k"]).then_inc(loaded, 16)
                sp.wait_ge(tails, 1)
                sp.dma_start(rv[:, :, :, 0:D0], I["rel_v"]).then_inc(loaded, 16)
                sp.wait_ge(zeroed, 1)
                for n in range(NN):
                    sp.dma_start(prob_d[n].rearrange("p j h -> p (j h)"), zeros[:, :]).then_inc(cleared, 16)
                sp.wait_ge(cleared, 16 * NN)
                sp.wait_ge(loaded, 16 * NLOAD)

            @block.gpsimd
            def _(pool):
                nc.gpsimd.memset(zeros[:, :], 0.0).then_inc(zeroed, 1)

            @block.tensor
            def _(pe):
                pe.wait_ge(loaded, 16 * NLOAD)
                for g in range(EC):
                    for c in range(EC):
                        ins = nc.tensor.matmul(pk[:, g, :], W["Wk"][:, c, g * P:(g + 1) * P], ctxT[:, c, :],
                                               start=c == 0, stop=c == EC - 1)
                ins.then_inc(k_done, 1)
                for b in range(BATCH):
                    for c in range(EC):
                        ins = nc.tensor.matmul(pv[:, b, :], ctxT[:, c, b * CTX:(b + 1) * CTX], W["Wv"][:, c, :],
                                               start=c == 0, stop=c == EC - 1)
                ins.then_inc(v_done, 1)
                for g in range(EC):
                    for n in range(TOKENS // BANK):
                        i = g * (TOKENS // BANK) + n
                        if i >= 4:
                            pe.wait_ge(q_out, i - 3)
                        for c in range(EC):
                            ins = nc.tensor.matmul(pq[i % 4][:, :], W["Wq"][:, c, g * P:(g + 1) * P],
                                                   xnT[:, c, n * BANK:(n + 1) * BANK], start=c == 0, stop=c == EC - 1)
                        ins.then_inc(q_done, 1)

            @block.scalar
            def _(act):
                act.wait_ge(bias_ready, 1)
                act.wait_ge(k_done, 1)
                for g in range(EC):
                    ins = nc.scalar.activation(kT[:, 0, g, :], pk[:, g, :], ACT.Identity, bias=bk[:, g:g + 1])
                ins.then_inc(k_out, 1)
                for g in range(EC):
                    for n in range(TOKENS // BANK):
                        i = g * (TOKENS // BANK) + n
                        act.wait_ge(q_done, i + 1)
                        nc.scalar.activation(QT[:, g, n * BANK:(n + 1) * BANK], pq[i % 4][:, :], ACT.Identity,
                                             bias=bqs[:, g:g + 1], scale=D0 ** -0.5).then_inc(q_out, 1)

            @block.vector
            def _(dve):
                s = Steps(dve, step)
                s.mark(nc.vector.memset(vones[:, :, :, :, D0:V0], 1.0))
                nc.vector.memset(rv[:, :, :, D0:V0], 0.0).then_inc(tails, 1)
                dve.wait_ge(loaded, 16 * NLOAD)
                nc.vector.tensor_scalar(bqs[:, :], bq[:, :], D0 ** -0.5, None, ALU.mult).then_inc(bias_ready, 1)
                for i in range(NEAR):
                    s.mark(nc.vector.tensor_tensor(
                        rblock[:, i, :, :], relk[:, i, :].unsqueeze(1).to_broadcast([P, GROUP, BAND]),
                        mask[:, :].unsqueeze(2).to_broadcast([P, GROUP, BAND]), ALU.mult))
                dve.wait_ge(v_done, 1)
                for b in range(BATCH):
                    s.mark(nc.vector.tensor_tensor(vnear[:, b, :], pv[:, b, :], bv[:, :], ALU.add))
                dve.wait_ge(step, s.n)
                for b in range(BATCH):
                    v = vnear[:, b, :].rearrange("p (h d) -> p h d", h=H0)
                    s.mark(nc.vector.tensor_copy(vones[:, 0, b, :, 0:D0], v))
                    s.mark(nc.vector.tensor_tensor(vones[:, 1, b, :, 0:D0], v,
                                                   rv0[:, :].rearrange("p (h d) -> p h d", h=H0), ALU.add))
                dve.wait_ge(k_out, 1)
                for g in range(EC):
                    s.mark(nc.vector.tensor_scalar(kT[:, 1, g, :], kT[:, 0, g, :], relk[:, 1, 0:1], None, ALU.add))
                dve.wait_ge(step, s.n)
                for far in range(2):
                    for b in range(BATCH):
                        for g in range(HEAD_GROUPS):
                            nc.vector.tensor_tensor(
                                kblock[:, far, b, g, :, :],
                                kT[:, far, g, b * CTX:(b + 1) * CTX].unsqueeze(1).to_broadcast([P, GROUP, CTX]),
                                mask[:, :].unsqueeze(2).to_broadcast([P, GROUP, CTX]), ALU.mult)

        GB = GROUP // 2
        SB = H0 // GB
        value_order = far_tiles + near_tiles
        soft_order = list(far_tiles)
        for n, t in enumerate(near_tiles):
            soft_order.insert(4 + 3 * n, t)
        dist = sb("dist", [P, 2, BAND, H0])
        near_scores = sb("near_scores", [P, NN, CTX, H0])
        shifted = sb("shifted", [P, H0, CTX])
        biased = sb("biased", [P, H0, CTX])
        peak = sb("peak", [P, 2, H0])
        prob = sb("prob", [P, 3, CTX, H0])
        near_prob = sb("near_prob", [P, NN, CTX, H0])
        band_prob = sb("band_prob", [P, 2, BAND, H0])
        probT = sb("probT", [P, 2, TURN, P])
        rsum = sb("rsum", [P, H0])
        O = sb("O", [P, H0, D0])
        OT = sb("OT", [P, EC, P])
        yb = sb("yb", [P, E])
        ps = ctx.enter_context(nc.psum_tensor("a0_ps", [P, SB, BANK], F32))
        pt = [ctx.enter_context(nc.psum_tensor(f"a0_pt{i}", [P, TURN, P], F32)) for i in range(2)]
        po = ctx.enter_context(nc.psum_tensor("a0_po", [P, H0, V0], F32))
        py = ctx.enter_context(nc.psum_tensor("a0_py", [P, BANK], F32))
        d_done, d_out = sem("d_done"), sem("d_out")
        d_stored = [sem(f"d_stored{i}") for i in range(2)]
        d_back = [sem(f"d_back{n}") for n in range(NN)]
        p_back = [sem(f"p_back{n}") for n in range(NN)]
        s_done, s_shift, p_done = (sem(n) for n in ("s_done", "s_shift", "p_done"))
        p_stored, t_done, t_out, pt_used = (sem(n) for n in ("p_stored", "t_done", "t_out", "pt_used"))
        o_out, ot_done, ot_out, y_done, y_out = (sem(n) for n in ("o_out", "ot_done", "ot_out", "y_done", "y_out"))
        step = sem("step")
        DHEADS = 2
        DGROUPS = H0 // DHEADS

        def rounds(t):
            blocks = [(h, None) for h in range(H0)]
            if t in near_tiles:
                blocks += [(h, c) for h in range(H0) for c in range(2)]
            return [blocks[i:i + TURN] for i in range(0, len(blocks), TURN)]

        ROUNDS = [(i, r, blocks) for i, t in enumerate(value_order) for r, blocks in enumerate(rounds(t))]
        until = [min(TILES, soft_order.index(t) + 2) if t in far_tiles else TILES for t in value_order[1:]] + [TILES]
        ahead = [list(range(until[i - 1] if i else 1, until[i])) for i in range(TILES)]
        assert max(map(len, ahead)) == 2
        prob_slot = {t: i % 3 for i, t in enumerate(far_tiles)}
        round_ends = {value_order[i]: n + 1 for n, (i, r, _) in enumerate(ROUNDS)}

        def prob_of(t):
            return near_prob[:, near_tiles.index(t)] if t in near_tiles else prob[:, prob_slot[t]]

        block = ctx.enter_context(nc.Block())

        @block.sync
        def _(sp):
            for n in range(NN):
                sp.wait_ge(d_out, DGROUPS * (n + 1))
                sp.dma_start(dist_d[n].rearrange("p j h -> p (j h)"),
                             dist[:, n % 2, :, :].rearrange("p j h -> p (j h)")).then_inc(d_stored[n % 2], 16)
                sp.wait_ge(d_stored[n % 2], 16 * (n // 2 + 1))
                sheared = bass.AP(dist_d, n * P * BAND * H0 + (P - 1) * H0, [[(BAND - 1) * H0, P], [1, CTX * H0]])
                sp.dma_start(near_scores[:, n].rearrange("p j h -> p (j h)"), sheared).then_inc(d_back[n], 16)
            for n, t in enumerate(near_tiles):
                sp.wait_ge(p_done, soft_order.index(t) + 1)
                sheared = bass.AP(prob_d, n * P * BAND * H0 + (P - 1) * H0, [[(BAND - 1) * H0, P], [1, CTX * H0]])
                sp.dma_start(sheared, near_prob[:, n].rearrange("p j h -> p (j h)")).then_inc(p_stored, 16)
            for n, t in enumerate(near_tiles):
                sp.wait_ge(p_stored, 16 * NN)
                if n >= 2:
                    sp.wait_ge(t_done, round_ends[near_tiles[n - 2]])
                sp.dma_start(band_prob[:, n % 2].rearrange("p j h -> p (j h)"),
                             prob_d[n].rearrange("p j h -> p (j h)")).then_inc(p_back[n], 16)

        @block.tensor
        def _(pe):
            for n, t in enumerate(near_tiles):
                for i in range(DGROUPS):
                    k = n * DGROUPS + i
                    if k >= SB:
                        pe.wait_ge(d_out, k - SB + 1)
                    g, h = divmod(i * DHEADS, GROUP)
                    nc.tensor.matmul(ps[:, k % SB, 0:DHEADS * BAND], QT[:, g, t * P:(t + 1) * P],
                                     rblock[:, n % NEAR, h:h + DHEADS, :],
                                     start=True, stop=True).then_inc(d_done, 1)
            pe.wait_ge(d_out, NN * DGROUPS)

            def scores(i):
                t = soft_order[i]
                far, b = int(t not in near_tiles), t // (SEQ // P)
                if i:
                    pe.wait_ge(s_shift, i)
                for j in range(SB):
                    g, h = divmod(j * GB, GROUP)
                    ins = nc.tensor.matmul(ps[:, j, 0:GB * CTX], QT[:, g, t * P:(t + 1) * P],
                                           kblock[:, far, b, g, h:h + GB, :], start=True, stop=True)
                ins.then_inc(s_done, 1)

            def turn(n):
                i, r, blocks = ROUNDS[n]
                t = value_order[i]
                if r == 0:
                    pe.wait_ge(p_done, soft_order.index(t) + 1)
                if n >= 2:
                    pe.wait_ge(t_out, n - 1)
                if blocks[0][1] is not None and ROUNDS[n - 1][2][0][1] is None:
                    pe.wait_ge(p_back[near_tiles.index(t)], 16)
                for j, (h, c) in enumerate(blocks):
                    if c is None:
                        ins = nc.tensor.transpose(pt[n % 2][0:CTX, j, :], prob_of(t)[:, :, h], ident[:, :])
                    else:
                        rows = slice(c * (BAND // 2), (c + 1) * (BAND // 2))
                        ins = nc.tensor.transpose(pt[n % 2][0:BAND // 2, j, :],
                                                  band_prob[:, near_tiles.index(t) % 2, rows, h], ident[:, :])
                ins.then_inc(t_done, 1)

            def weigh(n):
                i, r, blocks = ROUNDS[n]
                t = value_order[i]
                far, b = int(t not in near_tiles), t // (SEQ // P)
                pe.wait_ge(t_out, n + 1)
                if r == 0 and i:
                    pe.wait_ge(o_out, i)
                for j, (h, c) in enumerate(blocks):
                    rhs = vones[:, far, b, h, :] if c is None else rv[:, near_tiles.index(t) % NEAR, c, :]
                    rows = CTX if c is None else BAND // 2
                    ins = nc.tensor.matmul(po[:, h, :], probT[0:rows, n % 2, j, :], rhs,
                                           start=r == 0 and j == 0, stop=True, skip_group_check=True)
                ins.then_inc(pt_used, 1)

            def turn_outputs(i):
                pe.wait_ge(o_out, i + 1)
                if i:
                    pe.wait_ge(y_out, i)
                for c in range(EC):
                    ins = nc.tensor.transpose(py[:, c * P:(c + 1) * P],
                                              O[:, c * GROUP:(c + 1) * GROUP, :].rearrange("p h d -> p (h d)"), ident[:, :])
                ins.then_inc(ot_done, 1)

            def project_outputs(i):
                pe.wait_ge(ot_out, i + 1)
                for c in range(EC):
                    ins = nc.tensor.matmul(py[:, E:2 * E], OT[:, c, :], Wo[:, c, :], start=c == 0, stop=c == EC - 1)
                ins.then_inc(y_done, 1)

            scores(0)
            scores(ahead[0][0])
            turn(0)
            for n, (i, r, blocks) in enumerate(ROUNDS):
                if n + 1 < len(ROUNDS):
                    turn(n + 1)
                weigh(n)
                if r == 1 and i:
                    turn_outputs(i - 1)
                if r == 1 and len(ahead[i]) == 2:
                    scores(ahead[i][1])
                if r == 2 and i:
                    project_outputs(i - 1)
                if n + 1 == round_ends[value_order[i]] and i + 1 < TILES and ahead[i + 1]:
                    scores(ahead[i + 1][0])
            turn_outputs(TILES - 1)
            project_outputs(TILES - 1)

        @block.scalar
        def _(act):
            for k in range(NN * DGROUPS):
                act.wait_ge(d_done, k + 1)
                n = k // DGROUPS
                if k % DGROUPS == 0 and n >= 2:
                    act.wait_ge(d_stored[n % 2], 16 * (n // 2))
                h = k % DGROUPS * DHEADS
                nc.scalar.activation(dist[:, n % 2, :, h:h + DHEADS].rearrange("p j h -> p h j"),
                                     ps[:, k % SB, 0:DHEADS * BAND].rearrange("p (h j) -> p h j", h=DHEADS),
                                     ACT.Copy).then_inc(d_out, 1)

            def soft(i):
                t = soft_order[i]
                act.wait_ge(s_shift, i + 1)
                if t not in near_tiles and far_tiles.index(t) >= 3:
                    act.wait_ge(t_done, round_ends[far_tiles[far_tiles.index(t) - 3]])
                nc.scalar.activation(prob_of(t).rearrange("p k h -> p h k"), shifted[:, :, :], ACT.Exp).then_inc(p_done, 1)

            soft(0)
            for n, (i, r, blocks) in enumerate(ROUNDS):
                act.wait_ge(t_done, n + 1)
                if n >= 2:
                    act.wait_ge(pt_used, n - 1)
                rows = CTX if blocks[0][1] is None else BAND // 2
                nc.scalar.activation(probT[0:rows, n % 2, :, :], pt[n % 2][0:rows, :, :], ACT.Copy).then_inc(t_out, 1)
                if r == 2:
                    if i:
                        act.wait_ge(ot_done, i)
                        if i >= 2:
                            act.wait_ge(y_done, i - 1)
                        nc.scalar.activation(OT[:, :, :], py[:, 0:E].rearrange("p (c n) -> p c n", c=EC),
                                             ACT.Copy).then_inc(ot_out, 1)
                    if ahead[i]:
                        soft(ahead[i][0])
                if r == 3 and len(ahead[i]) == 2:
                    soft(ahead[i][1])
            act.wait_ge(ot_done, TILES)
            nc.scalar.activation(OT[:, :, :], py[:, 0:E].rearrange("p (c n) -> p c n", c=EC), ACT.Copy).then_inc(ot_out, 1)

        @block.vector
        def _(dve):
            s = Steps(dve, step)

            def shift(i):
                t = soft_order[i]
                dve.wait_ge(s_done, i + 1)
                src = ps[:, :, 0:GB * CTX].rearrange("p b (h k) -> p b h k", h=GB)
                if t in near_tiles:
                    dve.wait_ge(d_back[near_tiles.index(t)], 16)
                    for j in range(SB):
                        ins = nc.vector.tensor_tensor(
                            biased[:, j * GB:(j + 1) * GB, :], src[:, j],
                            near_scores[:, near_tiles.index(t), :, j * GB:(j + 1) * GB].rearrange("p k h -> p h k"), ALU.add)
                    s.after(ins)
                    src = biased[:, :, :].rearrange("p (b h) k -> p b h k", b=SB)
                s.after(nc.vector.tensor_reduce(peak[:, i % 2, :].rearrange("p (b h) -> p b h", b=SB), src, AX.X, ALU.max))
                if i:
                    dve.wait_ge(p_done, i)
                nc.vector.tensor_tensor(
                    shifted[:, :, :].rearrange("p (b h) k -> p b h k", b=SB), src,
                    peak[:, i % 2, :].rearrange("p (b h) -> p b h", b=SB).unsqueeze(3).to_broadcast([P, SB, GB, CTX]),
                    ALU.subtract).then_inc(s_shift, 1)

            def normalise(i):
                dve.wait_ge(pt_used, round_ends[value_order[i]])
                if i:
                    dve.wait_ge(ot_done, i)
                s.after(nc.vector.reciprocal(rsum[:, :], po[:, :, D0]))
                nc.vector.tensor_tensor(O[:, :, :], po[:, :, 0:D0],
                                        rsum[:, :].unsqueeze(2).to_broadcast([P, H0, D0]), ALU.mult).then_inc(o_out, 1)

            def add_outputs(i):
                t = value_order[i]
                dve.wait_ge(y_done, i + 1)
                nc.vector.tensor_tensor(yb[:, :], py[:, E:2 * E], bo[:, :], ALU.add).then_inc(y_out, 1)
                dve.wait_ge(y_out, i + 1)
                s.after(nc.vector.tensor_tensor(xres[:, t, :], xres[:, t, :], yb[:, :], ALU.add))

            shift(0)
            for i in range(TILES):
                if ahead[i]:
                    shift(ahead[i][0])
                if len(ahead[i]) == 2:
                    shift(ahead[i][1])
                if i:
                    add_outputs(i - 1)
                normalise(i)
            add_outputs(TILES - 1)


def route(nc, name, layer, xnT, lists, constants, constants_loaded, refill):
    with phase(nc) as ctx:
        sb = lambda n, s, d=F32: ctx.enter_context(nc.sbuf_tensor(f"{name}_{n}", s, d))
        sem = lambda n: nc.alloc_semaphore(f"{name}_{n}")
        Wr, br, iota, lane, before = constants
        ones = sb("ones", [P, P])
        logits = sb("logits", [P, TILES, NE])
        top = sb("top", [P, TILES, 8])
        topi = sb("topi", [P, TILES, 8], U32)
        pick = sb("pick", [P, TOPK, TILES])
        less = sb("less", [P, TILES, NE])
        ex = sb("ex", [P, TILES, NE])
        gap = sb("gap", [P, TILES])
        second = sb("second", [P, TILES])
        total = sb("total", [P, TILES])
        first = sb("first", [P, TILES])
        M = sb("M", [P, SLOT_COLS, NE])
        scan = [sb(f"scan{i}", [P, SLOT_COLS + 1, NE]) for i in range(2)]
        rank = sb("rank", [P, SLOT_COLS, NE])
        work = sb("work", [P, SLOT_COLS, NE])
        need = sb("need", [P, NE], I32)
        needb = sb("needb", [P, NE], I32)
        base = [sb(f"base{i}", [P, NE + 1]) for i in range(2)]
        pos = sb("pos", [P, SLOT_COLS])
        posi = sb("posi", [P, SLOT_COLS], I32)
        part = sb("part", [P, 2, SLOT_COLS], I32)
        partf = sb("partf", [P, 2, SLOT_COLS])
        row1h = lists["row1h"]
        blk1h = sb("blk1h", [P, SLOT_COLS, 3, BLOCKS], BF16)
        code = sb("code", [P, BLOCKS])
        free = sb("free", [P, BLOCKS])
        wrap = sb("wrap", [P, BLOCKS])
        cmp = sb("cmp", [P, BLOCKS, NE])
        own = sb("own", [P, BLOCKS])
        low = sb("low", [P, BLOCKS])
        unused = sb("unused", [P, BLOCKS])
        rk = sb("rk", [P, SLOT_COLS])
        keep = sb("keep", [P, SLOT_COLS])
        pl = ctx.enter_context(nc.psum_tensor(f"{name}_pl", [P, TILES, NE], F32))
        pp = ctx.enter_context(nc.psum_tensor(f"{name}_pp", [P, 2, SLOT_COLS * NE], F32))
        pinv = ctx.enter_context(nc.psum_tensor(f"{name}_pinv", [P, 3, BLOCKS], F32))
        step, shifted, exps = sem("step"), sem("shifted"), sem("exps")
        logits_done, masks_done, counts_done, hot_done, inverse_done = (
            sem(n) for n in ("logits_done", "masks_done", "counts_done", "hot_done", "inverse_done"))
        block = ctx.enter_context(nc.Block())

        @block.sync
        def _(sp):
            refill(sp, logits_done, inverse_done)

        @block.tensor
        def _(pe):
            pe.wait_ge(*constants_loaded)
            for t in range(TILES):
                for c in range(EC):
                    ins = nc.tensor.matmul(pl[:, t, :], xnT[:, c, t * P:(t + 1) * P], Wr[:, c, :],
                                           start=c == 0, stop=c == EC - 1)
            ins.then_inc(logits_done, 1)
            pe.wait_ge(masks_done, 1)
            m = M[:, :, :].rearrange("p s e -> p (s e)")
            nc.tensor.matmul(pp[:, 0, :], before[:, :], m, start=True, stop=True)
            nc.tensor.matmul(pp[:, 1, :], ones[:, :], m, start=True, stop=True).then_inc(counts_done, 1)
            pe.wait_ge(hot_done, 1)
            for s in range(SLOT_COLS):
                ins = nc.tensor.matmul(pinv[:, :, :], row1h[:, s, :], blk1h[:, s, :, :],
                                       start=s == 0, stop=s == SLOT_COLS - 1)
            ins.then_inc(inverse_done, 1)

        @block.scalar
        def _(act):
            act.wait_ge(shifted, 2)
            nc.scalar.activation(ex[:, :, :], less[:, :, :], ACT.Exp).then_inc(exps, 1)
            nc.scalar.activation(second[:, :], gap[:, :], ACT.Exp).then_inc(exps, 1)

        @block.vector
        def _(dve):
            s = Steps(dve, step)
            v = nc.vector
            s.mark(v.memset(ones[:, :], 1.0))
            for i in range(2):
                s.mark(v.memset(scan[i][:, 0, :], 0.0))
                s.mark(v.memset(base[i][:, 0:1], 0.0))
            dve.wait_ge(*constants_loaded)
            dve.wait_ge(logits_done, 1)
            if layer == 0:
                s.after(v.tensor_tensor(logits[:, :, :], pl[:, :, :], br[:, :].unsqueeze(1).to_broadcast([P, TILES, NE]), ALU.add))
            else:
                s.after(v.tensor_copy(logits[:, :, :], pl[:, :, :]))
            for t in range(TILES):
                s.mark(v.max(top[:, t, :], logits[:, t, :]))
            dve.wait_ge(step, s.n)
            v.tensor_tensor(less[:, :, :], logits[:, :, :], top[:, :, 0:1].to_broadcast([P, TILES, NE]),
                            ALU.subtract).then_inc(shifted, 1)
            v.tensor_tensor(gap[:, :], top[:, :, 1], top[:, :, 0], ALU.subtract).then_inc(shifted, 1)
            for t in range(TILES):
                s.mark(v.max_index(topi[:, t, :], top[:, t, :], logits[:, t, :]))
            dve.wait_ge(step, s.n)
            s.after(v.tensor_copy(pick[:, :, :], topi[:, :, 0:TOPK].rearrange("p t k -> p k t")))
            v.tensor_tensor(M[:, :, :], iota[:, 0:NE].unsqueeze(1).to_broadcast([P, SLOT_COLS, NE]),
                            pick[:, :, :].rearrange("p k t -> p (k t)").unsqueeze(2).to_broadcast([P, SLOT_COLS, NE]),
                            ALU.is_equal).then_inc(masks_done, 1)
            dve.wait_ge(exps, 2)
            s.after(v.tensor_reduce(total[:, :], ex[:, :, :], AX.X, ALU.add))
            s.after(v.reciprocal(first[:, :], total[:, :]))
            if layer == 0:
                s.mark(v.tensor_copy(lists["gates"][:, 0, :], first[:, :]))
                s.mark(v.tensor_tensor(lists["gates"][:, 1, :], second[:, :], first[:, :], ALU.mult))
            else:
                s.after(v.tensor_tensor(second[:, :], second[:, :], first[:, :], ALU.mult))
                s.after(v.scalar_tensor_tensor(total[:, :], first[:, :], 1e-9, second[:, :], ALU.add, ALU.add))
                s.after(v.reciprocal(total[:, :], total[:, :]))
                s.mark(v.tensor_tensor(lists["gates"][:, 0, :], first[:, :], total[:, :], ALU.mult))
                s.mark(v.tensor_tensor(lists["gates"][:, 1, :], second[:, :], total[:, :], ALU.mult))
            dve.wait_ge(counts_done, 1)
            s.after(v.tensor_copy(scan[0][:, 1:, :], pp[:, 1, :].rearrange("p (s e) -> p s e", e=NE)))
            src, k = 0, 1
            while k < SLOT_COLS:
                a, b = scan[src], scan[1 - src]
                s.mark(v.tensor_copy(b[:, 1:1 + k, :], a[:, 1:1 + k, :]))
                s.after(v.tensor_tensor(b[:, 1 + k:, :], a[:, 1 + k:, :], a[:, 1:SLOT_COLS + 1 - k, :], ALU.add))
                src, k = 1 - src, 2 * k
            counted = scan[src]
            s.mark(v.tensor_tensor(rank[:, :, :], pp[:, 0, :].rearrange("p (s e) -> p s e", e=NE),
                                   counted[:, 0:SLOT_COLS, :], ALU.add))
            s.after(v.tensor_scalar(need[:, :], counted[:, SLOT_COLS, :], float(P - 1), None, ALU.add))
            s.after(v.tensor_scalar(needb[:, :], need[:, :], 7, None, ALU.arith_shift_right))
            s.after(v.tensor_copy(base[0][:, 1:], needb[:, :]))
            src, k = 0, 1
            while k < NE:
                a, b = base[src], base[1 - src]
                s.mark(v.tensor_copy(b[:, 1:1 + k], a[:, 1:1 + k]))
                s.after(v.tensor_tensor(b[:, 1 + k:], a[:, 1 + k:], a[:, 1:NE + 1 - k], ALU.add))
                src, k = 1 - src, 2 * k
            start = base[src][:, 0:NE]
            if layer == 1:
                s.after(v.tensor_tensor(work[:, :, :], rank[:, :, :], M[:, :, :], ALU.mult))
                s.after(v.tensor_reduce(rk[:, :], work[:, :, :], AX.X, ALU.add))
                s.after(v.tensor_scalar(keep[:, :], rk[:, :], float(CAPACITY), None, ALU.is_lt))
                g = lists["gates"][:, :, :].rearrange("p k t -> p (k t)")
                s.after(v.tensor_tensor(g, g, keep[:, :], ALU.mult))
            s.after(v.scalar_tensor_tensor(rank[:, :, :], start.unsqueeze(1).to_broadcast([P, SLOT_COLS, NE]), float(P),
                                           rank[:, :, :], ALU.mult, ALU.add))
            s.after(v.tensor_tensor(work[:, :, :], rank[:, :, :], M[:, :, :], ALU.mult))
            s.after(v.tensor_reduce(pos[:, :], work[:, :, :], AX.X, ALU.add))
            s.after(v.tensor_copy(posi[:, :], pos[:, :]))
            s.mark(v.tensor_scalar(part[:, 0, :], posi[:, :], P - 1, None, ALU.bitwise_and))
            s.after(v.tensor_scalar(part[:, 1, :], posi[:, :], 7, None, ALU.arith_shift_right))
            s.after(v.tensor_copy(partf[:, :, :], part[:, :, :]))
            s.mark(v.tensor_tensor(row1h[:, :, :], iota[:, :].unsqueeze(1).to_broadcast([P, SLOT_COLS, P]),
                                   partf[:, 0, :].unsqueeze(2).to_broadcast([P, SLOT_COLS, P]), ALU.is_equal))
            s.after(v.tensor_tensor(blk1h[:, :, 2, :], iota[:, 0:BLOCKS].unsqueeze(1).to_broadcast([P, SLOT_COLS, BLOCKS]),
                                    partf[:, 1, :].unsqueeze(2).to_broadcast([P, SLOT_COLS, BLOCKS]), ALU.is_equal))
            s.mark(v.tensor_scalar(blk1h[:, :, 1, :], blk1h[:, :, 2, :], lane[:, 0:1], None, ALU.mult))
            s.after(v.tensor_tensor(blk1h[:, :, 0, :], blk1h[:, :, 2, :],
                                    iota[:, 0:SLOT_COLS].unsqueeze(2).to_broadcast([P, SLOT_COLS, BLOCKS]), ALU.mult))
            s.engine.sem_inc(hot_done, 1)
            s.after(v.tensor_tensor(cmp[:, :, :], iota[:, 0:BLOCKS].unsqueeze(2).to_broadcast([P, BLOCKS, NE]),
                                    start.unsqueeze(1).to_broadcast([P, BLOCKS, NE]), ALU.is_ge))
            s.after(v.tensor_reduce(own[:, :], cmp[:, :, :], AX.X, ALU.add))
            s.mark(v.tensor_scalar(lists["expert"][:, :], own[:, :], -1.0, None, ALU.add))
            dve.wait_ge(inverse_done, 1)
            s.mark(v.tensor_scalar(unused[:, :], iota[:, 0:BLOCKS], float(P), lane[:, 1:2], ALU.mult, ALU.add))
            s.mark(v.tensor_scalar(free[:, :], pinv[:, 2, :], -1.0, 1.0, ALU.mult, ALU.add))
            s.after(v.tensor_copy(low[:, :], pinv[:, 1, :]))
            s.after(v.scalar_tensor_tensor(code[:, :], pinv[:, 0, :], float(P), low[:, :], ALU.mult, ALU.add))
            s.after(v.tensor_tensor(free[:, :], free[:, :], unused[:, :], ALU.mult))
            s.mark(v.tensor_tensor(lists["scatter"][:, :], free[:, :], code[:, :], ALU.add))
            s.after(v.tensor_scalar(wrap[:, :], code[:, :], float(TOKENS), -float(TOKENS), ALU.is_ge, ALU.mult))
            s.after(v.tensor_tensor(lists["gather"][:, :], code[:, :], wrap[:, :], ALU.add))


def experts(nc, name, layer, ident, lists, xn_rows, y_rows, up, down, bup, bdown, weights_ready, ff):
    FC = ff // P
    UP = E * 4

    def reached(engine, sem, value):
        if not isinstance(value, int) or value > 0:
            engine.wait_ge(sem, value)

    with phase(nc) as ctx:
        sb = lambda n, s, d=F32: ctx.enter_context(nc.sbuf_tensor(f"{name}_{n}", s, d))
        sem = lambda n: nc.alloc_semaphore(f"{name}_{n}")
        ps = lambda n, s: ctx.enter_context(nc.psum_tensor(f"{name}_{n}", s, F32))
        xg = sb("xg", [P, GATHERS, E])
        xT = sb("xT", [P, EC, P])
        h = sb("h", [P, 2, UP])
        a = sb("a", [P, 2, ff]) if layer == 0 else h
        aT = sb("aT", [P, 2, FC, P])
        y = sb("y", [P, E])
        sig = sb("sig", [P, ff]) if layer == 0 else None
        pxT = ps("pxT", [P, BANK])
        ph = ps("ph", [P, 2, UP])
        paT = ps("paT", [P, max(FC, 4), P])
        py = ps("py", [P, BANK])
        gathered = [sem(f"gathered{q}") for q in range(GATHERS)]
        scattered = sem("scattered")
        xT_done, xT_out, h_done, h_out, a_done, aT_done, aT_out, y_done, y_out = (
            sem(n) for n in ("xT_done", "xT_out", "h_done", "h_out", "a_done", "aT_done", "aT_out", "y_done", "y_out"))
        step, gate_ready, sig_ready = sem("step"), sem("gate_ready"), sem("sig_ready")
        block = ctx.enter_context(nc.Block())

        def steps(engine, body):
            begin, end = 2 * GATHERS - 1, BLOCKS - 1
            assert (end - begin) % GATHERS == 0
            for s in range(begin):
                body(s, s % GATHERS)
            with engine.Fori(0, (end - begin) // GATHERS) as i:
                for k in range(GATHERS):
                    body(i * GATHERS + (begin + k), (begin + k) % GATHERS)
            for s in range(end, BLOCKS + 2):
                body(s, s % GATHERS)

        def within(b):
            return not isinstance(b, int) or 0 <= b < BLOCKS

        @block.gpsimd
        def _(pool):
            def gather(b):
                if b >= GATHERS:
                    pool.wait_ge(xT_done, b - GATHERS + 1)
                nc.gpsimd.indirect_dma_start(xg[:, b % GATHERS, :], None, xn_rows,
                                             bass.IndirectOffsetOnAxis(ap=lists["gather"][:, b:b + 1], axis=0)
                                             ).then_inc(gathered[b % GATHERS], 16)

            for b in range(GATHERS):
                gather(b)
            for b in range(BLOCKS):
                if b + GATHERS < BLOCKS:
                    gather(b + GATHERS)
                pool.wait_ge(y_out, b + 1)
                nc.gpsimd.indirect_dma_start(y_rows, bass.IndirectOffsetOnAxis(ap=lists["scatter"][:, b:b + 1], axis=0),
                                             y[:, :], None).then_inc(scattered, 16)
            pool.wait_ge(scattered, 16 * BLOCKS)

        @block.tensor
        def _(pe):
            def turn_x(b, r):
                pe.wait_ge(gathered[r], (b - r) * (16 // GATHERS) + 16)
                reached(pe, xT_out, b)
                for c in range(EC):
                    ins = nc.tensor.transpose(pxT[:, c * P:(c + 1) * P], xg[:, r, c * P:(c + 1) * P], ident[:, :])
                ins.then_inc(xT_done, 1)

            def body(s, r):
                q = r % 2
                if isinstance(s, int) and s == 0:
                    turn_x(0, 0)
                    pe.wait_ge(weights_ready[0], weights_ready[1])
                if within(s):
                    e = pe.value_load(lists["expert"][0:1, bass.ds(s, 1)], min_val=0, max_val=NE - 1)
                    pe.wait_ge(xT_out, s + 1)
                    reached(pe, h_out, s - 1)
                    for half in range(UP // BANK):
                        for c in range(EC):
                            cols = slice(half * BANK, (half + 1) * BANK)
                            ins = nc.tensor.matmul(ph[:, q, cols], xT[:, c, :],
                                                   up[:, bass.ds(e, 1), c, cols].rearrange("p a n -> p (a n)"),
                                                   start=c == 0, stop=c == EC - 1)
                    ins.then_inc(h_done, 1)
                if within(s - 1):
                    pe.wait_ge(a_done, s)
                    reached(pe, aT_out, s - 1)
                    for f in range(FC):
                        ins = nc.tensor.transpose(paT[:, f, :], a[:, 1 - q, f * P:(f + 1) * P], ident[:, :])
                    ins.then_inc(aT_done, 1)
                if within(s + 1):
                    turn_x(s + 1, (r + 1) % GATHERS)
                if within(s - 2):
                    e = pe.value_load(lists["expert"][0:1, bass.ds(s - 2, 1)], min_val=0, max_val=NE - 1)
                    pe.wait_ge(aT_out, s - 1)
                    reached(pe, y_out, s - 2)
                    for f in range(FC):
                        ins = nc.tensor.matmul(py[:, 0:E], aT[:, q, f, :],
                                               down[:, bass.ds(e, 1), f, :].rearrange("p a n -> p (a n)"),
                                               start=f == 0, stop=f == FC - 1)
                    ins.then_inc(y_done, 1)

            steps(pe, body)

        @block.scalar
        def _(act):
            def copy_x(b):
                act.wait_ge(xT_done, b + 1)
                reached(act, h_done, b)
                nc.scalar.activation(xT[:, :, :], pxT[:, 0:E].rearrange("p (c n) -> p c n", c=EC), ACT.Copy).then_inc(xT_out, 1)

            def body(s, r):
                q = r % 2
                if isinstance(s, int) and s == 0:
                    copy_x(0)
                if within(s - 1):
                    act.wait_ge(aT_done, s)
                    reached(act, y_done, s - 2)
                    nc.scalar.activation(aT[:, 1 - q, :, :], paT[:, 0:FC, :], ACT.Copy).then_inc(aT_out, 1)
                if within(s + 1):
                    copy_x(s + 1)
                if within(s):
                    if layer == 1:
                        act.wait_ge(h_out, s + 1)
                        nc.scalar.activation(a[:, q, :], h[:, q, :], ACT.Gelu).then_inc(a_done, 1)
                    else:
                        act.wait_ge(gate_ready, s + 1)
                        reached(act, a_done, s)
                        nc.scalar.activation(sig[:, :], h[:, q, 0:ff], ACT.Sigmoid, scale=1.702).then_inc(sig_ready, 1)

            steps(act, body)

        @block.vector
        def _(dve):
            v = nc.vector
            dve.wait_ge(weights_ready[0], weights_ready[1])

            def body(s, r):
                q = r % 2
                if within(s):
                    e = dve.value_load(lists["expert"][0:1, bass.ds(s, 1)], min_val=0, max_val=NE - 1)
                    dve.wait_ge(h_done, s + 1)
                    reached(dve, a_done if layer == 0 else aT_done, s - 1)
                    v.tensor_tensor(h[:, q, :], ph[:, q, :], bup[:, bass.ds(e, 1), :].rearrange("p a n -> p (a n)"),
                                    ALU.add).then_inc(h_out, 1)
                    if layer == 0:
                        dve.wait_ge(h_out, s + 1)
                        v.tensor_scalar(h[:, q, 0:ff], h[:, q, 0:ff], 7.0, None, ALU.min).then_inc(gate_ready, 1)
                        v.tensor_scalar(h[:, q, ff:], h[:, q, ff:], 7.0, -7.0, ALU.min, ALU.max).then_inc(step, 1)
                        dve.wait_ge(sig_ready, s + 1)
                        reached(dve, aT_done, s - 1)
                        v.tensor_tensor(a[:, q, :], h[:, q, 0:ff], sig[:, :], ALU.mult).then_inc(step, 1)
                        dve.wait_ge(step, s * 2 + 2)
                        v.scalar_tensor_tensor(a[:, q, :], h[:, q, ff:], 1.0, a[:, q, :], ALU.add, ALU.mult).then_inc(a_done, 1)
                if within(s - 2):
                    e = dve.value_load(lists["expert"][0:1, bass.ds(s - 2, 1)], min_val=0, max_val=NE - 1)
                    dve.wait_ge(y_done, s - 1)
                    reached(dve, scattered, (s - 2) * 16)
                    v.tensor_tensor(y[:, :], py[:, 0:E], bdown[:, bass.ds(e, 1), :].rearrange("p a n -> p (a n)"),
                                    ALU.add).then_inc(y_out, 1)

            steps(dve, body)


def combine(nc, name, gates, y_rows, xres):
    with phase(nc) as ctx:
        got = [ctx.enter_context(nc.sbuf_tensor(f"{name}_got{i}", [P, TOPK, E], F32)) for i in range(4)]
        loaded = [nc.alloc_semaphore(f"{name}_loaded{i}") for i in range(4)]
        added, half = nc.alloc_semaphore(f"{name}_added"), nc.alloc_semaphore(f"{name}_half")
        rows = y_rows[0:DUMP, :].rearrange("(k t p) e -> t p k e", k=TOPK, p=P)
        block = ctx.enter_context(nc.Block())

        @block.sync
        def _(sp):
            for t in range(TILES):
                if t >= 4:
                    sp.wait_ge(added, t - 3)
                sp.dma_start(got[t % 4][:, :, :], rows[t]).then_inc(loaded[t % 4], 16)

        @block.vector
        def _(dve):
            for t in range(TILES):
                dve.wait_ge(loaded[t % 4], 16 * (t // 4 + 1))
                nc.vector.scalar_tensor_tensor(xres[:, t, :], got[t % 4][:, 0, :], gates[:, 0, t:t + 1], xres[:, t, :],
                                               ALU.mult, ALU.add).then_inc(half, 1)
                dve.wait_ge(half, t + 1)
                nc.vector.scalar_tensor_tensor(xres[:, t, :], got[t % 4][:, 1, :], gates[:, 1, t:t + 1], xres[:, t, :],
                                               ALU.mult, ALU.add).then_inc(added, 1)


def mixture(nc, I, xres, ident, layer):
    name = f"m{layer}"
    ff = 512 if layer == 0 else 1024
    FC = ff // P
    wup, wbup, wdown, wbdown = (
        ("L0_ffn_gate_up_proj", "L0_ffn_gate_up_bias", "L0_ffn_down_proj", "L0_ffn_down_bias") if layer == 0 else
        ("L1_ffn_W1", "L1_ffn_b1", "L1_ffn_W2", "L1_ffn_b2"))
    xn_rows = nc.dram_tensor(f"{name}_xn_rows", [TOKENS, E], F32).ap()
    y_rows = nc.dram_tensor(f"{name}_y_rows", [DUMP + BLOCKS * P, E], F32).ap()
    with phase(nc) as ctx:
        gates = ctx.enter_context(nc.sbuf_tensor(f"{name}_gates", [P, TOPK, TILES], F32))
        with ExitStack() as c2:
            sb = lambda n, s, d=F32: c2.enter_context(nc.sbuf_tensor(f"{name}_{n}", s, d))
            sem = lambda n: nc.alloc_semaphore(f"{name}_{n}")
            lists = {"gates": gates, "gather": sb("gather", [P, BLOCKS], U32), "scatter": sb("scatter", [P, BLOCKS], U32),
                     "expert": sb("expert", [P, BLOCKS], I32)}
            constants_loaded, weights_loaded, rows_stored = sem("constants_loaded"), sem("weights_loaded"), sem("rows_stored")
            up = sb("up", [P, NE, EC, E * 4])
            bup, bdown = sb("bup", [P, NE, E * 4]), sb("bdown", [P, NE, E])
            down = sb("down", [P, NE, FC, E])
            c3 = c2.enter_context(ExitStack())
            sb3 = lambda n, s, d=F32: c3.enter_context(nc.sbuf_tensor(f"{name}_{n}", s, d))
            Wr, br = sb3("Wr", [P, EC, NE]), sb3("br", [P, NE])
            iota = sb3("iota", [P, P])
            lane = sb3("lane", [P, 2])
            before = sb3("before", [P, P])
            lent = TILES // FC
            xn = down[:, NE - lent:, :, :].rearrange("p e f n -> p (e f) n")
            xnT = down[:, NE - 2 * lent:NE - lent, :, :].rearrange("p e f n -> p (e f n)").rearrange("p (c t) -> p c t", c=EC)

            lists["row1h"] = bdown[:, :, :].rearrange("p e n -> p (e n)").bitcast(BF16).rearrange("p (s r) -> p s r", r=P)

            def load_down(sp, experts_):
                for e in experts_:
                    sp.dma_start(down[:, e], I[wdown][e].rearrange("(c p) n -> p c n", p=P)).then_inc(weights_loaded, 16)

            def refill(sp, logits_done, inverse_done):
                sp.wait_ge(rows_stored, 16 * TILES)
                load_down(sp, range(NE - lent, NE))
                sp.wait_ge(logits_done, 1)
                load_down(sp, range(NE - 2 * lent, NE - lent))
                sp.wait_ge(inverse_done, 1)
                sp.dma_start(bdown[:, :, :].rearrange("p e n -> p (e n)"),
                             I[wbdown].to_broadcast([P, NE * E])).then_inc(weights_loaded, 16)

            constants = [(Wr[:, :, :], I[f"L{layer}_router"].rearrange("(c p) n -> p c n", p=P)),
                         (iota[:, :], I["iota"].to_broadcast([P, P])), (lane[:, :], I["lane"]), (before[:, :], I["before"])]
            if layer == 0:
                constants.append((br[:, :], I["L0_ffn_router_bias"].to_broadcast([P, NE])))
            with nc.Block() as block:
                @block.sync
                def _(sp):
                    for dst, src in constants:
                        sp.dma_start(dst, src).then_inc(constants_loaded, 16)
                    for e in range(NE):
                        sp.dma_start(up[:, e], I[wup][e].rearrange("(c p) n -> p c n", p=P)).then_inc(weights_loaded, 16)
                    sp.dma_start(bup[:, :, :].rearrange("p e n -> p (e n)"),
                                 I[wbup].to_broadcast([P, NE * E * 4])).then_inc(weights_loaded, 16)
                    load_down(sp, range(NE - 2 * lent))
            layer_norm(nc, f"{name}ln", xres, xn, ident, xnT, store=(xn_rows, rows_stored))
            route(nc, f"{name}r", layer, xnT, lists, (Wr, br, iota, lane, before), (constants_loaded, 16 * len(constants)), refill)
            c3.close()
            experts(nc, f"{name}e", layer, ident, lists, xn_rows, y_rows, up, down, bup, bdown,
                    (weights_loaded, 16 * (2 * NE + 2)), ff)
        combine(nc, f"{name}c", gates, y_rows, xres)


class Pair:

    def __init__(self, g, b, hp, parity):
        self.g, self.b, self.hp, self.parity = g, b, hp, parity

    def next(self):
        if isinstance(self.g, int):
            return Pair(self.g + 1, *divmod(self.g + 1, PAIRS), 1 - self.parity) if self.g + 1 < BATCH * PAIRS else None
        return Pair(self.g + 1, self.b, self.hp + 1, 1 - self.parity)


UNITS = 2 * (SEQ // P)

PIECES = ["Ka", "Kb", "c", "Qa", "Qb", "Va", "K0a", "K0b", "Kc", "K1a", "K1b", "Q0a", "Q1a", "Q0b", "Q1b", "Vb"]
PROJECTED = ["Ka", "Kb", "c", "Qa", "Qb", "Va", "Vb"]
KEY_TURNS = ["K0a", "K0b", "Kc", "K1a", "K1b"]
QUERY_TURNS = ["Q0a", "Q1a", "Q0b", "Q1b"]
TURNS = KEY_TURNS + QUERY_TURNS


def count(pair, step, steps):
    return pair.g * len(steps) + (steps.index(step) + 1)


def ahead(pair, u, by):
    return (pair, u + by) if u + by < UNITS else (pair.next(), u + by - UNITS)


def all_pairs(engine, body):
    for b in range(BATCH):
        with engine.Fori(0, PAIRS // 2 - 1) as i:
            for r in range(2):
                body(Pair(i * 2 + (b * PAIRS + r), b, i * 2 + r, r))
        for hp in (PAIRS - 2, PAIRS - 1):
            body(Pair(b * PAIRS + hp, b, hp, hp % 2))


def layer1_attention(nc, I, xres, ident):
    with phase(nc) as outer:
        o_rows = nc.dram_tensor("a1_o_rows", [TOKENS, H1 * D1], F32).ap()
        attn = outer.enter_context(ExitStack())
        sb = lambda n, s, d=F32: attn.enter_context(nc.sbuf_tensor(f"a1_{n}", s, d))
        sem = lambda n: nc.alloc_semaphore(f"a1_{n}")
        latT = sb("latT", [P, EC, TOKENS])
        ctxT = sb("ctxT", [P, EC, BATCH * CTX])
        Wq = sb("Wq", [P, EC, H1 * D1])
        Wkv = sb("Wkv", [P, EC, 2 * H1 * D1])
        valid = sb("valid", [CTX, BATCH])
        gamma = sb("gamma", [P, 1])

        with ExitStack() as c2:
            sb2 = lambda n, s, d=F32: c2.enter_context(nc.sbuf_tensor(f"a1n_{n}", s, d))
            sem2 = lambda n: nc.alloc_semaphore(f"a1n_{n}")
            lat = sb2("lat", [P, TILES, E])
            lat2 = sb2("lat2", [P, TILES, E])
            lng, lnb = sb2("lng", [P, EC]), sb2("lnb", [P, EC])
            cng, cnb = sb2("cng", [P, EC]), sb2("cnb", [P, EC])
            qg, kg = sb2("qg", [P, 1]), sb2("kg", [P, 1])
            mask = sb2("mask", [P, BATCH, CTX], U8)
            maskT = sb2("maskT", [CTX, BATCH], U8)
            maskf, maskn = sb2("maskf", [P, BATCH, CTX]), sb2("maskn", [P, BATCH, CTX])
            stand_in = sb2("stand_in", [P, EC, BATCH * CTX])
            c = sb2("c", [CTX, BATCH, E])
            stats, moments = sb2("stats", [CTX, BATCH, 6]), sb2("moments", [CTX, BATCH, 2])
            var, expo, rstd = sb2("var", [CTX, BATCH]), sb2("expo", [CTX, BATCH]), sb2("rstd", [CTX, BATCH])
            cn = sb2("cn", [CTX, BATCH, E])
            pc = c2.enter_context(nc.psum_tensor("a1_pc", [P, EC, BATCH, 128], F32))
            loaded, step, expo_set, var_done, rstd_done = (sem2(n) for n in ("loaded", "step", "expo_set", "var_done", "rstd_done"))
            cn_done, pc_done, ctxT_done, gamma_done = (sem2(n) for n in ("cn_done", "pc_done", "ctxT_done", "gamma_done"))
            with nc.Block() as block:
                @block.sync
                def _(sp):
                    for dst, src in ((lng, "ln_l_g"), (lnb, "ln_l_b"), (cng, "ln_x_g"), (cnb, "ln_x_b")):
                        sp.dma_start(dst[:, :], I[f"L1_xattn_{src}"]).then_inc(loaded, 16)
                    sp.dma_start(qg[:, :], I["L1_xattn_qn_g"]).then_inc(loaded, 16)
                    sp.dma_start(kg[:, :], I["L1_xattn_kn_g"]).then_inc(loaded, 16)
                    sp.dma_start(mask[:, :, :].rearrange("p b k -> p (b k)"),
                                 I["mask"].to_broadcast([P, BATCH * CTX])).then_inc(loaded, 16)
                    sp.dma_start(maskT[:, :], I["maskT"]).then_inc(loaded, 16)
                    sp.dma_start(c[:, :, :], I["ctx"].rearrange("b k e -> k b e")).then_inc(loaded, 16)
                    sp.dma_start(Wq[:, :, :], I["L1_xattn_Wq"].rearrange("(c p) n -> p c n", p=P)).then_inc(loaded, 16)
                    sp.dma_start(Wkv[:, :, :], I["L1_xattn_Wkv"].rearrange("(c p) n -> p c n", p=P)).then_inc(loaded, 16)
                    sp.wait_ge(loaded, 176)

                @block.gpsimd
                def _(pool):
                    nc.gpsimd.memset(expo[:, :], -0.5).then_inc(expo_set, 1)
                    pool.wait_ge(expo_set, 1)
                    pool.wait_ge(var_done, 1)
                    nc.gpsimd.tensor_tensor(rstd[:, :], var[:, :], expo[:, :], ALU.pow).then_inc(rstd_done, 1)

                @block.vector
                def _(dve):
                    s = Steps(dve, step)
                    v = nc.vector
                    dve.wait_ge(loaded, 176)
                    s.mark(v.tensor_copy(maskf[:, :, :], mask[:, :, :]))
                    s.mark(v.tensor_scalar(maskn[:, :, :], mask[:, :, :], -1.0, 1.0, ALU.mult, ALU.add))
                    s.mark(v.tensor_copy(valid[:, :], maskT[:, :]))
                    s.mark(v.scalar_tensor_tensor(gamma[:, :], qg[:, :], D1 ** -0.5, kg[:, :], ALU.mult, ALU.mult))
                    for b in range(BATCH):
                        s.after(v.bn_stats(stats[:, b, :], c[:, b, :]))
                        s.after(v.bn_aggr(moments[:, b, :], stats[:, b, :]))
                    assert s.n == 2 * BATCH + 4
                    v.tensor_scalar(var[:, :], moments[:, :, 1], LN_EPS, None, ALU.add).then_inc(var_done, 1)
                    dve.wait_ge(rstd_done, 1)
                    for b in range(BATCH):
                        v.tensor_scalar(cn[:, b, :], c[:, b, :], moments[:, b, 0:1], rstd[:, b:b + 1],
                                        ALU.subtract, ALU.mult).then_inc(cn_done, 1)

                @block.tensor
                def _(pe):
                    pe.wait_ge(cn_done, BATCH)
                    for b in range(BATCH):
                        for e in range(EC):
                            ins = nc.tensor.transpose(pc[:, e, b, 0:CTX], cn[:, b, e * P:(e + 1) * P], ident[0:CTX, 0:CTX])
                    ins.then_inc(pc_done, 1)

                @block.scalar
                def _(act):
                    act.wait_ge(loaded, 176)
                    act.wait_ge(pc_done, 1)
                    for e in range(EC):
                        nc.scalar.activation(ctxT[:, e, :].rearrange("p (b k) -> p b k", b=BATCH), pc[:, e, :, 0:CTX],
                                             ACT.Identity, bias=cnb[:, e:e + 1], scale=cng[:, e:e + 1])
            layer_norm(nc, "a1lat", xres, lat, ident)
            layer_norm(nc, "a1ln", lat, lat2, ident, latT, gain=lng, shift=lnb)
            with nc.Block() as block:
                @block.vector
                def _(dve):
                    s = Steps(dve, step)
                    s.n = 2 * BATCH + 4
                    v = nc.vector
                    for e in range(EC):
                        x = ctxT[:, e, :].rearrange("p (b k) -> p b k", b=BATCH)
                        y = stand_in[:, e, :].rearrange("p (b k) -> p b k", b=BATCH)
                        first = latT[:, e, :].rearrange("p (b s) -> p b s", b=BATCH)[:, :, 0:1].to_broadcast([P, BATCH, CTX])
                        s.mark(v.tensor_tensor(x, x, maskf[:, :, :], ALU.mult))
                        s.after(v.tensor_tensor(y, first, maskn[:, :, :], ALU.mult))
                        s.after(v.tensor_tensor(x, x, y, ALU.add))

        W2 = KEYS + 1
        S = SEQ // P
        KHL = sb("KHL", [P, 2, 2, 2, W2], F32R)
        QHL = sb("QHL", [P, 2, 2, SEQ], F32R)
        V1 = sb("V1", [P, 2, KT_TILES, 2, D1 + 1])
        knat, qnat = sb("knat", [P, KT_TILES, P]), sb("qnat", [P, S, P])
        ksq, qsq = sb("ksq", [P, KT_TILES, P]), sb("qsq", [P, S, P])
        kvar, qvar = sb("kvar", [P, KT_TILES * 2]), sb("qvar", [P, S * 2])
        kinv, qinv = sb("kinv", [P, KT_TILES * 2]), sb("qinv", [P, S * 2])
        expo = sb("expo", [P, KT_TILES * 2])
        kdup = sb("kdup", [P, KT_TILES, 2, 2, D1])
        qdup = sb("qdup", [P, S, 2, 2, D1])
        qgam = sb("qgam", [P, BANK])
        npeak = sb("npeak", [P, 2])
        prob = sb("prob", [P, 2, KEYS])
        probT = sb("probT", [P, 2, KT_TILES, P])
        part_peak = sb("part_peak", [P, 2, 3])
        rsum = sb("rsum", [P, 2, 2])
        O = sb("O", [P, 2, S, P])
        slot = [attn.enter_context(nc.psum_tensor(f"a1_slot{i}", [P, 3 * BANK], F32)) for i in range(2)]
        side = attn.enter_context(nc.psum_tensor("a1_side", [P, BANK], F32))
        po = attn.enter_context(nc.psum_tensor("a1_po", [P, 2, D1 + 1], F32))
        filled, act_freed, dve_freed = sem("filled"), sem("act_freed"), sem("dve_freed")
        set_up, padded, squared, meaned, powered, scaled, summed = (
            sem(n) for n in ("set_up", "padded", "squared", "meaned", "powered", "scaled", "summed"))
        khigh, qhigh, qlow, bank_filled, part_peaked, peaked = (
            sem(n) for n in ("khigh", "qhigh", "qlow", "bank_filled", "part_peaked", "peaked"))
        exped, turned, turned_act, turned_dve, weighed, rsum_done, o_out = (
            sem(n) for n in ("exped", "turned", "turned_act", "turned_dve", "weighed", "rsum_done", "o_out"))
        o_stored = [sem(f"o_stored{i}") for i in range(2)]
        NSET = 6
        block = attn.enter_context(nc.Block())

        @block.sync
        def _(sp):
            for i in range(2):
                sp.sem_inc(o_stored[i], 16)

            def body(pair):
                sp.wait_ge(o_out, pair.g * (UNITS // 2) + (UNITS // 2 + 1))
                rows = o_rows[pair.b * SEQ:(pair.b + 1) * SEQ, :].rearrange("(t p) n -> p t n", p=P)
                hp = pair.hp
                cols = bass.ds(hp * P, P)
                sp.dma_start(rows[:, :, cols], O[:, pair.parity, :, :]).then_inc(o_stored[pair.parity], 16)

            all_pairs(sp, body)
            for i in range(2):
                sp.wait_ge(o_stored[i], 16 * BATCH * PAIRS // 2 + 16)

        @block.gpsimd
        def _(pool):
            g_ = nc.gpsimd
            g_.memset(expo[:, :], -0.5).then_inc(set_up, 1)
            g_.memset(knat[:, KT_TILES - 1, :], 0.0).then_inc(set_up, 1)
            for p in range(2):
                for h in range(2):
                    g_.memset(V1[:, p, 0:S, h, D1:D1 + 1], 1.0).then_inc(set_up, 1)
            pool.wait_ge(set_up, NSET)

            def body(pair, first):
                n = pair.g
                for nat, sq, step in ((knat, ksq, "c"), (qnat, qsq, "Qb")):
                    pool.wait_ge(act_freed, count(pair, step, PROJECTED))
                    if not first:
                        pool.wait_ge(meaned, n * 2)
                    g_.tensor_tensor(sq[:, :, :], nat[:, :, :], nat[:, :, :], ALU.mult).then_inc(squared, 1)
                for j, (nat, dup, var, inv, last) in enumerate(((knat, kdup, kvar, kinv, "K1b"), (qnat, qdup, qvar, qinv, "Q1b"))):
                    tiles = nat.shape[1]
                    pool.wait_ge(meaned, n * 2 + (j + 1))
                    g_.tensor_tensor(inv[:, :], var[:, :], expo[:, 0:2 * tiles], ALU.pow).then_inc(powered, 1)
                    pool.wait_ge(powered, n * 2 + (j + 1))
                    if not first:
                        pool.wait_ge(filled, count(Pair(pair.g - 1, 0, 0, 0), last, PIECES))
                    for h in range(2):
                        src = nat[:, :, h * D1:(h + 1) * D1]
                        scale = inv[:, :].rearrange("p (t h) -> p t h", h=2)[:, :, h:h + 1].to_broadcast([P, tiles, D1])
                        for d in range(2):
                            ins = g_.tensor_tensor(dup[:, :, h, d, :], src, scale, ALU.mult)
                    ins.then_inc(scaled, 1)

            body(Pair(0, 0, 0, 0), True)
            body(Pair(1, 0, 0, 0), False)
            with pool.Fori(2, BATCH * PAIRS) as g:
                body(Pair(g, 0, 0, 0), False)

        HALF = S // 2

        @block.tensor
        def _(pe):
            t_ = nc.tensor

            def project(out, x, W, hp):
                for c in range(EC):
                    ins = t_.matmul(out, x[:, c, :], W[:, c, bass.ds(hp, P)], start=c == 0, stop=c == EC - 1)
                return ins

            def piece(pair, step):
                k = PIECES.index(step)
                if k or not (isinstance(pair.g, int) and pair.g == 0):
                    before = PIECES[k - 1]
                    owner = pair if k else Pair(pair.g - 1, 0, 0, 0)
                    if before in PROJECTED:
                        pe.wait_ge(act_freed, count(owner, before, PROJECTED))
                    else:
                        pe.wait_ge(dve_freed, count(owner, before, TURNS))
                b, hp = pair.b, pair.hp
                ctx = ctxT[:, :, b * CTX:(b + 1) * CTX]
                lo = HALF if step.endswith("b") else 0
                if step == "c":
                    project(side[0:CTX, 0:P], ctx, Wkv, hp * P)
                    ins = project(side[0:CTX, P:2 * P], ctx, Wkv, hp * P + H1 * D1)
                elif step in PROJECTED:
                    W, off = {"K": (Wkv, 0), "V": (Wkv, H1 * D1), "Q": (Wq, 0)}[step[0]]
                    for j in range(HALF):
                        t = b * S + lo + j
                        ins = project(side[:, j * P:(j + 1) * P], latT[:, :, t * P:(t + 1) * P], W, hp * P + off)
                else:
                    pe.wait_ge(scaled, pair.g * 2 + (1 if step[0] == "K" else 2))
                    dup = kdup if step[0] == "K" else qdup
                    if step == "Kc":
                        for h in range(2):
                            ins = t_.transpose(side[:, h * CTX:(h + 1) * CTX], dup[0:CTX, S, h, :, :].rearrange("p a d -> p (a d)"),
                                               ident[0:CTX, 0:CTX])
                    else:
                        h = int(step[1])
                        for j in range(HALF):
                            ins = t_.transpose(side[:, j * P:(j + 1) * P], dup[:, lo + j, h, :, :].rearrange("p a d -> p (a d)"),
                                               ident[:, :])
                ins.then_inc(filled, 1)

            def score(pair, u):
                out = slot[u % 2]
                t, h = divmod(u, 2)
                if u == 0:
                    pe.wait_ge(dve_freed, count(pair, "K1b", TURNS))
                if u in (0, 1, 2 * HALF, 2 * HALF + 1):
                    pe.wait_ge(qlow, count(pair, QUERY_TURNS[u % 2 + (2 if u >= 2 * HALF else 0)], QUERY_TURNS))
                q = QHL[:, pair.parity, h, t * P:(t + 1) * P]
                for lo, hi in ((0, BANK), (BANK, SEQ), (SEQ, W2)):
                    for part in range(2):
                        ins = t_.matmul(out[:, lo:hi], q, KHL[:, pair.parity, h, part, lo:hi],
                                        start=part == 0, stop=part == 1)
                    ins.then_inc(bank_filled, 1)

            def turn(pair, u):
                out = slot[u % 2]
                pe.wait_ge(exped, pair.g * UNITS + (u + 1))
                for j in range(S):
                    ins = t_.transpose(out[:, j * P:(j + 1) * P], prob[:, u % 2, j * P:(j + 1) * P], ident[:, :])
                    if j == BANK // P - 1:
                        ins.then_inc(turned, 1)
                t_.transpose(out[0:CTX, SEQ:SEQ + P], prob[:, u % 2, SEQ:KEYS], ident[:, :]).then_inc(turned, 1)

            def await_copies(pair, u):
                pe.wait_ge(turned_act, pair.g * UNITS + (u + 1))
                pe.wait_ge(turned_dve, pair.g * UNITS + (u + 1))

            def weigh(pair, u):
                t, h = divmod(u, 2)
                if u == 0:
                    pe.wait_ge(act_freed, count(pair, "Vb", PROJECTED))
                await_copies(pair, u)
                if h == 0:
                    pe.wait_ge(o_out, pair.g * S + (t + 1))
                for j in range(KT_TILES):
                    rows = P if j < S else CTX
                    ins = t_.matmul(po[:, h, :], probT[0:rows, u % 2, j, :], V1[0:rows, pair.parity, j, h, :],
                                    start=j == 0, stop=j == S)
                ins.then_inc(weighed, 1)

            start = Pair(0, 0, 0, 0)
            for step in PIECES:
                piece(start, step)
            pe.wait_ge(padded, 10)
            score(start, 0)
            score(start, 1)

            def body(pair):
                after = pair.next()
                for u in range(UNITS):
                    turn(pair, u)
                    if after:
                        piece(after, PIECES[u])
                    if u > 0:
                        weigh(pair, u - 1)
                    nxt = ahead(pair, u, 2)
                    if nxt[0]:
                        await_copies(pair, u)
                        score(*nxt)
                weigh(pair, UNITS - 1)

            all_pairs(pe, body)

        @block.scalar
        def _(act):
            a_ = nc.scalar

            def piece(pair, step):
                if step in QUERY_TURNS:
                    return
                act.wait_ge(filled, count(pair, step, PIECES))
                first = isinstance(pair.g, int) and pair.g == 0
                lo = HALF if step.endswith("b") else 0
                half = side[:, :].rearrange("p (t h d) -> p t h d", h=2, d=D1)
                V = V1[:, pair.parity]
                K = knat[:, :, :].rearrange("p t (h d) -> p t h d", h=2)
                Q = qnat[:, :, :].rearrange("p t (h d) -> p t h d", h=2)
                if step in ("Ka", "Qa"):
                    if first:
                        act.wait_ge(set_up, NSET)
                    else:
                        act.wait_ge(scaled, pair.g * 2 - (1 if step == "Ka" else 0))
                if step == "c":
                    ok = valid[:, pair.b:pair.b + 1]
                    a_.activation(K[0:CTX, S], half[0:CTX, 0], ACT.Copy)
                    a_.activation(V[0:CTX, S, :, D1], ok.to_broadcast([CTX, 2]), ACT.Copy)
                    a_.activation(V[0:CTX, S, :, 0:D1], half[0:CTX, 1], ACT.Identity, scale=ok).then_inc(act_freed, 1)
                elif step in PROJECTED:
                    dst = {"K": K, "Q": Q}[step[0]][:, lo:lo + HALF] if step[0] != "V" else V[:, lo:lo + HALF, :, 0:D1]
                    a_.activation(dst, half, ACT.Copy).then_inc(act_freed, 1)
                elif step == "Kc":
                    a_.activation(KHL[:, pair.parity, :, 0, SEQ:KEYS], side[:, 0:2 * CTX].rearrange("p (h k) -> p h k", h=2),
                                  ACT.Copy).then_inc(khigh, 1)
                else:
                    a_.activation(KHL[:, pair.parity, int(step[1]), 0, lo * P:lo * P + BANK], side[:, :], ACT.Copy).then_inc(khigh, 1)

            def exponentials(pair, u):
                act.wait_ge(peaked, pair.g * UNITS + (u + 1))
                a_.activation(prob[:, u % 2, :], slot[u % 2][:, 0:KEYS], ACT.Exp, bias=npeak[:, u % 2:u % 2 + 1]).then_inc(exped, 1)

            def copy(pair, u):
                act.wait_ge(turned, (pair.g * UNITS + u) * 2 + 1)
                a_.activation(probT[:, u % 2, 0:BANK // P, :], slot[u % 2][:, 0:BANK].rearrange("p (t q) -> p t q", q=P),
                              ACT.Copy).then_inc(turned_act, 1)

            start = Pair(0, 0, 0, 0)
            for step in PIECES:
                piece(start, step)
            exponentials(start, 0)

            def body(pair):
                after = pair.next()
                for u in range(UNITS):
                    copy(pair, u)
                    nxt = ahead(pair, u, 1)
                    if nxt[0]:
                        exponentials(*nxt)
                    if after:
                        piece(after, PIECES[u])

            all_pairs(act, body)

        @block.vector
        def _(dve):
            v = nc.vector
            dve.sem_inc(o_out, 1)
            for p in range(2):
                for h in range(2):
                    for part in range(2):
                        v.memset(KHL[:, p, h, part, KEYS:W2].bitcast(F32), 0.0).then_inc(padded, 1)
            for i in range(2):
                v.memset(slot[i][:, 2 * BANK:], 0.0).then_inc(padded, 1)

            def peak(pair, u):
                n = (pair.g * UNITS + u) * 3
                part = part_peak[:, u % 2, :]
                for i, (lo, hi) in enumerate(((0, BANK), (BANK, SEQ), (SEQ, KEYS))):
                    dve.wait_ge(bank_filled, n + (i + 1))
                    v.tensor_reduce(part[:, i:i + 1], slot[u % 2][:, lo:hi], AX.X, ALU.max).then_inc(part_peaked, 1)
                dve.wait_ge(part_peaked, n + 3)
                v.tensor_reduce(npeak[:, u % 2:u % 2 + 1], part, AX.X, ALU.max, negate=True).then_inc(peaked, 1)

            def piece(pair, step):
                lo = BANK if step.endswith("b") else 0
                if step in KEY_TURNS:
                    dve.wait_ge(khigh, count(pair, step, KEY_TURNS))
                    if step == "Kc":
                        K, src = KHL[:, pair.parity, :, :, SEQ:KEYS], side[:, 0:2 * CTX].rearrange("p (h k) -> p h k", h=2)
                        v.tensor_tensor(K[:, :, 1], src, K[:, :, 0], ALU.subtract).then_inc(dve_freed, 1)
                    else:
                        K = KHL[:, pair.parity, int(step[1]), :, lo:lo + BANK]
                        v.tensor_tensor(K[:, 1], side[:, :], K[:, 0], ALU.subtract).then_inc(dve_freed, 1)
                elif step in QUERY_TURNS:
                    n = count(pair, step, QUERY_TURNS)
                    q = QHL[:, pair.parity, int(step[1]), lo:lo + BANK]
                    dve.wait_ge(filled, count(pair, step, PIECES))
                    if step != QUERY_TURNS[0] or not (isinstance(pair.g, int) and pair.g == 0):
                        dve.wait_ge(qlow, n - 1)
                    v.tensor_scalar(qgam[:, :], side[:, :], gamma[:, 0:1], None, ALU.mult).then_inc(dve_freed, 1)
                    dve.wait_ge(dve_freed, count(pair, step, TURNS))
                    v.tensor_copy(q, qgam[:, :]).then_inc(qhigh, 1)
                    dve.wait_ge(qhigh, n)
                    v.tensor_tensor(q[D1:, :], qgam[D1:, :], q[D1:, :], ALU.subtract).then_inc(qlow, 1)

            def sums(pair, j):
                sq, var = ((ksq, kvar), (qsq, qvar))[j]
                n = pair.g * 2 + (j + 1)
                dve.wait_ge(squared, n)
                v.tensor_reduce(var[:, :], sq[:, :, :].rearrange("p t (h d) -> p (t h) d", h=2), AX.X, ALU.add).then_inc(summed, 1)
                dve.wait_ge(summed, n)
                v.tensor_scalar(var[:, :], var[:, :], 1.0 / D1, 1e-16, ALU.mult, ALU.max).then_inc(meaned, 1)

            def copy(pair, u):
                dve.wait_ge(turned, (pair.g * UNITS + u) * 2 + 2)
                v.tensor_copy(probT[:, u % 2, BANK // P:, :], slot[u % 2][:, BANK:SEQ + P].rearrange("p (t q) -> p t q", q=P)
                              ).then_inc(turned_dve, 1)

            def normalise(pair, t):
                dve.wait_ge(weighed, pair.g * UNITS + (2 * t + 2))
                v.reciprocal(rsum[:, t % 2, :], po[:, :, D1]).then_inc(rsum_done, 1)
                dve.wait_ge(rsum_done, pair.g * S + (t + 1))
                if t == 0:
                    dve.wait_ge(o_stored[pair.parity], (pair.g - pair.parity) * 8 + 16)
                v.tensor_tensor(O[:, pair.parity, t, :].rearrange("p (h d) -> p h d", h=2), po[:, :, 0:D1],
                                rsum[:, t % 2, :].unsqueeze(2).to_broadcast([P, 2, D1]), ALU.mult).then_inc(o_out, 1)

            start = Pair(0, 0, 0, 0)
            sums(start, 0)
            sums(start, 1)
            for step in PIECES:
                piece(start, step)
            peak(start, 0)
            peak(start, 1)

            def body(pair):
                after = pair.next()
                for u in range(UNITS):
                    copy(pair, u)
                    if after:
                        piece(after, PIECES[u])
                        if PIECES[u] in ("Qa", "Va"):
                            sums(after, int(PIECES[u] == "Va"))
                    if u and u % 2 == 0:
                        normalise(pair, u // 2 - 1)
                    nxt = ahead(pair, u, 2)
                    if nxt[0]:
                        peak(*nxt)
                normalise(pair, S - 1)

            all_pairs(dve, body)
        attn.close()

        with ExitStack() as c3:
            sb3 = lambda n, s, d=F32: c3.enter_context(nc.sbuf_tensor(f"a1o_{n}", s, d))
            sem3 = lambda n: nc.alloc_semaphore(f"a1o_{n}")
            OC = H1 * D1 // P
            Wout, bout = sb3("Wout", [P, OC, E]), sb3("bout", [P, E])
            o = sb3("o", [P, 4, H1 * D1])
            oT = sb3("oT", [P, 2, OC, P])
            yb = sb3("yb", [P, 2, E])
            pT = [c3.enter_context(nc.psum_tensor(f"a1o_pT{i}", [P, OC, P], F32)) for i in range(2)]
            py = [c3.enter_context(nc.psum_tensor(f"a1o_py{i}", [P, BANK], F32)) for i in range(2)]
            w_loaded, t_done, t_out, y_done, y_out, added = (sem3(n) for n in ("w_loaded", "t_done", "t_out", "y_done", "y_out", "added"))
            o_loaded = [sem3(f"o_loaded{i}") for i in range(4)]
            with nc.Block() as block:
                @block.sync
                def _(sp):
                    sp.dma_start(Wout[:, :, :], I["L1_xattn_Wout"].rearrange("(c p) n -> p c n", p=P)).then_inc(w_loaded, 16)
                    sp.dma_start(bout[:, :], I["L1_xattn_bout"].to_broadcast([P, E])).then_inc(w_loaded, 16)
                    for t in range(TILES):
                        if t >= 4:
                            sp.wait_ge(t_done, t - 3)
                        sp.dma_start(o[:, t % 4, :], o_rows[t * P:(t + 1) * P, :]).then_inc(o_loaded[t % 4], 16)

                @block.tensor
                def _(pe):
                    def project(t):
                        pe.wait_ge(t_out, t + 1)
                        if t >= 2:
                            pe.wait_ge(y_out, t - 1)
                        for c in range(OC):
                            ins = nc.tensor.matmul(py[t % 2][:, 0:E], oT[:, t % 2, c, :], Wout[:, c, :],
                                                   start=c == 0, stop=c == OC - 1)
                        ins.then_inc(y_done, 1)

                    pe.wait_ge(w_loaded, 32)
                    for t in range(TILES):
                        pe.wait_ge(o_loaded[t % 4], 16 * (t // 4 + 1))
                        if t >= 2:
                            pe.wait_ge(t_out, t - 1)
                        for c in range(OC):
                            ins = nc.tensor.transpose(pT[t % 2][:, c, :], o[:, t % 4, c * P:(c + 1) * P], ident[:, :])
                        ins.then_inc(t_done, 1)
                        if t:
                            project(t - 1)
                    project(TILES - 1)

                @block.scalar
                def _(act):
                    for t in range(TILES):
                        act.wait_ge(t_done, t + 1)
                        if t >= 2:
                            act.wait_ge(y_done, t - 1)
                        nc.scalar.activation(oT[:, t % 2, :, :], pT[t % 2][:, :, :], ACT.Copy).then_inc(t_out, 1)

                @block.vector
                def _(dve):
                    dve.wait_ge(w_loaded, 32)
                    for t in range(TILES):
                        dve.wait_ge(y_done, t + 1)
                        if t >= 2:
                            dve.wait_ge(added, t - 1)
                        nc.vector.tensor_tensor(yb[:, t % 2, :], py[t % 2][:, 0:E], bout[:, :], ALU.add).then_inc(y_out, 1)
                        dve.wait_ge(y_out, t + 1)
                        nc.vector.tensor_tensor(xres[:, t, :], xres[:, t, :], yb[:, t % 2, :], ALU.add).then_inc(added, 1)
                    dve.wait_ge(added, TILES)


def layer0_mixture(nc, I, xres, ident):
    mixture(nc, I, xres, ident, 0)


def layer1_mixture(nc, I, xres, ident):
    mixture(nc, I, xres, ident, 1)


PHASES = [layer0_attention, layer0_mixture, layer1_attention, layer1_mixture]


def lay_out(inputs):
    a = {n: np.asarray(v) for n, v in inputs.items()}
    out = {"x": a["x"], "ident": np.eye(P, dtype=np.float32)}
    for n in ("Wq", "Wk", "Wv", "Wo"):
        out[f"L0_xattn_{n}T"] = a[f"L0_xattn_{n}"].T
    out["ctxT"] = a["ctx_1024"].reshape(BATCH * CTX, E).T
    for n in ("bq", "bk"):
        out[f"L0_xattn_{n}"] = a[f"L0_xattn_{n}"].reshape(EC, P).T
    for n in ("bv", "bo"):
        out[f"L0_xattn_{n}"] = a[f"L0_xattn_{n}"].reshape(1, E)
    out["head_mask"] = (np.arange(P)[:, None] // D0 == np.arange(GROUP)).astype(np.float32)
    rows = np.clip(np.arange(BAND)[None, :] - (P - 1) - P * np.arange(NEAR)[:, None], -REACH, REACH) + REACH
    out["rel_k"] = np.tile(np.moveaxis(a["L0_xattn_rk_table"][rows], 2, 0), (GROUP, 1, 1))
    out["rel_v"] = a["L0_xattn_rv_table"][rows].reshape(NEAR, 2, BAND // 2, D0).transpose(2, 0, 1, 3)
    out["rv_far"] = np.tile(a["L0_xattn_rv_table"][0], H0)[None, :]
    out["iota"] = np.arange(P, dtype=np.float32)[None, :]
    out["lane"] = np.stack([np.arange(P), DUMP + np.arange(P)], 1).astype(np.float32)
    out["before"] = np.triu(np.ones((P, P), np.float32), 1)
    out["L0_router"] = a["L0_ffn_router_weight"].T
    out["L0_ffn_router_bias"] = a["L0_ffn_router_bias"][None, :]
    out["L1_router"] = a["L1_ffn_Wg"]
    for n in ("L0_ffn_gate_up_proj", "L0_ffn_down_proj", "L1_ffn_W1", "L1_ffn_W2"):
        out[n] = a[n]
    for n in ("L0_ffn_gate_up_bias", "L0_ffn_down_bias", "L1_ffn_b1", "L1_ffn_b2"):
        out[n] = a[n].reshape(1, -1)
    for n in ("ln_x_g", "ln_x_b", "ln_l_g", "ln_l_b"):
        out[f"L1_xattn_{n}"] = a[f"L1_xattn_{n}"].reshape(EC, P).T
    for n in ("qn_g", "kn_g"):
        out[f"L1_xattn_{n}"] = np.tile(a[f"L1_xattn_{n}"], 2)[:, None]
    out["mask"] = a["mask_BxS2_bf1"].reshape(1, -1).view(np.uint8)
    out["maskT"] = a["mask_BxS2_bf1"].T.view(np.uint8)
    out["ctx"] = a["ctx_1024"]
    for n in ("Wq", "Wkv", "Wout"):
        out[f"L1_xattn_{n}"] = a[f"L1_xattn_{n}"]
    out["L1_xattn_bout"] = a["L1_xattn_bout"][None, :]
    return {n: np.ascontiguousarray(v) for n, v in out.items()}


def program(nc, I, out):
    with ExitStack() as ctx:
        xres = ctx.enter_context(nc.sbuf_tensor("xres", [P, TILES, E], F32))
        ident = ctx.enter_context(nc.sbuf_tensor("ident", [P, P], F32))
        load_residual(nc, I["x"], I["ident"], xres, ident)
        for phase in PHASES:
            phase(nc, I, xres, ident)
        store_residual(nc, xres, out)


def kernel(**inputs):
    import concourse.bacc as bacc
    from concourse.bass_utils import run_bass_kernel_spmd

    nc = bacc.Bacc("TRN2", target_bir_lowering=False, num_devices=1)
    arrays = {f"in_{n}_dram": v for n, v in lay_out(inputs).items()}
    aps = {n[3:-5]: nc.dram_tensor(n, v.shape, mybir.dt.from_np(v.dtype), kind="ExternalInput").ap()
           for n, v in arrays.items()}
    out = nc.dram_tensor("out_0_dram", (BATCH, SEQ, E), F32, kind="ExternalOutput").ap()
    program(nc, aps, out)
    r = run_bass_kernel_spmd(nc, [arrays], core_ids=[0])
    return r.results[0]["out_0_dram"]
```

```python
from contextlib import ExitStack, contextmanager

import concourse.bass as bass
from concourse import mybir
import numpy as np

F32 = mybir.dt.float32
F32R = mybir.dt.float32r
BF16 = mybir.dt.bfloat16
I32 = mybir.dt.int32
U32 = mybir.dt.uint32
U8 = mybir.dt.uint8
ALU = mybir.AluOpType
ACT = mybir.ActivationFunctionType
AX = mybir.AxisListType

P = 128
BATCH, SEQ, E = 2, 1024, 256
CTX = 77
TOKENS = BATCH * SEQ
TILES = TOKENS // P
EC = E // P
LN_EPS = 1e-5

H0 = 16
D0 = E // H0
REACH = 128
GROUP = P // D0
GATHERS = 4
LN_GROUP = 4
CHUNKS = -(-H0 * CTX // P)
CHUNK_HEADS = 3
TURN = 4
HEAD_GROUPS = H0 // GROUP
BAND = CTX + P - 1
V0 = D0 + 1
NEAR = 2
BANK = 512

NE = 8
TOPK = 2
SLOT_COLS = TOPK * TILES
BLOCKS = (TOPK * TOKENS + NE * (P - 1)) // P
DUMP = TOPK * TOKENS

H1, D1 = 16, 64
KEYS = SEQ + CTX
KT_TILES = SEQ // P + 1
PAIRS = H1 // 2
CAPACITY = 2 * TOPK * TOKENS // NE


@contextmanager
def phase(nc):
    with nc.cleanup_on_exit(), ExitStack() as ctx:
        yield ctx


class Steps:

    def __init__(self, engine, sem):
        self.engine, self.sem, self.n = engine, sem, 0

    def mark(self, ins):
        self.n += 1
        return ins.then_inc(self.sem, 1)

    def after(self, ins):
        self.mark(ins)
        self.engine.wait_ge(self.sem, self.n)


def layer_norm(nc, name, src, dst, ident, dstT=None, gain=None, shift=None, store=None):
    with phase(nc) as ctx:
        sb = lambda n, s, d=F32: ctx.enter_context(nc.sbuf_tensor(f"{name}_{n}", s, d))
        sem = lambda n: nc.alloc_semaphore(f"{name}_{n}")
        stats = sb("stats", [P, TILES, 6])
        moments = sb("moments", [P, TILES, 2])
        variance = sb("variance", [P, TILES])
        exponent = sb("exponent", [P, TILES])
        rstd = sb("rstd", [P, TILES])
        turned = [ctx.enter_context(nc.psum_tensor(f"{name}_turned{i}", [P, EC, P], F32)) for i in range(4)]
        stats_done, moments_done, variance_done = sem("stats_done"), sem("moments_done"), sem("variance_done")
        exponent_set, rstd_done, dst_done = sem("exponent_set"), sem("rstd_done"), sem("dst_done")
        turned_done, copied = sem("turned_done"), sem("copied")
        block = ctx.enter_context(nc.Block())

        @block.vector
        def _(dve):
            def moments_of(g):
                tiles = range(g * LN_GROUP, (g + 1) * LN_GROUP)
                for t in tiles:
                    nc.vector.bn_stats(stats[:, t, :], src[:, t, :]).then_inc(stats_done, 1)
                for t in tiles:
                    dve.wait_ge(stats_done, t + 1)
                    nc.vector.bn_aggr(moments[:, t, :], stats[:, t, :]).then_inc(moments_done, 1)
                dve.wait_ge(moments_done, tiles.stop)
                cols = slice(tiles.start, tiles.stop)
                nc.vector.tensor_scalar(variance[:, cols], moments[:, cols, 1], LN_EPS, None, ALU.add).then_inc(variance_done, 1)

            moments_of(0)
            for g in range(TILES // LN_GROUP):
                if (g + 1) * LN_GROUP < TILES:
                    moments_of(g + 1)
                dve.wait_ge(rstd_done, g + 1)
                for t in range(g * LN_GROUP, (g + 1) * LN_GROUP):
                    nc.vector.tensor_scalar(dst[:, t, :], src[:, t, :], moments[:, t, 0:1], rstd[:, t:t + 1],
                                            ALU.subtract, ALU.mult).then_inc(dst_done, 1)

        @block.gpsimd
        def _(pool):
            nc.gpsimd.memset(exponent[:, :], -0.5).then_inc(exponent_set, 1)
            pool.wait_ge(exponent_set, 1)
            for g in range(TILES // LN_GROUP):
                pool.wait_ge(variance_done, g + 1)
                cols = slice(g * LN_GROUP, (g + 1) * LN_GROUP)
                nc.gpsimd.tensor_tensor(rstd[:, cols], variance[:, cols], exponent[:, cols], ALU.pow).then_inc(rstd_done, 1)

        @block.tensor
        def _(pe):
            for t in range(TILES if dstT is not None else 0):
                pe.wait_ge(dst_done, t + 1)
                if t >= 4:
                    pe.wait_ge(copied, t - 3)
                for c in range(EC):
                    ins = nc.tensor.transpose(turned[t % 4][:, c, :], dst[:, t, c * P:(c + 1) * P], ident[:, :])
                ins.then_inc(turned_done, 1)

        @block.scalar
        def _(act):
            for t in range(TILES if dstT is not None else 0):
                act.wait_ge(turned_done, t + 1)
                cols = slice(t * P, (t + 1) * P)
                if gain is None:
                    nc.scalar.activation(dstT[:, :, cols], turned[t % 4][:, :, :], ACT.Copy).then_inc(copied, 1)
                else:
                    for c in range(EC):
                        ins = nc.scalar.activation(dstT[:, c, cols], turned[t % 4][:, c, :], ACT.Identity,
                                                   bias=shift[:, c:c + 1], scale=gain[:, c:c + 1])
                    ins.then_inc(copied, 1)

        @block.sync
        def _(sp):
            if store is not None:
                rows, stored = store
                for t in range(TILES):
                    sp.wait_ge(dst_done, t + 1)
                    sp.dma_start(rows[t * P:(t + 1) * P, :], dst[:, t, :]).then_inc(stored, 16)


def load_residual(nc, x, ident_in, xres, ident):
    with phase(nc) as ctx:
        x_loaded = nc.alloc_semaphore("x_loaded")
        block = ctx.enter_context(nc.Block())

        @block.sync
        def _(sp):
            sp.dma_start(xres[:, :, :], x.rearrange("b (t p) e -> p (b t) e", p=P)).then_inc(x_loaded, 16)
            sp.dma_start(ident[:, :], ident_in).then_inc(x_loaded, 16)
            sp.wait_ge(x_loaded, 32)


def layer0_attention(nc, I, xres, ident):
    with phase(nc) as ctx:
        sb = lambda n, s, d=F32: ctx.enter_context(nc.sbuf_tensor(f"a0_{n}", s, d))
        sem = lambda n: nc.alloc_semaphore(f"a0_{n}")
        XW = BAND + 1
        near_tiles = [b * (SEQ // P) + i for b in range(BATCH) for i in range(NEAR)]
        far_tiles = [t for t in range(TILES) if t not in near_tiles]
        NN = len(near_tiles)

        QT = sb("QT", [P, EC, TOKENS])
        dist_d = nc.dram_tensor("a0_dist_dram", [NN, P, BAND, H0], F32)
        prob_d = nc.dram_tensor("a0_prob_dram", [NN, P, BAND, H0], F32)
        Wo = sb("Wo", [P, EC, E])
        bo = sb("bo", [P, E])
        kblock = sb("kblock", [P, 2, BATCH, HEAD_GROUPS, GROUP, CTX])
        rblock = sb("rblock", [P, NEAR, GROUP, BAND])
        vones = sb("vones", [CTX, 2, BATCH, H0, V0])
        rv = sb("rv", [BAND // 2, NEAR, 2, 2 * GROUP - 1, V0])
        vpacked = sb("vpacked", [P, CHUNKS, BATCH, CHUNK_HEADS, V0])

        with ExitStack() as c2:
            sb2 = lambda n, s, d=F32: c2.enter_context(nc.sbuf_tensor(f"a0p_{n}", s, d))
            sem2 = lambda n: nc.alloc_semaphore(f"a0p_{n}")
            xn = sb2("xn", [P, TILES, E])
            xnT = sb2("xnT", [P, EC, TOKENS])
            W = {n: sb2(n, [P, EC, E]) for n in ("Wq", "Wk", "Wv")}
            ctxT = sb2("ctxT", [P, EC, BATCH * CTX])
            bq, bqs, bk = sb2("bq", [P, EC]), sb2("bqs", [P, EC]), sb2("bk", [P, EC])
            bv, rv0 = sb2("bv", [CTX, E]), sb2("rv0", [CTX, E])
            mask = sb2("mask", [P, GROUP])
            relk = sb2("relk", [P, NEAR, BAND])
            kT = sb2("kT", [P, 2, EC, BATCH * CTX])
            vnear = sb2("vnear", [CTX, BATCH, E])
            zeros = sb2("zeros", [P, BAND * H0])
            loaded = sem2("loaded")
            with nc.Block() as block:
                @block.sync
                def _(sp):
                    for n, dst in (("Wk", W["Wk"]), ("Wv", W["Wv"]), ("Wq", W["Wq"]), ("Wo", Wo)):
                        sp.dma_start(dst[:, :, :], I["L0_xattn_" + n + "T"].rearrange("(c p) n -> p c n", p=P)).then_inc(loaded, 16)
                    sp.dma_start(ctxT[:, :, :], I["ctxT"].rearrange("(c p) n -> p c n", p=P)).then_inc(loaded, 16)
                    sp.dma_start(bq[:, :], I["L0_xattn_bq"]).then_inc(loaded, 16)
                    sp.dma_start(bk[:, :], I["L0_xattn_bk"]).then_inc(loaded, 16)
                    sp.dma_start(bv[:, :], I["L0_xattn_bv"].to_broadcast([CTX, E])).then_inc(loaded, 16)
                    sp.dma_start(rv0[:, :], I["rv_far"].to_broadcast([CTX, E])).then_inc(loaded, 16)
                    sp.dma_start(bo[:, :], I["L0_xattn_bo"].to_broadcast([P, E])).then_inc(loaded, 16)
                    sp.dma_start(mask[:, :], I["head_mask"]).then_inc(loaded, 16)
                    sp.dma_start(relk[:, :, :], I["rel_k"]).then_inc(loaded, 16)
            layer_norm(nc, "a0ln", xres, xn, ident, xnT)
            pq = [c2.enter_context(nc.psum_tensor(f"a0_pq{i}", [P, BANK], F32)) for i in range(4)]
            pk = c2.enter_context(nc.psum_tensor("a0_pk", [P, EC, BATCH * CTX], F32))
            pv = c2.enter_context(nc.psum_tensor("a0_pv", [CTX, BATCH, E], F32))
            rv_loaded, zeroed, cleared = sem2("rv_loaded"), sem2("zeroed"), sem2("cleared")
            q_done, q_out, k_done, k_out, v_done = (sem2(n) for n in ("q_done", "q_out", "k_done", "k_out", "v_done"))
            step, bias_ready, tails = sem2("step"), sem2("bias_ready"), sem2("tails")
            NLOAD = 12
            block = c2.enter_context(nc.Block())

            @block.sync
            def _(sp):
                sp.wait_ge(tails, 1)
                sp.dma_start(rv[:, :, :, GROUP - 1, 0:D0], I["rel_v"]).then_inc(rv_loaded, 16)
                sp.wait_ge(zeroed, 1)
                for n in range(NN):
                    sp.dma_start(prob_d[n].rearrange("p j h -> p (j h)"), zeros[:, :]).then_inc(cleared, 16)
                sp.wait_ge(cleared, 16 * NN)
                sp.wait_ge(rv_loaded, 16)

            @block.gpsimd
            def _(pool):
                nc.gpsimd.memset(zeros[:, :], 0.0).then_inc(zeroed, 1)
                nc.gpsimd.memset(vpacked[:, :, :, :, :], 0.0)

            @block.tensor
            def _(pe):
                pe.wait_ge(loaded, 16 * NLOAD)
                for g in range(EC):
                    for c in range(EC):
                        ins = nc.tensor.matmul(pk[:, g, :], W["Wk"][:, c, g * P:(g + 1) * P], ctxT[:, c, :],
                                               start=c == 0, stop=c == EC - 1)
                ins.then_inc(k_done, 1)
                for b in range(BATCH):
                    for c in range(EC):
                        ins = nc.tensor.matmul(pv[:, b, :], ctxT[:, c, b * CTX:(b + 1) * CTX], W["Wv"][:, c, :],
                                               start=c == 0, stop=c == EC - 1)
                ins.then_inc(v_done, 1)
                for g in range(EC):
                    for n in range(TOKENS // BANK):
                        i = g * (TOKENS // BANK) + n
                        if i >= 4:
                            pe.wait_ge(q_out, i - 3)
                        for c in range(EC):
                            ins = nc.tensor.matmul(pq[i % 4][:, :], W["Wq"][:, c, g * P:(g + 1) * P],
                                                   xnT[:, c, n * BANK:(n + 1) * BANK], start=c == 0, stop=c == EC - 1)
                        ins.then_inc(q_done, 1)

            @block.scalar
            def _(act):
                act.wait_ge(bias_ready, 1)
                act.wait_ge(k_done, 1)
                for g in range(EC):
                    ins = nc.scalar.activation(kT[:, 0, g, :], pk[:, g, :], ACT.Identity, bias=bk[:, g:g + 1])
                ins.then_inc(k_out, 1)
                for g in range(EC):
                    for n in range(TOKENS // BANK):
                        i = g * (TOKENS // BANK) + n
                        act.wait_ge(q_done, i + 1)
                        nc.scalar.activation(QT[:, g, n * BANK:(n + 1) * BANK], pq[i % 4][:, :], ACT.Identity,
                                             bias=bqs[:, g:g + 1], scale=D0 ** -0.5).then_inc(q_out, 1)

            @block.vector
            def _(dve):
                s = Steps(dve, step)
                s.mark(nc.vector.memset(vones[:, :, :, :, D0:V0], 1.0))
                nc.vector.memset(rv[:, :, :, :, :], 0.0).then_inc(tails, 1)
                dve.wait_ge(loaded, 16 * NLOAD)
                nc.vector.tensor_scalar(bqs[:, :], bq[:, :], D0 ** -0.5, None, ALU.mult).then_inc(bias_ready, 1)
                for i in range(NEAR):
                    s.mark(nc.vector.tensor_tensor(
                        rblock[:, i, :, :], relk[:, i, :].unsqueeze(1).to_broadcast([P, GROUP, BAND]),
                        mask[:, :].unsqueeze(2).to_broadcast([P, GROUP, BAND]), ALU.mult))
                dve.wait_ge(v_done, 1)
                for b in range(BATCH):
                    s.mark(nc.vector.tensor_tensor(vnear[:, b, :], pv[:, b, :], bv[:, :], ALU.add))
                dve.wait_ge(step, s.n)
                for b in range(BATCH):
                    v = vnear[:, b, :].rearrange("p (h d) -> p h d", h=H0)
                    s.mark(nc.vector.tensor_copy(vones[:, 0, b, :, 0:D0], v))
                    s.mark(nc.vector.tensor_tensor(vones[:, 1, b, :, 0:D0], v,
                                                   rv0[:, :].rearrange("p (h d) -> p h d", h=H0), ALU.add))
                dve.wait_ge(k_out, 1)
                for g in range(EC):
                    s.mark(nc.vector.tensor_scalar(kT[:, 1, g, :], kT[:, 0, g, :], relk[:, 1, 0:1], None, ALU.add))
                dve.wait_ge(step, s.n)
                for far in range(2):
                    for b in range(BATCH):
                        for g in range(HEAD_GROUPS):
                            nc.vector.tensor_tensor(
                                kblock[:, far, b, g, :, :],
                                kT[:, far, g, b * CTX:(b + 1) * CTX].unsqueeze(1).to_broadcast([P, GROUP, CTX]),
                                mask[:, :].unsqueeze(2).to_broadcast([P, GROUP, CTX]), ALU.mult)

        GB = GROUP // 2
        SB = H0 // GB
        value_order = far_tiles + near_tiles
        soft_order = list(far_tiles)
        for n, t in enumerate(near_tiles):
            soft_order.insert(4 + 3 * n, t)
        dist = sb("dist", [P, 2, BAND, H0])
        near_scores = sb("near_scores", [P, NN, CTX, H0])
        shifted = sb("shifted", [P, H0, CTX])
        biased = sb("biased", [P, H0, CTX])
        peak = sb("peak", [P, 2, H0])
        prob = sb("prob", [P, 3, CHUNKS * P])
        near_prob = sb("near_prob", [P, NN, CTX, H0])
        band_prob = sb("band_prob", [P, 2, BAND, H0])
        probT = sb("probT", [P, 2, TURN, P])
        rsum = sb("rsum", [P, H0])
        O = sb("O", [P, H0, D0])
        OT = sb("OT", [P, EC, P])
        yb = sb("yb", [P, E])
        ps = ctx.enter_context(nc.psum_tensor("a0_ps", [P, SB, BANK], F32))
        pt = [ctx.enter_context(nc.psum_tensor(f"a0_pt{i}", [P, TURN, P], F32)) for i in range(2)]
        po = ctx.enter_context(nc.psum_tensor("a0_po", [P, H0, V0], F32))
        py = ctx.enter_context(nc.psum_tensor("a0_py", [P, BANK], F32))
        d_done, d_out = sem("d_done"), sem("d_out")
        d_stored = [sem(f"d_stored{i}") for i in range(2)]
        d_back = [sem(f"d_back{n}") for n in range(NN)]
        p_back = [sem(f"p_back{n}") for n in range(NN)]
        s_done, s_shift, p_done = (sem(n) for n in ("s_done", "s_shift", "p_done"))
        p_stored, t_done, t_out, pt_used = (sem(n) for n in ("p_stored", "t_done", "t_out", "pt_used"))
        o_out, ot_done, ot_out, y_done, y_out = (sem(n) for n in ("o_out", "ot_done", "ot_out", "y_done", "y_out"))
        step = sem("step")
        DHEADS = 2
        DGROUPS = H0 // DHEADS

        def rounds(t):
            def cut(blocks):
                return [blocks[i:i + TURN] for i in range(0, len(blocks), TURN)]

            if t not in near_tiles:
                return cut(list(range(CHUNKS)))
            keys, band = cut([(h, None) for h in range(H0)]), cut([(h, c) for h in range(H0) for c in range(2)])
            return [r for i, k in enumerate(keys) for r in (k, band[2 * i], band[2 * i + 1])]

        ROUNDS = [(i, r, blocks) for i, t in enumerate(value_order) for r, blocks in enumerate(rounds(t))]
        until = [min(TILES, soft_order.index(t) + 2) if t in far_tiles else TILES for t in value_order[1:]] + [TILES]
        ahead = [list(range(until[i - 1] if i else 1, until[i])) for i in range(TILES)]
        assert max(map(len, ahead)) == 2
        prob_slot = {t: i % 3 for i, t in enumerate(far_tiles)}
        round_ends = {value_order[i]: n + 1 for n, (i, r, _) in enumerate(ROUNDS)}

        def is_band(blocks):
            return isinstance(blocks[0], tuple) and blocks[0][1] is not None

        def rows_of(blocks):
            return P if not isinstance(blocks[0], tuple) else BAND // 2 if is_band(blocks) else CTX

        PLACES = []
        for h in range(H0):
            for c in range(h * CTX // P, ((h + 1) * CTX - 1) // P + 1):
                lo, hi = max(h * CTX, c * P), min((h + 1) * CTX, (c + 1) * P)
                PLACES.append((h, lo - h * CTX, hi - lo, c, lo - c * P))
        first_head = [min(h for h, _, _, c, _ in PLACES if c == k) for k in range(CHUNKS)]
        heads_in = [max(h for h, _, _, c, _ in PLACES if c == k) + 1 - first_head[k] for k in range(CHUNKS)]
        padded, v_placed = sem("padded"), sem("v_placed")

        block = ctx.enter_context(nc.Block())

        @block.sync
        def _(sp):
            for n in range(NN):
                sp.wait_ge(d_out, DGROUPS * (n + 1))
                sp.dma_start(dist_d[n].rearrange("p j h -> p (j h)"),
                             dist[:, n % 2, :, :].rearrange("p j h -> p (j h)")).then_inc(d_stored[n % 2], 16)
                sp.wait_ge(d_stored[n % 2], 16 * (n // 2 + 1))
                sheared = bass.AP(dist_d, n * P * BAND * H0 + (P - 1) * H0, [[(BAND - 1) * H0, P], [1, CTX * H0]])
                sp.dma_start(near_scores[:, n].rearrange("p j h -> p (j h)"), sheared).then_inc(d_back[n], 16)
            for n, t in enumerate(near_tiles):
                sp.wait_ge(p_done, soft_order.index(t) + 1)
                sheared = bass.AP(prob_d, n * P * BAND * H0 + (P - 1) * H0, [[(BAND - 1) * H0, P], [1, CTX * H0]])
                sp.dma_start(sheared, near_prob[:, n].rearrange("p j h -> p (j h)")).then_inc(p_stored, 16)
            for n, t in enumerate(near_tiles):
                sp.wait_ge(p_stored, 16 * NN)
                if n >= 2:
                    sp.wait_ge(t_done, round_ends[near_tiles[n - 2]])
                sp.dma_start(band_prob[:, n % 2].rearrange("p j h -> p (j h)"),
                             prob_d[n].rearrange("p j h -> p (j h)")).then_inc(p_back[n], 16)

        @block.gpsimd
        def _(pool):
            for h, key, keys, c, row in PLACES:
                nc.gpsimd.dma_start(vpacked[row:row + keys, c, :, h - first_head[c], :],
                                    vones[key:key + keys, 1, :, h, :]).then_inc(v_placed, 16)
            pool.wait_ge(v_placed, 16 * len(PLACES))

        @block.tensor
        def _(pe):
            for n, t in enumerate(near_tiles):
                for i in range(DGROUPS):
                    k = n * DGROUPS + i
                    if k >= SB:
                        pe.wait_ge(d_out, k - SB + 1)
                    g, h = divmod(i * DHEADS, GROUP)
                    nc.tensor.matmul(ps[:, k % SB, 0:DHEADS * BAND], QT[:, g, t * P:(t + 1) * P],
                                     rblock[:, n % NEAR, h:h + DHEADS, :],
                                     start=True, stop=True).then_inc(d_done, 1)
            pe.wait_ge(d_out, NN * DGROUPS)

            def scores(i):
                t = soft_order[i]
                far, b = int(t not in near_tiles), t // (SEQ // P)
                if i:
                    pe.wait_ge(s_shift, i)
                for j in range(SB):
                    g, h = divmod(j * GB, GROUP)
                    ins = nc.tensor.matmul(ps[:, j, 0:GB * CTX], QT[:, g, t * P:(t + 1) * P],
                                           kblock[:, far, b, g, h:h + GB, :], start=True, stop=True)
                ins.then_inc(s_done, 1)

            def turn(n):
                i, r, blocks = ROUNDS[n]
                t = value_order[i]
                if r == 0:
                    pe.wait_ge(p_done, soft_order.index(t) + 1)
                if n >= 2:
                    pe.wait_ge(t_out, n - 1)
                if is_band(blocks) and not is_band(ROUNDS[n - 1][2]):
                    pe.wait_ge(p_back[near_tiles.index(t)], 16)
                for j, block_ in enumerate(blocks):
                    if t not in near_tiles:
                        ins = nc.tensor.transpose(pt[n % 2][:, j, :], prob[:, prob_slot[t], block_ * P:(block_ + 1) * P], ident[:, :])
                        continue
                    h, c = block_
                    if c is None:
                        ins = nc.tensor.transpose(pt[n % 2][0:CTX, j, :], near_prob[:, near_tiles.index(t), :, h], ident[:, :])
                    else:
                        rows = slice(c * (BAND // 2), (c + 1) * (BAND // 2))
                        ins = nc.tensor.transpose(pt[n % 2][0:BAND // 2, j, :],
                                                  band_prob[:, near_tiles.index(t) % 2, rows, h], ident[:, :])
                ins.then_inc(t_done, 1)

            def weigh(n):
                i, r, blocks = ROUNDS[n]
                t = value_order[i]
                b = t // (SEQ // P)
                pe.wait_ge(t_out, n + 1)
                if r == 0 and i:
                    pe.wait_ge(o_out, i)
                for j, block_ in enumerate(blocks):
                    if t not in near_tiles:
                        h, heads = first_head[block_], heads_in[block_]
                        ins = nc.tensor.matmul(po[:, h:h + heads, :], probT[:, n % 2, j, :], vpacked[:, block_, b, 0:heads, :],
                                               start=r == 0 and j == 0, stop=True, skip_group_check=True)
                        continue
                    h, c = block_
                    if c is None:
                        rows, rhs, dst = CTX, vones[:, 0, b, h, :], po[:, h, :]
                    else:
                        g, m = divmod(h, GROUP)
                        rows, dst = BAND // 2, po[:, g * GROUP:(g + 1) * GROUP, :]
                        rhs = rv[:, near_tiles.index(t) % NEAR, c, GROUP - 1 - m:2 * GROUP - 1 - m, :]
                    ins = nc.tensor.matmul(dst, probT[0:rows, n % 2, j, :], rhs,
                                           start=r == 0 and j == 0, stop=True, skip_group_check=True)
                ins.then_inc(pt_used, 1)

            def turn_outputs(i):
                pe.wait_ge(o_out, i + 1)
                if i:
                    pe.wait_ge(y_out, i)
                for c in range(EC):
                    ins = nc.tensor.transpose(py[:, c * P:(c + 1) * P],
                                              O[:, c * GROUP:(c + 1) * GROUP, :].rearrange("p h d -> p (h d)"), ident[:, :])
                ins.then_inc(ot_done, 1)

            def project_outputs(i):
                pe.wait_ge(ot_out, i + 1)
                for c in range(EC):
                    ins = nc.tensor.matmul(py[:, E:2 * E], OT[:, c, :], Wo[:, c, :], start=c == 0, stop=c == EC - 1)
                ins.then_inc(y_done, 1)

            scores(0)
            scores(ahead[0][0])
            pe.wait_ge(padded, 1)
            pe.wait_ge(v_placed, 16 * len(PLACES))
            turn(0)
            for n, (i, r, blocks) in enumerate(ROUNDS):
                if n + 1 < len(ROUNDS):
                    turn(n + 1)
                weigh(n)
                if r == 1 and i:
                    turn_outputs(i - 1)
                if r == 1 and len(ahead[i]) == 2:
                    scores(ahead[i][1])
                if r == 2 and i:
                    project_outputs(i - 1)
                if n + 1 == round_ends[value_order[i]] and i + 1 < TILES and ahead[i + 1]:
                    scores(ahead[i + 1][0])
            turn_outputs(TILES - 1)
            project_outputs(TILES - 1)

        @block.scalar
        def _(act):
            for k in range(NN * DGROUPS):
                act.wait_ge(d_done, k + 1)
                n = k // DGROUPS
                if k % DGROUPS == 0 and n >= 2:
                    act.wait_ge(d_stored[n % 2], 16 * (n // 2))
                h = k % DGROUPS * DHEADS
                nc.scalar.activation(dist[:, n % 2, :, h:h + DHEADS].rearrange("p j h -> p h j"),
                                     ps[:, k % SB, 0:DHEADS * BAND].rearrange("p (h j) -> p h j", h=DHEADS),
                                     ACT.Copy).then_inc(d_out, 1)

            def soft(i):
                t = soft_order[i]
                act.wait_ge(s_shift, i + 1)
                if t not in near_tiles and far_tiles.index(t) >= 3:
                    act.wait_ge(t_done, round_ends[far_tiles[far_tiles.index(t) - 3]])
                dst = (near_prob[:, near_tiles.index(t)].rearrange("p k h -> p h k") if t in near_tiles else
                       prob[:, prob_slot[t], 0:H0 * CTX].rearrange("p (h k) -> p h k", h=H0))
                nc.scalar.activation(dst, shifted[:, :, :], ACT.Exp).then_inc(p_done, 1)

            soft(0)
            for n, (i, r, blocks) in enumerate(ROUNDS):
                act.wait_ge(t_done, n + 1)
                if n >= 2:
                    act.wait_ge(pt_used, n - 1)
                rows, k = rows_of(blocks), len(blocks)
                nc.scalar.activation(probT[0:rows, n % 2, 0:k, :], pt[n % 2][0:rows, 0:k, :], ACT.Copy).then_inc(t_out, 1)
                if r == 2:
                    if i:
                        act.wait_ge(ot_done, i)
                        if i >= 2:
                            act.wait_ge(y_done, i - 1)
                        nc.scalar.activation(OT[:, :, :], py[:, 0:E].rearrange("p (c n) -> p c n", c=EC),
                                             ACT.Copy).then_inc(ot_out, 1)
                    if ahead[i]:
                        soft(ahead[i][0])
                    if len(ahead[i]) == 2:
                        soft(ahead[i][1])
            act.wait_ge(ot_done, TILES)
            nc.scalar.activation(OT[:, :, :], py[:, 0:E].rearrange("p (c n) -> p c n", c=EC), ACT.Copy).then_inc(ot_out, 1)

        @block.vector
        def _(dve):
            s = Steps(dve, step)
            nc.vector.memset(prob[:, :, H0 * CTX:], 0.0).then_inc(padded, 1)

            def shift(i):
                t = soft_order[i]
                dve.wait_ge(s_done, i + 1)
                src = ps[:, :, 0:GB * CTX].rearrange("p b (h k) -> p b h k", h=GB)
                if t in near_tiles:
                    dve.wait_ge(d_back[near_tiles.index(t)], 16)
                    for j in range(SB):
                        ins = nc.vector.tensor_tensor(
                            biased[:, j * GB:(j + 1) * GB, :], src[:, j],
                            near_scores[:, near_tiles.index(t), :, j * GB:(j + 1) * GB].rearrange("p k h -> p h k"), ALU.add)
                    s.after(ins)
                    src = biased[:, :, :].rearrange("p (b h) k -> p b h k", b=SB)
                s.after(nc.vector.tensor_reduce(peak[:, i % 2, :].rearrange("p (b h) -> p b h", b=SB), src, AX.X, ALU.max))
                if i:
                    dve.wait_ge(p_done, i)
                nc.vector.tensor_tensor(
                    shifted[:, :, :].rearrange("p (b h) k -> p b h k", b=SB), src,
                    peak[:, i % 2, :].rearrange("p (b h) -> p b h", b=SB).unsqueeze(3).to_broadcast([P, SB, GB, CTX]),
                    ALU.subtract).then_inc(s_shift, 1)

            def normalise(i):
                dve.wait_ge(pt_used, round_ends[value_order[i]])
                if i:
                    dve.wait_ge(ot_done, i)
                s.after(nc.vector.reciprocal(rsum[:, :], po[:, :, D0]))
                nc.vector.tensor_tensor(O[:, :, :], po[:, :, 0:D0],
                                        rsum[:, :].unsqueeze(2).to_broadcast([P, H0, D0]), ALU.mult).then_inc(o_out, 1)

            def add_outputs(i):
                t = value_order[i]
                dve.wait_ge(y_done, i + 1)
                nc.vector.tensor_tensor(yb[:, :], py[:, E:2 * E], bo[:, :], ALU.add).then_inc(y_out, 1)
                dve.wait_ge(y_out, i + 1)
                s.after(nc.vector.tensor_tensor(xres[:, t, :], xres[:, t, :], yb[:, :], ALU.add))

            shift(0)
            for i in range(TILES):
                if ahead[i]:
                    shift(ahead[i][0])
                if len(ahead[i]) == 2:
                    shift(ahead[i][1])
                if i:
                    add_outputs(i - 1)
                normalise(i)
            add_outputs(TILES - 1)


def route(nc, name, layer, xnT, lists, constants, constants_loaded, refill):
    with phase(nc) as ctx:
        sb = lambda n, s, d=F32: ctx.enter_context(nc.sbuf_tensor(f"{name}_{n}", s, d))
        sem = lambda n: nc.alloc_semaphore(f"{name}_{n}")
        Wr, br, iota, lane, before = constants
        ones = sb("ones", [P, P])
        logits = sb("logits", [P, TILES, NE])
        top = sb("top", [P, TILES, 8])
        topi = sb("topi", [P, TILES, 8], U32)
        pick = sb("pick", [P, TOPK, TILES])
        less = sb("less", [P, TILES, NE])
        ex = sb("ex", [P, TILES, NE])
        gap = sb("gap", [P, TILES])
        second = sb("second", [P, TILES])
        total = sb("total", [P, TILES])
        first = sb("first", [P, TILES])
        M = sb("M", [P, SLOT_COLS, NE])
        scan = [sb(f"scan{i}", [P, SLOT_COLS + 1, NE]) for i in range(2)]
        rank = sb("rank", [P, SLOT_COLS, NE])
        work = sb("work", [P, SLOT_COLS, NE])
        need = sb("need", [P, NE], I32)
        needb = sb("needb", [P, NE], I32)
        base = [sb(f"base{i}", [P, NE + 1]) for i in range(2)]
        pos = sb("pos", [P, SLOT_COLS])
        posi = sb("posi", [P, SLOT_COLS], I32)
        part = sb("part", [P, 2, SLOT_COLS], I32)
        partf = sb("partf", [P, 2, SLOT_COLS])
        row1h = lists["row1h"]
        blk1h = sb("blk1h", [P, SLOT_COLS, 3, BLOCKS], BF16)
        code = sb("code", [P, BLOCKS])
        free = sb("free", [P, BLOCKS])
        wrap = sb("wrap", [P, BLOCKS])
        cmp = sb("cmp", [P, BLOCKS, NE])
        own = sb("own", [P, BLOCKS])
        low = sb("low", [P, BLOCKS])
        unused = sb("unused", [P, BLOCKS])
        rk = sb("rk", [P, SLOT_COLS])
        keep = sb("keep", [P, SLOT_COLS])
        pl = ctx.enter_context(nc.psum_tensor(f"{name}_pl", [P, TILES, NE], F32))
        pp = ctx.enter_context(nc.psum_tensor(f"{name}_pp", [P, 2, SLOT_COLS * NE], F32))
        pinv = ctx.enter_context(nc.psum_tensor(f"{name}_pinv", [P, 3, BLOCKS], F32))
        step, shifted, exps = sem("step"), sem("shifted"), sem("exps")
        logits_done, masks_done, counts_done, hot_done, inverse_done = (
            sem(n) for n in ("logits_done", "masks_done", "counts_done", "hot_done", "inverse_done"))
        block = ctx.enter_context(nc.Block())

        @block.sync
        def _(sp):
            refill(sp, logits_done, inverse_done)

        @block.tensor
        def _(pe):
            pe.wait_ge(*constants_loaded)
            for t in range(TILES):
                for c in range(EC):
                    ins = nc.tensor.matmul(pl[:, t, :], xnT[:, c, t * P:(t + 1) * P], Wr[:, c, :],
                                           start=c == 0, stop=c == EC - 1)
            ins.then_inc(logits_done, 1)
            pe.wait_ge(masks_done, 1)
            m = M[:, :, :].rearrange("p s e -> p (s e)")
            nc.tensor.matmul(pp[:, 0, :], before[:, :], m, start=True, stop=True)
            nc.tensor.matmul(pp[:, 1, :], ones[:, :], m, start=True, stop=True).then_inc(counts_done, 1)
            pe.wait_ge(hot_done, 1)
            for s in range(SLOT_COLS):
                ins = nc.tensor.matmul(pinv[:, :, :], row1h[:, s, :], blk1h[:, s, :, :],
                                       start=s == 0, stop=s == SLOT_COLS - 1)
            ins.then_inc(inverse_done, 1)

        @block.scalar
        def _(act):
            act.wait_ge(shifted, 2)
            nc.scalar.activation(ex[:, :, :], less[:, :, :], ACT.Exp).then_inc(exps, 1)
            nc.scalar.activation(second[:, :], gap[:, :], ACT.Exp).then_inc(exps, 1)

        @block.vector
        def _(dve):
            s = Steps(dve, step)
            v = nc.vector
            s.mark(v.memset(ones[:, :], 1.0))
            for i in range(2):
                s.mark(v.memset(scan[i][:, 0, :], 0.0))
                s.mark(v.memset(base[i][:, 0:1], 0.0))
            dve.wait_ge(*constants_loaded)
            dve.wait_ge(logits_done, 1)
            if layer == 0:
                s.after(v.tensor_tensor(logits[:, :, :], pl[:, :, :], br[:, :].unsqueeze(1).to_broadcast([P, TILES, NE]), ALU.add))
            else:
                s.after(v.tensor_copy(logits[:, :, :], pl[:, :, :]))
            for t in range(TILES):
                s.mark(v.max(top[:, t, :], logits[:, t, :]))
            dve.wait_ge(step, s.n)
            v.tensor_tensor(less[:, :, :], logits[:, :, :], top[:, :, 0:1].to_broadcast([P, TILES, NE]),
                            ALU.subtract).then_inc(shifted, 1)
            v.tensor_tensor(gap[:, :], top[:, :, 1], top[:, :, 0], ALU.subtract).then_inc(shifted, 1)
            for t in range(TILES):
                s.mark(v.max_index(topi[:, t, :], top[:, t, :], logits[:, t, :]))
            dve.wait_ge(step, s.n)
            s.after(v.tensor_copy(pick[:, :, :], topi[:, :, 0:TOPK].rearrange("p t k -> p k t")))
            v.tensor_tensor(M[:, :, :], iota[:, 0:NE].unsqueeze(1).to_broadcast([P, SLOT_COLS, NE]),
                            pick[:, :, :].rearrange("p k t -> p (k t)").unsqueeze(2).to_broadcast([P, SLOT_COLS, NE]),
                            ALU.is_equal).then_inc(masks_done, 1)
            dve.wait_ge(exps, 2)
            s.after(v.tensor_reduce(total[:, :], ex[:, :, :], AX.X, ALU.add))
            s.after(v.reciprocal(first[:, :], total[:, :]))
            if layer == 0:
                s.mark(v.tensor_copy(lists["gates"][:, 0, :], first[:, :]))
                s.mark(v.tensor_tensor(lists["gates"][:, 1, :], second[:, :], first[:, :], ALU.mult))
            else:
                s.after(v.tensor_tensor(second[:, :], second[:, :], first[:, :], ALU.mult))
                s.after(v.scalar_tensor_tensor(total[:, :], first[:, :], 1e-9, second[:, :], ALU.add, ALU.add))
                s.after(v.reciprocal(total[:, :], total[:, :]))
                s.mark(v.tensor_tensor(lists["gates"][:, 0, :], first[:, :], total[:, :], ALU.mult))
                s.mark(v.tensor_tensor(lists["gates"][:, 1, :], second[:, :], total[:, :], ALU.mult))
            dve.wait_ge(counts_done, 1)
            s.after(v.tensor_copy(scan[0][:, 1:, :], pp[:, 1, :].rearrange("p (s e) -> p s e", e=NE)))
            src, k = 0, 1
            while k < SLOT_COLS:
                a, b = scan[src], scan[1 - src]
                s.mark(v.tensor_copy(b[:, 1:1 + k, :], a[:, 1:1 + k, :]))
                s.after(v.tensor_tensor(b[:, 1 + k:, :], a[:, 1 + k:, :], a[:, 1:SLOT_COLS + 1 - k, :], ALU.add))
                src, k = 1 - src, 2 * k
            counted = scan[src]
            s.mark(v.tensor_tensor(rank[:, :, :], pp[:, 0, :].rearrange("p (s e) -> p s e", e=NE),
                                   counted[:, 0:SLOT_COLS, :], ALU.add))
            s.after(v.tensor_scalar(need[:, :], counted[:, SLOT_COLS, :], float(P - 1), None, ALU.add))
            s.after(v.tensor_scalar(needb[:, :], need[:, :], 7, None, ALU.arith_shift_right))
            s.after(v.tensor_copy(base[0][:, 1:], needb[:, :]))
            src, k = 0, 1
            while k < NE:
                a, b = base[src], base[1 - src]
                s.mark(v.tensor_copy(b[:, 1:1 + k], a[:, 1:1 + k]))
                s.after(v.tensor_tensor(b[:, 1 + k:], a[:, 1 + k:], a[:, 1:NE + 1 - k], ALU.add))
                src, k = 1 - src, 2 * k
            start = base[src][:, 0:NE]
            if layer == 1:
                s.after(v.tensor_tensor(work[:, :, :], rank[:, :, :], M[:, :, :], ALU.mult))
                s.after(v.tensor_reduce(rk[:, :], work[:, :, :], AX.X, ALU.add))
                s.after(v.tensor_scalar(keep[:, :], rk[:, :], float(CAPACITY), None, ALU.is_lt))
                g = lists["gates"][:, :, :].rearrange("p k t -> p (k t)")
                s.after(v.tensor_tensor(g, g, keep[:, :], ALU.mult))
            s.after(v.scalar_tensor_tensor(rank[:, :, :], start.unsqueeze(1).to_broadcast([P, SLOT_COLS, NE]), float(P),
                                           rank[:, :, :], ALU.mult, ALU.add))
            s.after(v.tensor_tensor(work[:, :, :], rank[:, :, :], M[:, :, :], ALU.mult))
            s.after(v.tensor_reduce(pos[:, :], work[:, :, :], AX.X, ALU.add))
            s.after(v.tensor_copy(posi[:, :], pos[:, :]))
            s.mark(v.tensor_scalar(part[:, 0, :], posi[:, :], P - 1, None, ALU.bitwise_and))
            s.after(v.tensor_scalar(part[:, 1, :], posi[:, :], 7, None, ALU.arith_shift_right))
            s.after(v.tensor_copy(partf[:, :, :], part[:, :, :]))
            s.mark(v.tensor_tensor(row1h[:, :, :], iota[:, :].unsqueeze(1).to_broadcast([P, SLOT_COLS, P]),
                                   partf[:, 0, :].unsqueeze(2).to_broadcast([P, SLOT_COLS, P]), ALU.is_equal))
            s.after(v.tensor_tensor(blk1h[:, :, 2, :], iota[:, 0:BLOCKS].unsqueeze(1).to_broadcast([P, SLOT_COLS, BLOCKS]),
                                    partf[:, 1, :].unsqueeze(2).to_broadcast([P, SLOT_COLS, BLOCKS]), ALU.is_equal))
            s.mark(v.tensor_scalar(blk1h[:, :, 1, :], blk1h[:, :, 2, :], lane[:, 0:1], None, ALU.mult))
            s.after(v.tensor_tensor(blk1h[:, :, 0, :], blk1h[:, :, 2, :],
                                    iota[:, 0:SLOT_COLS].unsqueeze(2).to_broadcast([P, SLOT_COLS, BLOCKS]), ALU.mult))
            s.engine.sem_inc(hot_done, 1)
            s.after(v.tensor_tensor(cmp[:, :, :], iota[:, 0:BLOCKS].unsqueeze(2).to_broadcast([P, BLOCKS, NE]),
                                    start.unsqueeze(1).to_broadcast([P, BLOCKS, NE]), ALU.is_ge))
            s.after(v.tensor_reduce(own[:, :], cmp[:, :, :], AX.X, ALU.add))
            s.mark(v.tensor_scalar(lists["expert"][:, :], own[:, :], -1.0, None, ALU.add))
            dve.wait_ge(inverse_done, 1)
            s.mark(v.tensor_scalar(unused[:, :], iota[:, 0:BLOCKS], float(P), lane[:, 1:2], ALU.mult, ALU.add))
            s.mark(v.tensor_scalar(free[:, :], pinv[:, 2, :], -1.0, 1.0, ALU.mult, ALU.add))
            s.after(v.tensor_copy(low[:, :], pinv[:, 1, :]))
            s.after(v.scalar_tensor_tensor(code[:, :], pinv[:, 0, :], float(P), low[:, :], ALU.mult, ALU.add))
            s.after(v.tensor_tensor(free[:, :], free[:, :], unused[:, :], ALU.mult))
            s.mark(v.tensor_tensor(lists["scatter"][:, :], free[:, :], code[:, :], ALU.add))
            s.after(v.tensor_scalar(wrap[:, :], code[:, :], float(TOKENS), -float(TOKENS), ALU.is_ge, ALU.mult))
            s.after(v.tensor_tensor(lists["gather"][:, :], code[:, :], wrap[:, :], ALU.add))


def experts(nc, name, layer, ident, lists, xn_rows, y_rows, up, down, bup, bdown, weights_ready, ff):
    FC = ff // P
    UP = E * 4

    def reached(engine, sem, value):
        if not isinstance(value, int) or value > 0:
            engine.wait_ge(sem, value)

    with phase(nc) as ctx:
        sb = lambda n, s, d=F32: ctx.enter_context(nc.sbuf_tensor(f"{name}_{n}", s, d))
        sem = lambda n: nc.alloc_semaphore(f"{name}_{n}")
        ps = lambda n, s: ctx.enter_context(nc.psum_tensor(f"{name}_{n}", s, F32))
        xg = sb("xg", [P, GATHERS, E])
        xT = sb("xT", [P, EC, P])
        h = sb("h", [P, 2, UP])
        a = sb("a", [P, 2, ff]) if layer == 0 else h
        aT = sb("aT", [P, 2, FC, P])
        y = sb("y", [P, E])
        sig = sb("sig", [P, ff]) if layer == 0 else None
        pxT = ps("pxT", [P, BANK])
        ph = ps("ph", [P, 2, UP])
        paT = ps("paT", [P, max(FC, 4), P])
        py = ps("py", [P, BANK])
        gathered = [sem(f"gathered{q}") for q in range(GATHERS)]
        scattered = sem("scattered")
        xT_done, xT_out, h_done, h_out, a_done, aT_done, aT_out, y_done, y_out = (
            sem(n) for n in ("xT_done", "xT_out", "h_done", "h_out", "a_done", "aT_done", "aT_out", "y_done", "y_out"))
        step, gate_ready, sig_ready = sem("step"), sem("gate_ready"), sem("sig_ready")
        block = ctx.enter_context(nc.Block())

        def steps(engine, body):
            end = BLOCKS - 1
            begin = end % GATHERS + GATHERS
            for s in range(begin):
                body(s, s % GATHERS)
            with engine.Fori(0, (end - begin) // GATHERS) as i:
                for k in range(GATHERS):
                    body(i * GATHERS + (begin + k), (begin + k) % GATHERS)
            for s in range(end, BLOCKS + 2):
                body(s, s % GATHERS)

        def within(b):
            return not isinstance(b, int) or 0 <= b < BLOCKS

        @block.gpsimd
        def _(pool):
            def gather(b):
                if b >= GATHERS:
                    pool.wait_ge(xT_done, b - GATHERS + 1)
                nc.gpsimd.indirect_dma_start(xg[:, b % GATHERS, :], None, xn_rows,
                                             bass.IndirectOffsetOnAxis(ap=lists["gather"][:, b:b + 1], axis=0)
                                             ).then_inc(gathered[b % GATHERS], 16)

            for b in range(GATHERS):
                gather(b)
            for b in range(BLOCKS):
                if b + GATHERS < BLOCKS:
                    gather(b + GATHERS)
                pool.wait_ge(y_out, b + 1)
                nc.gpsimd.indirect_dma_start(y_rows, bass.IndirectOffsetOnAxis(ap=lists["scatter"][:, b:b + 1], axis=0),
                                             y[:, :], None).then_inc(scattered, 16)
            pool.wait_ge(scattered, 16 * BLOCKS)

        @block.tensor
        def _(pe):
            def turn_x(b, r):
                pe.wait_ge(gathered[r], (b - r) * (16 // GATHERS) + 16)
                reached(pe, xT_out, b)
                for c in range(EC):
                    ins = nc.tensor.transpose(pxT[:, c * P:(c + 1) * P], xg[:, r, c * P:(c + 1) * P], ident[:, :])
                ins.then_inc(xT_done, 1)

            def body(s, r):
                q = r % 2
                if isinstance(s, int) and s == 0:
                    turn_x(0, 0)
                    pe.wait_ge(weights_ready[0], weights_ready[1])
                if within(s):
                    e = pe.value_load(lists["expert"][0:1, bass.ds(s, 1)], min_val=0, max_val=NE - 1)
                    pe.wait_ge(xT_out, s + 1)
                    reached(pe, h_out, s - 1)
                    for half in range(UP // BANK):
                        for c in range(EC):
                            cols = slice(half * BANK, (half + 1) * BANK)
                            ins = nc.tensor.matmul(ph[:, q, cols], xT[:, c, :],
                                                   up[:, bass.ds(e, 1), c, cols].rearrange("p a n -> p (a n)"),
                                                   start=c == 0, stop=c == EC - 1)
                    ins.then_inc(h_done, 1)
                if within(s - 1):
                    pe.wait_ge(a_done, s)
                    reached(pe, aT_out, s - 1)
                    for f in range(FC):
                        ins = nc.tensor.transpose(paT[:, f, :], a[:, 1 - q, f * P:(f + 1) * P], ident[:, :])
                    ins.then_inc(aT_done, 1)
                if within(s + 1):
                    turn_x(s + 1, (r + 1) % GATHERS)
                if within(s - 2):
                    e = pe.value_load(lists["expert"][0:1, bass.ds(s - 2, 1)], min_val=0, max_val=NE - 1)
                    pe.wait_ge(aT_out, s - 1)
                    reached(pe, y_out, s - 2)
                    for f in range(FC):
                        ins = nc.tensor.matmul(py[:, 0:E], aT[:, q, f, :],
                                               down[:, bass.ds(e, 1), f, :].rearrange("p a n -> p (a n)"),
                                               start=f == 0, stop=f == FC - 1)
                    ins.then_inc(y_done, 1)

            steps(pe, body)

        @block.scalar
        def _(act):
            def copy_x(b):
                act.wait_ge(xT_done, b + 1)
                reached(act, h_done, b)
                nc.scalar.activation(xT[:, :, :], pxT[:, 0:E].rearrange("p (c n) -> p c n", c=EC), ACT.Copy).then_inc(xT_out, 1)

            def body(s, r):
                q = r % 2
                if isinstance(s, int) and s == 0:
                    copy_x(0)
                if within(s - 1):
                    act.wait_ge(aT_done, s)
                    reached(act, y_done, s - 2)
                    nc.scalar.activation(aT[:, 1 - q, :, :], paT[:, 0:FC, :], ACT.Copy).then_inc(aT_out, 1)
                if within(s + 1):
                    copy_x(s + 1)
                if within(s):
                    if layer == 1:
                        act.wait_ge(h_out, s + 1)
                        nc.scalar.activation(a[:, q, :], h[:, q, :], ACT.Gelu).then_inc(a_done, 1)
                    else:
                        act.wait_ge(gate_ready, s + 1)
                        reached(act, a_done, s)
                        nc.scalar.activation(sig[:, :], h[:, q, 0:ff], ACT.Sigmoid, scale=1.702).then_inc(sig_ready, 1)

            steps(act, body)

        @block.vector
        def _(dve):
            v = nc.vector
            dve.wait_ge(weights_ready[0], weights_ready[1])

            def body(s, r):
                q = r % 2
                if within(s):
                    e = dve.value_load(lists["expert"][0:1, bass.ds(s, 1)], min_val=0, max_val=NE - 1)
                    dve.wait_ge(h_done, s + 1)
                    reached(dve, a_done if layer == 0 else aT_done, s - 1)
                    v.tensor_tensor(h[:, q, :], ph[:, q, :], bup[:, bass.ds(e, 1), :].rearrange("p a n -> p (a n)"),
                                    ALU.add).then_inc(h_out, 1)
                    if layer == 0:
                        dve.wait_ge(h_out, s + 1)
                        v.tensor_scalar(h[:, q, 0:ff], h[:, q, 0:ff], 7.0, None, ALU.min).then_inc(gate_ready, 1)
                        v.tensor_scalar(h[:, q, ff:], h[:, q, ff:], 7.0, -7.0, ALU.min, ALU.max).then_inc(step, 1)
                        dve.wait_ge(sig_ready, s + 1)
                        reached(dve, aT_done, s - 1)
                        v.tensor_tensor(a[:, q, :], h[:, q, 0:ff], sig[:, :], ALU.mult).then_inc(step, 1)
                        dve.wait_ge(step, s * 2 + 2)
                        v.scalar_tensor_tensor(a[:, q, :], h[:, q, ff:], 1.0, a[:, q, :], ALU.add, ALU.mult).then_inc(a_done, 1)
                if within(s - 2):
                    e = dve.value_load(lists["expert"][0:1, bass.ds(s - 2, 1)], min_val=0, max_val=NE - 1)
                    dve.wait_ge(y_done, s - 1)
                    reached(dve, scattered, (s - 2) * 16)
                    v.tensor_tensor(y[:, :], py[:, 0:E], bdown[:, bass.ds(e, 1), :].rearrange("p a n -> p (a n)"),
                                    ALU.add).then_inc(y_out, 1)

            steps(dve, body)


def combine(nc, name, gates, y_rows, xres, out=None):
    with phase(nc) as ctx:
        got = [ctx.enter_context(nc.sbuf_tensor(f"{name}_got{i}", [P, TOPK, E], F32)) for i in range(4)]
        loaded = [nc.alloc_semaphore(f"{name}_loaded{i}") for i in range(4)]
        added, half = nc.alloc_semaphore(f"{name}_added"), nc.alloc_semaphore(f"{name}_half")
        stored = nc.alloc_semaphore(f"{name}_stored")
        rows = y_rows[0:DUMP, :].rearrange("(k t p) e -> t p k e", k=TOPK, p=P)
        block = ctx.enter_context(nc.Block())

        @block.sync
        def _(sp):
            for t in range(TILES):
                if t >= 4:
                    sp.wait_ge(added, t - 3)
                sp.dma_start(got[t % 4][:, :, :], rows[t]).then_inc(loaded[t % 4], 16)

        @block.scalar
        def _(act):
            if out is not None:
                tiles = out.rearrange("b (t p) e -> (b t) p e", p=P)
                for t in range(TILES):
                    act.wait_ge(added, t + 1)
                    act.dma_start(tiles[t], xres[:, t, :]).then_inc(stored, 16)
                act.wait_ge(stored, 16 * TILES)

        @block.vector
        def _(dve):
            for t in range(TILES):
                dve.wait_ge(loaded[t % 4], 16 * (t // 4 + 1))
                nc.vector.scalar_tensor_tensor(xres[:, t, :], got[t % 4][:, 0, :], gates[:, 0, t:t + 1], xres[:, t, :],
                                               ALU.mult, ALU.add).then_inc(half, 1)
                dve.wait_ge(half, t + 1)
                nc.vector.scalar_tensor_tensor(xres[:, t, :], got[t % 4][:, 1, :], gates[:, 1, t:t + 1], xres[:, t, :],
                                               ALU.mult, ALU.add).then_inc(added, 1)


def mixture(nc, I, xres, ident, layer, out=None):
    name = f"m{layer}"
    ff = 512 if layer == 0 else 1024
    FC = ff // P
    wup, wbup, wdown, wbdown = (
        ("L0_ffn_gate_up_proj", "L0_ffn_gate_up_bias", "L0_ffn_down_proj", "L0_ffn_down_bias") if layer == 0 else
        ("L1_ffn_W1", "L1_ffn_b1", "L1_ffn_W2", "L1_ffn_b2"))
    xn_rows = nc.dram_tensor(f"{name}_xn_rows", [TOKENS, E], F32).ap()
    y_rows = nc.dram_tensor(f"{name}_y_rows", [DUMP + BLOCKS * P, E], F32).ap()
    with phase(nc) as ctx:
        gates = ctx.enter_context(nc.sbuf_tensor(f"{name}_gates", [P, TOPK, TILES], F32))
        with ExitStack() as c2:
            sb = lambda n, s, d=F32: c2.enter_context(nc.sbuf_tensor(f"{name}_{n}", s, d))
            sem = lambda n: nc.alloc_semaphore(f"{name}_{n}")
            lists = {"gates": gates, "gather": sb("gather", [P, BLOCKS], U32), "scatter": sb("scatter", [P, BLOCKS], U32),
                     "expert": sb("expert", [P, BLOCKS], I32)}
            constants_loaded, weights_loaded, rows_stored = sem("constants_loaded"), sem("weights_loaded"), sem("rows_stored")
            up = sb("up", [P, NE, EC, E * 4])
            bup, bdown = sb("bup", [P, NE, E * 4]), sb("bdown", [P, NE, E])
            down = sb("down", [P, NE, FC, E])
            c3 = c2.enter_context(ExitStack())
            sb3 = lambda n, s, d=F32: c3.enter_context(nc.sbuf_tensor(f"{name}_{n}", s, d))
            Wr, br = sb3("Wr", [P, EC, NE]), sb3("br", [P, NE])
            iota = sb3("iota", [P, P])
            lane = sb3("lane", [P, 2])
            before = sb3("before", [P, P])
            lent = TILES // FC
            xn = down[:, NE - lent:, :, :].rearrange("p e f n -> p (e f) n")
            xnT = down[:, NE - 2 * lent:NE - lent, :, :].rearrange("p e f n -> p (e f n)").rearrange("p (c t) -> p c t", c=EC)

            lists["row1h"] = bdown[:, :, :].rearrange("p e n -> p (e n)").bitcast(BF16).rearrange("p (s r) -> p s r", r=P)

            def load_down(sp, experts_):
                for e in experts_:
                    sp.dma_start(down[:, e], I[wdown][e].rearrange("(c p) n -> p c n", p=P)).then_inc(weights_loaded, 16)

            def refill(sp, logits_done, inverse_done):
                sp.wait_ge(rows_stored, 16 * TILES)
                load_down(sp, range(NE - lent, NE))
                sp.wait_ge(logits_done, 1)
                load_down(sp, range(NE - 2 * lent, NE - lent))
                sp.wait_ge(inverse_done, 1)
                sp.dma_start(bdown[:, :, :].rearrange("p e n -> p (e n)"),
                             I[wbdown].to_broadcast([P, NE * E])).then_inc(weights_loaded, 16)

            constants = [(Wr[:, :, :], I[f"L{layer}_router"].rearrange("(c p) n -> p c n", p=P)),
                         (iota[:, :], I["iota"].to_broadcast([P, P])), (lane[:, :], I["lane"]), (before[:, :], I["before"])]
            if layer == 0:
                constants.append((br[:, :], I["L0_ffn_router_bias"].to_broadcast([P, NE])))
            with nc.Block() as block:
                @block.sync
                def _(sp):
                    for dst, src in constants:
                        sp.dma_start(dst, src).then_inc(constants_loaded, 16)
                    for e in range(NE):
                        sp.dma_start(up[:, e], I[wup][e].rearrange("(c p) n -> p c n", p=P)).then_inc(weights_loaded, 16)
                    sp.dma_start(bup[:, :, :].rearrange("p e n -> p (e n)"),
                                 I[wbup].to_broadcast([P, NE * E * 4])).then_inc(weights_loaded, 16)
                    load_down(sp, range(NE - 2 * lent))
            layer_norm(nc, f"{name}ln", xres, xn, ident, xnT, store=(xn_rows, rows_stored))
            route(nc, f"{name}r", layer, xnT, lists, (Wr, br, iota, lane, before), (constants_loaded, 16 * len(constants)), refill)
            c3.close()
            experts(nc, f"{name}e", layer, ident, lists, xn_rows, y_rows, up, down, bup, bdown,
                    (weights_loaded, 16 * (2 * NE + 2)), ff)
        combine(nc, f"{name}c", gates, y_rows, xres, out)


class Pair:

    def __init__(self, g, b, hp, parity):
        self.g, self.b, self.hp, self.parity = g, b, hp, parity

    def previous(self):
        return Pair(self.g - 1, self.b, self.hp - 1, 1 - self.parity)

    def next(self):
        if isinstance(self.g, int):
            return Pair(self.g + 1, *divmod(self.g + 1, PAIRS), 1 - self.parity) if self.g + 1 < BATCH * PAIRS else None
        return Pair(self.g + 1, self.b, self.hp + 1, 1 - self.parity)


UNITS = 2 * (SEQ // P)
GROUPS = UNITS // 2


def tile_head(u):
    return u // 4 * 2 + u % 2, u // 2 % 2


PIECES = ["Ka", "Kb", "c", "Qa", "Qb", "Va", "Vb", "K0a", "K0b", "K1a", "K1b", "Kc", "Q0a", "Q1a", "Q0b", "Q1b"]
QUERY_TURNS = ["Q0a", "Q1a", "Q0b", "Q1b"]
COPIED = ["Ka", "Kb", "Qa", "Qb"] + QUERY_TURNS
SPLIT = [p for p in PIECES if p not in COPIED]


def count(pair, step, steps):
    return pair.g * len(steps) + (steps.index(step) + 1)


def ahead(pair, u, by):
    return (pair, u + by) if u + by < UNITS else (pair.next(), u + by - UNITS)


def all_pairs(engine, body):
    for b in range(BATCH):
        with engine.Fori(0, PAIRS // 2 - 1) as i:
            for r in range(2):
                body(Pair(i * 2 + (b * PAIRS + r), b, i * 2 + r, r))
        for hp in (PAIRS - 2, PAIRS - 1):
            body(Pair(b * PAIRS + hp, b, hp, hp % 2))


def layer1_attention(nc, I, xres, ident):
    with phase(nc) as outer:
        o_rows = nc.dram_tensor("a1_o_rows", [TOKENS, H1 * D1], F32).ap()
        OC = H1 * D1 // P
        Wout, bout = (outer.enter_context(nc.sbuf_tensor(f"a1o_{n}", s, F32)) for n, s in (("Wout", [P, OC, E]), ("bout", [P, E])))
        w_out_loaded = nc.alloc_semaphore("a1o_w_out_loaded")
        attn = outer.enter_context(ExitStack())
        sb = lambda n, s, d=F32: attn.enter_context(nc.sbuf_tensor(f"a1_{n}", s, d))
        sem = lambda n: nc.alloc_semaphore(f"a1_{n}")
        latT = sb("latT", [P, EC, TOKENS])
        ctxT = sb("ctxT", [P, EC, BATCH * CTX])
        valid = sb("valid", [CTX, BATCH])
        gamma = sb("gamma", [P, 1])
        maskf = sb("maskf", [P, BATCH, CTX])

        with ExitStack() as c2:
            sb2 = lambda n, s, d=F32: c2.enter_context(nc.sbuf_tensor(f"a1n_{n}", s, d))
            sem2 = lambda n: nc.alloc_semaphore(f"a1n_{n}")
            lat = sb2("lat", [P, TILES, E])
            lat2 = sb2("lat2", [P, TILES, E])
            lng, lnb = sb2("lng", [P, EC]), sb2("lnb", [P, EC])
            cng, cnb = sb2("cng", [P, EC]), sb2("cnb", [P, EC])
            qg, kg = sb2("qg", [P, 1]), sb2("kg", [P, 1])
            mask = sb2("mask", [P, BATCH, CTX], U8)
            maskT = sb2("maskT", [CTX, BATCH], U8)
            maskn = sb2("maskn", [P, BATCH, CTX])
            stand_in = sb2("stand_in", [P, EC, BATCH * CTX])
            c = sb2("c", [CTX, BATCH, E])
            stats, moments = sb2("stats", [CTX, BATCH, 6]), sb2("moments", [CTX, BATCH, 2])
            var, expo, rstd = sb2("var", [CTX, BATCH]), sb2("expo", [CTX, BATCH]), sb2("rstd", [CTX, BATCH])
            cn = sb2("cn", [CTX, BATCH, E])
            pc = c2.enter_context(nc.psum_tensor("a1_pc", [P, EC, BATCH, 128], F32))
            loaded, step, expo_set, var_done, rstd_done = (sem2(n) for n in ("loaded", "step", "expo_set", "var_done", "rstd_done"))
            cn_done, pc_done, ctxT_done, gamma_done = (sem2(n) for n in ("cn_done", "pc_done", "ctxT_done", "gamma_done"))
            with nc.Block() as block:
                @block.sync
                def _(sp):
                    for dst, src in ((lng, "ln_l_g"), (lnb, "ln_l_b"), (cng, "ln_x_g"), (cnb, "ln_x_b")):
                        sp.dma_start(dst[:, :], I[f"L1_xattn_{src}"]).then_inc(loaded, 16)
                    sp.dma_start(qg[:, :], I["L1_xattn_qn_g"]).then_inc(loaded, 16)
                    sp.dma_start(kg[:, :], I["L1_xattn_kn_g"]).then_inc(loaded, 16)
                    sp.dma_start(mask[:, :, :].rearrange("p b k -> p (b k)"),
                                 I["mask"].to_broadcast([P, BATCH * CTX])).then_inc(loaded, 16)
                    sp.dma_start(maskT[:, :], I["maskT"]).then_inc(loaded, 16)
                    sp.dma_start(c[:, :, :], I["ctx"].rearrange("b k e -> k b e")).then_inc(loaded, 16)
                    sp.dma_start(Wout[:, :, :], I["L1_xattn_Wout"].rearrange("(c p) n -> p c n", p=P)).then_inc(w_out_loaded, 16)
                    sp.dma_start(bout[:, :], I["L1_xattn_bout"].to_broadcast([P, E])).then_inc(w_out_loaded, 16)
                    sp.wait_ge(loaded, 144)

                @block.gpsimd
                def _(pool):
                    nc.gpsimd.memset(expo[:, :], -0.5).then_inc(expo_set, 1)
                    pool.wait_ge(expo_set, 1)
                    pool.wait_ge(var_done, 1)
                    nc.gpsimd.tensor_tensor(rstd[:, :], var[:, :], expo[:, :], ALU.pow).then_inc(rstd_done, 1)

                @block.vector
                def _(dve):
                    s = Steps(dve, step)
                    v = nc.vector
                    dve.wait_ge(loaded, 144)
                    s.mark(v.tensor_copy(maskf[:, :, :], mask[:, :, :]))
                    s.mark(v.tensor_scalar(maskn[:, :, :], mask[:, :, :], -1.0, 1.0, ALU.mult, ALU.add))
                    s.mark(v.tensor_copy(valid[:, :], maskT[:, :]))
                    s.mark(v.scalar_tensor_tensor(gamma[:, :], qg[:, :], D1 ** 0.5, kg[:, :], ALU.mult, ALU.mult))
                    for b in range(BATCH):
                        s.after(v.bn_stats(stats[:, b, :], c[:, b, :]))
                        s.after(v.bn_aggr(moments[:, b, :], stats[:, b, :]))
                    assert s.n == 2 * BATCH + 4
                    v.tensor_scalar(var[:, :], moments[:, :, 1], LN_EPS, None, ALU.add).then_inc(var_done, 1)
                    dve.wait_ge(rstd_done, 1)
                    for b in range(BATCH):
                        v.tensor_scalar(cn[:, b, :], c[:, b, :], moments[:, b, 0:1], rstd[:, b:b + 1],
                                        ALU.subtract, ALU.mult).then_inc(cn_done, 1)

                @block.tensor
                def _(pe):
                    pe.wait_ge(cn_done, BATCH)
                    for b in range(BATCH):
                        for e in range(EC):
                            ins = nc.tensor.transpose(pc[:, e, b, 0:CTX], cn[:, b, e * P:(e + 1) * P], ident[0:CTX, 0:CTX])
                    ins.then_inc(pc_done, 1)

                @block.scalar
                def _(act):
                    act.wait_ge(loaded, 144)
                    act.wait_ge(pc_done, 1)
                    for e in range(EC):
                        nc.scalar.activation(ctxT[:, e, :].rearrange("p (b k) -> p b k", b=BATCH), pc[:, e, :, 0:CTX],
                                             ACT.Identity, bias=cnb[:, e:e + 1], scale=cng[:, e:e + 1])
            layer_norm(nc, "a1lat", xres, lat, ident)
            layer_norm(nc, "a1ln", lat, lat2, ident, latT, gain=lng, shift=lnb)
            with nc.Block() as block:
                @block.vector
                def _(dve):
                    s = Steps(dve, step)
                    s.n = 2 * BATCH + 4
                    v = nc.vector
                    for e in range(EC):
                        x = ctxT[:, e, :].rearrange("p (b k) -> p b k", b=BATCH)
                        y = stand_in[:, e, :].rearrange("p (b k) -> p b k", b=BATCH)
                        first = latT[:, e, :].rearrange("p (b s) -> p b s", b=BATCH)[:, :, 0:1].to_broadcast([P, BATCH, CTX])
                        s.mark(v.tensor_tensor(x, x, maskf[:, :, :], ALU.mult))
                        s.after(v.tensor_tensor(y, first, maskn[:, :, :], ALU.mult))
                        s.after(v.tensor_tensor(x, x, y, ALU.add))

        W2 = KEYS + 1
        S = SEQ // P
        KHL = sb("KHL", [P, 2, 2, 2, W2], F32R)
        QHL = sb("QHL", [P, 2, 2, SEQ], F32R)
        VHL = sb("VHL", [P, 2, KT_TILES, 2, 2, D1], F32R)
        W = sb("W", [P, 2, 3, EC, P])
        knat, qnat = sb("knat", [P, KT_TILES, P]), sb("qnat", [P, S, P])
        square = sb("square", [P, KT_TILES, P])
        kvar, qvar = sb("kvar", [P, KT_TILES * 2]), sb("qvar", [P, S * 2])
        kinv, qinv = sb("kinv", [P, KT_TILES * 2]), sb("qinv", [P, S * 2])
        expo = sb("expo", [P, KT_TILES * 2])
        one = sb("one", [P, 1])
        kdup = sb("kdup", [P, KT_TILES, 2, 2, D1])
        qdup = sb("qdup", [P, S, 2, 2, D1])
        qgam = sb("qgam", [P, 2, BANK])
        npeak = sb("npeak", [P, 2])
        prob = sb("prob", [P, 2, KEYS])
        probT = sb("probT", [P, 2, 2, KT_TILES, 2, P], F32R)
        part_peak = sb("part_peak", [P, 2, 2])
        latent_sum = sb("latent_sum", [P, 2])
        masked = sb("masked", [P, CTX])
        rsum = sb("rsum", [P, 4, 2])
        fold = sb("fold", [P, D1])
        OT = sb("OT", [P, 2 * P])
        O = sb("O", [P, 2, S, P])
        slot = [attn.enter_context(nc.psum_tensor(f"a1_slot{i}", [P, 3 * BANK], F32)) for i in range(2)]
        side = attn.enter_context(nc.psum_tensor("a1_side", [P, BANK], F32))
        po = attn.enter_context(nc.psum_tensor("a1_po", [P, BANK], F32))
        po_t, po_n = po[:, 0:2 * P], po[:, 2 * P:2 * P + 2 * D1]
        filled, act_freed, dve_freed = sem("filled"), sem("act_freed"), sem("dve_freed")
        set_up, padded, squared, bounded, powered, scaled, summed = (
            sem(n) for n in ("set_up", "padded", "squared", "bounded", "powered", "scaled", "summed"))
        high, qhigh, qlow, bank_filled, part_peaked, peaked = (
            sem(n) for n in ("high", "qhigh", "qlow", "bank_filled", "part_peaked", "peaked"))
        exped, turned, probT_high, probT_low, row_summed, weighed, OT_out, folded, rsum_done, o_out = (
            sem(n) for n in ("exped", "turned", "probT_high", "probT_low", "row_summed", "weighed", "OT_out", "folded",
                             "rsum_done", "o_out"))
        o_stored = [sem(f"o_stored{i}") for i in range(2)]
        w_loaded = [sem(f"w_loaded{i}") for i in range(2)]
        NSET = 9
        FOLDS = D1.bit_length() - 1
        HALF = S // 2
        block = attn.enter_context(nc.Block())

        @block.sync
        def _(sp):
            def load_weights(b_hp, parity):
                for i, (name, off) in enumerate((("Wq", 0), ("Wkv", 0), ("Wkv", H1 * D1))):
                    src = I[f"L1_xattn_{name}"].rearrange("(c p) n -> p c n", p=P)
                    sp.dma_start(W[:, parity, i, :, :], src[:, :, bass.ds(b_hp * P + off, P)]).then_inc(w_loaded[parity], 16)

            for i in range(2):
                sp.sem_inc(o_stored[i], 16)
                load_weights(i, i)

            def body(pair):
                if not isinstance(pair.g, int) or pair.g + 2 < BATCH * PAIRS:
                    sp.wait_ge(filled, count(pair, PIECES[-1], PIECES))
                    load_weights((pair.hp + 2) % PAIRS if isinstance(pair.g, int) else pair.hp + 2, pair.parity)
                sp.wait_ge(o_out, pair.g * GROUPS + (GROUPS + 2))
                rows = o_rows[pair.b * SEQ:(pair.b + 1) * SEQ, :].rearrange("(t p) n -> p t n", p=P)
                hp = pair.hp
                cols = bass.ds(hp * P, P)
                sp.dma_start(rows[:, :, cols], O[:, pair.parity, :, :]).then_inc(o_stored[pair.parity], 16)

            all_pairs(sp, body)
            for i in range(2):
                sp.wait_ge(o_stored[i], 16 * BATCH * PAIRS // 2 + 16)

        @block.gpsimd
        def _(pool):
            g_ = nc.gpsimd
            g_.memset(expo[:, :], -0.5).then_inc(set_up, 1)
            g_.memset(one[:, :], 1.0).then_inc(set_up, 1)
            g_.memset(knat[:, KT_TILES - 1, :], 0.0).then_inc(set_up, 1)
            g_.memset(VHL[:, 1].bitcast(F32), 0.0).then_inc(set_up, 1)
            g_.memset(probT[:, 1].bitcast(F32), 0.0).then_inc(set_up, 1)
            g_.memset(rsum[:, :, :], 1.0).then_inc(set_up, 1)
            g_.memset(OT[:, :], 0.0).then_inc(set_up, 1)
            pool.wait_ge(set_up, NSET)

            def body(pair, first):
                n = pair.g
                for j, (nat, dup, var, inv, step, last) in enumerate(((knat, kdup, kvar, kinv, "c", "Kc"),
                                                                      (qnat, qdup, qvar, qinv, "Qb", "Q1b"))):
                    tiles = nat.shape[1]
                    if j == 0:
                        pool.wait_ge(high, count(pair, step, SPLIT))
                    else:
                        pool.wait_ge(act_freed, count(pair, step, COPIED))
                    sq = square[:, 0:tiles, :]
                    g_.tensor_tensor(sq, nat[:, :, :], nat[:, :, :], ALU.mult).then_inc(squared, 1)
                    pool.wait_ge(squared, n * 2 + (j + 1))
                    half, folds = sq.rearrange("p t (h d) -> p (t h) d", h=2), FOLDS
                    for k in range(folds):
                        w = D1 >> (k + 1)
                        g_.tensor_tensor(half[:, :, 0:w], half[:, :, 0:w], half[:, :, w:2 * w], ALU.add).then_inc(summed, 1)
                        if k + 1 < folds:
                            pool.wait_ge(summed, (n * 2 + j) * folds + (k + 1))
                    pool.wait_ge(bounded, n * 2 + (j + 1))
                    g_.tensor_tensor(inv[:, :], var[:, :], expo[:, 0:2 * tiles], ALU.pow).then_inc(powered, 1)
                    pool.wait_ge(powered, n * 2 + (j + 1))
                    if not first:
                        pool.wait_ge(filled, count(Pair(pair.g - 1, 0, 0, 0), last, PIECES))
                    for h in range(2):
                        src = nat[:, :, h * D1:(h + 1) * D1]
                        scale = inv[:, :].rearrange("p (t h) -> p t h", h=2)[:, :, h:h + 1].to_broadcast([P, tiles, D1])
                        for d in range(2):
                            ins = g_.tensor_tensor(dup[:, :, h, d, :], src, scale, ALU.mult)
                    ins.then_inc(scaled, 1)
                for k, step in enumerate(QUERY_TURNS):
                    lo = BANK if step.endswith("b") else 0
                    pool.wait_ge(act_freed, count(pair, step, COPIED))
                    q = QHL[:, pair.parity, int(step[1]), lo:lo + BANK]
                    g_.tensor_tensor(q, qgam[:, k % 2, :], one[:, :].to_broadcast([P, BANK]), ALU.mult).then_inc(qhigh, 1)
                    pool.wait_ge(qhigh, n * 4 + (k + 1))
                    g_.tensor_tensor(q[D1:, :], qgam[D1:, k % 2, :], q[D1:, :], ALU.subtract).then_inc(qlow, 1)
                    pool.wait_ge(qlow, n * 4 + (k + 1))

            body(Pair(0, 0, 0, 0), True)
            body(Pair(1, 0, 0, 1), False)
            with pool.Fori(1, BATCH * PAIRS // 2) as i:
                for r in range(2):
                    body(Pair(i * 2 + r, 0, 0, r), False)


        @block.tensor
        def _(pe):
            t_ = nc.tensor

            def project(out, x, i, parity):
                for c in range(EC):
                    ins = t_.matmul(out, x[:, c, :], W[:, parity, i, c, :], start=c == 0, stop=c == EC - 1)
                return ins

            def piece(pair, step):
                k = PIECES.index(step)
                if k or not (isinstance(pair.g, int) and pair.g == 0):
                    before = PIECES[k - 1]
                    owner = pair if k else Pair(pair.g - 1, 0, 0, 0)
                    if before in COPIED:
                        pe.wait_ge(act_freed, count(owner, before, COPIED))
                    else:
                        pe.wait_ge(dve_freed, count(owner, before, SPLIT))
                if k == 0:
                    pe.wait_ge(w_loaded[pair.parity], (pair.g - pair.parity) * 24 + 48)
                b, par = pair.b, pair.parity
                ctx = ctxT[:, :, b * CTX:(b + 1) * CTX]
                lo = HALF if step.endswith("b") else 0
                if step == "c":
                    project(side[0:CTX, 0:P], ctx, 1, par)
                    ins = project(side[0:CTX, P:2 * P], ctx, 2, par)
                elif len(step) == 2 and step != "Kc":
                    for j in range(HALF):
                        t = b * S + lo + j
                        ins = project(side[:, j * P:(j + 1) * P], latT[:, :, t * P:(t + 1) * P], "QKV".index(step[0]), par)
                else:
                    pe.wait_ge(scaled, pair.g * 2 + (1 if step[0] == "K" else 2))
                    dup = kdup if step[0] == "K" else qdup
                    if step == "Kc":
                        for h in range(2):
                            ins = t_.transpose(side[:, h * CTX:(h + 1) * CTX], dup[0:CTX, S, h, :, :].rearrange("p a d -> p (a d)"),
                                               ident[0:CTX, 0:CTX])
                    else:
                        h = int(step[1])
                        for j in range(HALF):
                            ins = t_.transpose(side[:, j * P:(j + 1) * P], dup[:, lo + j, h, :, :].rearrange("p a d -> p (a d)"),
                                               ident[:, :])
                ins.then_inc(filled, 1)

            def score(pair, u):
                out = slot[u % 2]
                t, h = tile_head(u)
                if u == 0:
                    pe.wait_ge(dve_freed, count(pair, "Kc", SPLIT))
                if u % 2 == 0 and t % HALF == 0:
                    pe.wait_ge(qlow, count(pair, QUERY_TURNS[h + t // HALF * 2], QUERY_TURNS))
                q = QHL[:, pair.parity, h, t * P:(t + 1) * P]
                for lo, hi in ((0, BANK), (BANK, SEQ), (SEQ, W2)):
                    for part in range(2):
                        ins = t_.matmul(out[:, lo:hi], q, KHL[:, pair.parity, h, part, lo:hi],
                                        start=part == 0, stop=part == 1)
                    ins.then_inc(bank_filled, 1)

            def turn(pair, u):
                out = slot[u % 2]
                pe.wait_ge(exped, pair.g * UNITS + (u + 1))
                for j in range(S):
                    ins = t_.transpose(out[:, j * P:(j + 1) * P], prob[:, u % 2, j * P:(j + 1) * P], ident[:, :])
                    if j == HALF - 1:
                        ins.then_inc(turned, 1)
                t_.transpose(out[0:CTX, SEQ:SEQ + P], prob[:, u % 2, SEQ:KEYS], ident[:, :]).then_inc(turned, 1)

            def weigh(pair, gi, part):
                if part == 0:
                    pe.wait_ge(probT_low, (pair.g * GROUPS + gi) * 4 + 5)
                    pe.wait_ge(o_out, pair.g * GROUPS + (gi + 2))
                    if gi == 0:
                        pe.wait_ge(dve_freed, count(pair, "Vb", SPLIT))
                for j in range(KT_TILES):
                    rows = P if j < S else CTX
                    ins = t_.matmul(po_t, VHL[0:rows, pair.parity, j, gi % 2, :, :].rearrange("p a d -> p (a d)"),
                                    probT[0:rows, gi % 2, part, j, :, :].rearrange("p t q -> p (t q)"),
                                    start=part == 0 and j == 0, stop=part == 1 and j == S)
                if part == 1:
                    ins.then_inc(weighed, 1)

            def fold_outputs(pair, gi):
                pe.wait_ge(OT_out, pair.g * GROUPS + (gi + 3))
                for i in range(2):
                    ins = t_.matmul(po_n[:, i * D1:(i + 1) * D1], OT[:, i * P:(i + 1) * P], fold[:, :], start=True, stop=True)
                ins.then_inc(folded, 1)

            start = Pair(0, 0, 0, 0)
            for step in PIECES:
                piece(start, step)
            pe.wait_ge(padded, 10)
            score(start, 0)
            score(start, 1)
            pe.wait_ge(set_up, NSET)

            def body(pair):
                after, before = pair.next(), pair.previous()
                for u in range(UNITS):
                    turn(pair, u)
                    if u % 2 == 0:
                        fold_outputs(*(pair, u // 2 - 2) if u >= 4 else (before, u // 2 - 2 + GROUPS))
                    if after:
                        piece(after, PIECES[u])
                    weigh(*(pair, u // 2 - 1) if u >= 2 else (before, GROUPS - 1), u % 2)
                    nxt = ahead(pair, u, 2)
                    if nxt[0]:
                        pe.wait_ge(probT_low, (pair.g * UNITS + u) * 2 + 3)
                        score(*nxt)

            all_pairs(pe, body)
            last = Pair(BATCH * PAIRS - 1, BATCH - 1, PAIRS - 1, (PAIRS - 1) % 2)
            fold_outputs(last, GROUPS - 2)
            for part in range(2):
                weigh(last, GROUPS - 1, part)
            fold_outputs(last, GROUPS - 1)

        @block.scalar
        def _(act):
            a_ = nc.scalar
            act.sem_inc(OT_out, 1)

            def piece(pair, step):
                act.wait_ge(filled, count(pair, step, PIECES))
                first = isinstance(pair.g, int) and pair.g == 0
                lo = HALF if step.endswith("b") else 0
                half = side[:, :].rearrange("p (t h d) -> p t h d", h=2, d=D1)
                V = VHL[:, pair.parity]
                K = knat[:, :, :].rearrange("p t (h d) -> p t h d", h=2)
                Q = qnat[:, :, :].rearrange("p t (h d) -> p t h d", h=2)
                if step in ("Ka", "Qa"):
                    if first:
                        act.wait_ge(set_up, NSET)
                    else:
                        act.wait_ge(scaled, pair.g * 2 - (1 if step == "Ka" else 0))
                if step in QUERY_TURNS:
                    k = QUERY_TURNS.index(step)
                    if k >= 2 or not first:
                        act.wait_ge(qlow, count(pair, step, QUERY_TURNS) - 2)
                    a_.activation(qgam[:, k % 2, :], side[:, :], ACT.Copy, scale=gamma[:, 0:1]).then_inc(act_freed, 1)
                elif step in COPIED:
                    a_.activation((K if step[0] == "K" else Q)[:, lo:lo + HALF], half, ACT.Copy).then_inc(act_freed, 1)
                elif step == "c":
                    a_.activation(K[0:CTX, S], half[0:CTX, 0], ACT.Copy)
                    a_.activation(V[0:CTX, S, :, 0], half[0:CTX, 1], ACT.Identity,
                                  scale=valid[:, pair.b:pair.b + 1]).then_inc(high, 1)
                elif step[0] == "V":
                    a_.activation(V[:, lo:lo + HALF, :, 0], half, ACT.Copy).then_inc(high, 1)
                elif step == "Kc":
                    a_.activation(KHL[:, pair.parity, :, 0, SEQ:KEYS], side[:, 0:2 * CTX].rearrange("p (h k) -> p h k", h=2),
                                  ACT.Copy).then_inc(high, 1)
                else:
                    a_.activation(KHL[:, pair.parity, int(step[1]), 0, lo * P:lo * P + BANK], side[:, :], ACT.Copy).then_inc(high, 1)

            def exponentials(pair, u):
                act.wait_ge(peaked, pair.g * UNITS + (u + 1))
                bias = npeak[:, u % 2:u % 2 + 1]
                a_.activation(prob[:, u % 2, 0:SEQ], slot[u % 2][:, 0:SEQ], ACT.Exp, bias=bias, accum_out=latent_sum[:, u % 2:u % 2 + 1])
                a_.activation(prob[:, u % 2, SEQ:KEYS], slot[u % 2][:, SEQ:KEYS], ACT.Exp, bias=bias).then_inc(exped, 1)

            def copy_high(pair, u):
                n = (pair.g * UNITS + u) * 2
                for i, (lo, hi) in enumerate(((0, HALF), (HALF, KT_TILES))):
                    act.wait_ge(turned, n + (i + 1))
                    a_.activation(probT[:, u // 2 % 2, 0, lo:hi, u % 2, :], slot[u % 2][:, lo * P:hi * P].rearrange("p (t q) -> p t q", q=P),
                                  ACT.Copy).then_inc(probT_high, 1)

            def copy_outputs(pair, gi):
                act.wait_ge(weighed, pair.g * GROUPS + (gi + 2))
                a_.activation(OT[:, :], po_t, ACT.Copy).then_inc(OT_out, 1)

            start = Pair(0, 0, 0, 0)
            for step in PIECES:
                piece(start, step)
            exponentials(start, 0)

            def body(pair):
                after, before = pair.next(), pair.previous()
                for u in range(UNITS):
                    copy_high(pair, u)
                    early = after and PIECES[u] in ("K0a", "K0b", "Kc", "K1a", "K1b")
                    if early:
                        piece(after, PIECES[u])
                    nxt = ahead(pair, u, 1)
                    if nxt[0]:
                        exponentials(*nxt)
                    if after and not early:
                        piece(after, PIECES[u])
                    if u % 2:
                        copy_outputs(*(pair, u // 2 - 1) if u >= 2 else (before, GROUPS - 1))

            all_pairs(act, body)
            copy_outputs(Pair(BATCH * PAIRS - 1, 0, 0, 0), GROUPS - 1)

        @block.vector
        def _(dve):
            v = nc.vector
            dve.sem_inc(probT_low, 1)
            dve.sem_inc(rsum_done, 1)
            dve.sem_inc(row_summed, 5)
            for h in range(2):
                rows = slice(h * D1, (h + 1) * D1)
                v.tensor_copy(fold[rows, :], ident[rows, rows]).then_inc(set_up, 1)
            dve.wait_ge(set_up, NSET)
            for p in range(2):
                for h in range(2):
                    for part in range(2):
                        v.memset(KHL[:, p, h, part, KEYS:W2].bitcast(F32), 0.0).then_inc(padded, 1)
            for i in range(2):
                v.memset(slot[i][:, 2 * BANK:], 0.0).then_inc(padded, 1)

            def peak(pair, u):
                n = (pair.g * UNITS + u) * 3
                part = part_peak[:, u % 2, :]
                for i, (lo, hi, banks) in enumerate(((0, BANK, 1), (BANK, KEYS, 3))):
                    dve.wait_ge(bank_filled, n + banks)
                    v.tensor_reduce(part[:, i:i + 1], slot[u % 2][:, lo:hi], AX.X, ALU.max).then_inc(part_peaked, 1)
                dve.wait_ge(part_peaked, (pair.g * UNITS + u) * 2 + 2)
                v.tensor_reduce(npeak[:, u % 2:u % 2 + 1], part, AX.X, ALU.max, negate=True).then_inc(peaked, 1)

            def piece(pair, step):
                lo = HALF if step.endswith("b") else 0
                if step in SPLIT:
                    dve.wait_ge(high, count(pair, step, SPLIT))
                    if step == "Kc":
                        K, src = KHL[:, pair.parity, :, :, SEQ:KEYS], side[:, 0:2 * CTX].rearrange("p (h k) -> p h k", h=2)
                        ins = v.tensor_tensor(K[:, :, 1], src, K[:, :, 0], ALU.subtract)
                    elif step == "c":
                        V = VHL[0:CTX, pair.parity, S]
                        src = side[0:CTX, P:2 * P].rearrange("p (h d) -> p h d", h=2)
                        ins = v.scalar_tensor_tensor(V[:, :, 1], src, valid[:, pair.b:pair.b + 1], V[:, :, 0], ALU.mult, ALU.subtract)
                    elif step[0] == "V":
                        V = VHL[:, pair.parity, lo:lo + HALF]
                        src = side[:, :].rearrange("p (t h d) -> p t h d", h=2, d=D1)
                        ins = v.tensor_tensor(V[:, :, :, 1], src, V[:, :, :, 0], ALU.subtract)
                    else:
                        K = KHL[:, pair.parity, int(step[1]), :, lo * P:lo * P + BANK]
                        ins = v.tensor_tensor(K[:, 1], side[:, :], K[:, 0], ALU.subtract)
                    ins.then_inc(dve_freed, 1)

            def bound(pair, step):
                if step in ("Qb", "K0b"):
                    j = int(step == "K0b")
                    var = (kvar, qvar)[j]
                    dve.wait_ge(summed, pair.g * (2 * FOLDS) + (j + 1) * FOLDS)
                    sums = square[:, 0:(KT_TILES, S)[j], :].rearrange("p t (h d) -> p (t h) d", h=2)
                    v.tensor_scalar(var[:, :], sums[:, :, 0], D1 * 1e-16, None, ALU.max).then_inc(bounded, 1)

            def row_sum(pair, u):
                n = pair.g * UNITS + u
                dve.wait_ge(exped, n + 1)
                dve.wait_ge(row_summed, n + 5)
                v.tensor_tensor_reduce(masked[:, :], prob[:, u % 2, SEQ:KEYS], maskf[:, pair.b, :], 1.0,
                                       latent_sum[:, u % 2:u % 2 + 1], ALU.mult, ALU.add,
                                       accum_out=rsum[:, u // 2 % 4, u % 2:u % 2 + 1]).then_inc(row_summed, 1)

            def copy_low(pair, u, i):
                lo, hi = ((0, HALF), (HALF, KT_TILES))[i]
                dve.wait_ge(probT_high, (pair.g * UNITS + u) * 2 + (i + 1))
                pT = probT[:, u // 2 % 2, :, lo:hi, u % 2, :]
                v.tensor_tensor(pT[:, 1], slot[u % 2][:, lo * P:hi * P].rearrange("p (t q) -> p t q", q=P), pT[:, 0],
                                ALU.subtract).then_inc(probT_low, 1)

            def invert(pair, gi):
                r = rsum[:, gi % 4, :]
                dve.wait_ge(row_summed, (pair.g * GROUPS + gi) * 2 + 7)
                v.reciprocal(r, r).then_inc(rsum_done, 1)

            def normalise(pair, gi):
                n = pair.g * GROUPS + (gi + 3)
                r = rsum[:, gi % 4, :]
                dve.wait_ge(rsum_done, n)
                dve.wait_ge(folded, n)
                if gi == 0:
                    dve.wait_ge(o_stored[pair.parity], (pair.g - pair.parity) * 8 + 16)
                t, h = tile_head(2 * gi)
                v.tensor_tensor(O[:, pair.parity, t:t + 2, h * D1:(h + 1) * D1], po_n.rearrange("p (t d) -> p t d", t=2),
                                r.unsqueeze(2).to_broadcast([P, 2, D1]), ALU.mult).then_inc(o_out, 1)

            start = Pair(0, 0, 0, 0)
            for step in PIECES:
                piece(start, step)
                bound(start, step)
            peak(start, 0)
            peak(start, 1)

            def body(pair):
                after, before = pair.next(), pair.previous()
                for u in range(UNITS):
                    if u % 2 == 0:
                        normalise(*(pair, u // 2 - 2) if u >= 4 else (before, u // 2 - 2 + GROUPS))
                    copy_low(pair, u, 0)
                    copy_low(pair, u, 1)
                    row_sum(pair, u)
                    if u % 2:
                        invert(*(pair, u // 2 - 1) if u >= 2 else (before, GROUPS - 1))
                    if after:
                        piece(after, PIECES[u])
                    nxt = ahead(pair, u, 2)
                    if nxt[0]:
                        peak(*nxt)
                    if after:
                        bound(after, PIECES[u])

            all_pairs(dve, body)
            last = Pair(BATCH * PAIRS - 1, 0, 0, (PAIRS - 1) % 2)
            invert(last, GROUPS - 1)
            normalise(last, GROUPS - 2)
            normalise(last, GROUPS - 1)
        attn.close()

        with ExitStack() as c3:
            sb3 = lambda n, s, d=F32: c3.enter_context(nc.sbuf_tensor(f"a1o_{n}", s, d))
            sem3 = lambda n: nc.alloc_semaphore(f"a1o_{n}")
            o = sb3("o", [P, 4, H1 * D1])
            oT = sb3("oT", [P, 2, OC, P])
            yb = sb3("yb", [P, 2, E])
            pT = [c3.enter_context(nc.psum_tensor(f"a1o_pT{i}", [P, OC, P], F32)) for i in range(2)]
            py = [c3.enter_context(nc.psum_tensor(f"a1o_py{i}", [P, BANK], F32)) for i in range(2)]
            t_done, t_out, y_done, y_out, added = (sem3(n) for n in ("t_done", "t_out", "y_done", "y_out", "added"))
            o_loaded = [sem3(f"o_loaded{i}") for i in range(4)]
            with nc.Block() as block:
                @block.sync
                def _(sp):
                    for t in range(TILES):
                        if t >= 4:
                            sp.wait_ge(t_done, t - 3)
                        sp.dma_start(o[:, t % 4, :], o_rows[t * P:(t + 1) * P, :]).then_inc(o_loaded[t % 4], 16)

                @block.tensor
                def _(pe):
                    def project(t):
                        pe.wait_ge(t_out, t + 1)
                        if t >= 2:
                            pe.wait_ge(y_out, t - 1)
                        for c in range(OC):
                            ins = nc.tensor.matmul(py[t % 2][:, 0:E], oT[:, t % 2, c, :], Wout[:, c, :],
                                                   start=c == 0, stop=c == OC - 1)
                        ins.then_inc(y_done, 1)

                    pe.wait_ge(w_out_loaded, 32)
                    for t in range(TILES):
                        pe.wait_ge(o_loaded[t % 4], 16 * (t // 4 + 1))
                        if t >= 2:
                            pe.wait_ge(t_out, t - 1)
                        for c in range(OC):
                            ins = nc.tensor.transpose(pT[t % 2][:, c, :], o[:, t % 4, c * P:(c + 1) * P], ident[:, :])
                        ins.then_inc(t_done, 1)
                        if t:
                            project(t - 1)
                    project(TILES - 1)

                @block.scalar
                def _(act):
                    for t in range(TILES):
                        act.wait_ge(t_done, t + 1)
                        if t >= 2:
                            act.wait_ge(y_done, t - 1)
                        nc.scalar.activation(oT[:, t % 2, :, :], pT[t % 2][:, :, :], ACT.Copy).then_inc(t_out, 1)

                @block.vector
                def _(dve):
                    dve.wait_ge(w_out_loaded, 32)
                    for t in range(TILES):
                        dve.wait_ge(y_done, t + 1)
                        if t >= 2:
                            dve.wait_ge(added, t - 1)
                        nc.vector.tensor_tensor(yb[:, t % 2, :], py[t % 2][:, 0:E], bout[:, :], ALU.add).then_inc(y_out, 1)
                        dve.wait_ge(y_out, t + 1)
                        nc.vector.tensor_tensor(xres[:, t, :], xres[:, t, :], yb[:, t % 2, :], ALU.add).then_inc(added, 1)
                    dve.wait_ge(added, TILES)


def layer0_mixture(nc, I, xres, ident):
    mixture(nc, I, xres, ident, 0)


def layer1_mixture(nc, I, xres, ident, out=None):
    mixture(nc, I, xres, ident, 1, out)


PHASES = [layer0_attention, layer0_mixture, layer1_attention, layer1_mixture]


def lay_out(inputs):
    a = {n: np.asarray(v) for n, v in inputs.items()}
    out = {"x": a["x"], "ident": np.eye(P, dtype=np.float32)}
    for n in ("Wq", "Wk", "Wv", "Wo"):
        out[f"L0_xattn_{n}T"] = a[f"L0_xattn_{n}"].T
    out["ctxT"] = a["ctx_1024"].reshape(BATCH * CTX, E).T
    for n in ("bq", "bk"):
        out[f"L0_xattn_{n}"] = a[f"L0_xattn_{n}"].reshape(EC, P).T
    for n in ("bv", "bo"):
        out[f"L0_xattn_{n}"] = a[f"L0_xattn_{n}"].reshape(1, E)
    out["head_mask"] = (np.arange(P)[:, None] // D0 == np.arange(GROUP)).astype(np.float32)
    rows = np.clip(np.arange(BAND)[None, :] - (P - 1) - P * np.arange(NEAR)[:, None], -REACH, REACH) + REACH
    out["rel_k"] = np.tile(np.moveaxis(a["L0_xattn_rk_table"][rows], 2, 0), (GROUP, 1, 1))
    out["rel_v"] = a["L0_xattn_rv_table"][rows].reshape(NEAR, 2, BAND // 2, D0).transpose(2, 0, 1, 3)
    out["rv_far"] = np.tile(a["L0_xattn_rv_table"][0], H0)[None, :]
    out["iota"] = np.arange(P, dtype=np.float32)[None, :]
    out["lane"] = np.stack([np.arange(P), DUMP + np.arange(P)], 1).astype(np.float32)
    out["before"] = np.triu(np.ones((P, P), np.float32), 1)
    out["L0_router"] = a["L0_ffn_router_weight"].T
    out["L0_ffn_router_bias"] = a["L0_ffn_router_bias"][None, :]
    out["L1_router"] = a["L1_ffn_Wg"]
    for n in ("L0_ffn_gate_up_proj", "L0_ffn_down_proj", "L1_ffn_W1", "L1_ffn_W2"):
        out[n] = a[n]
    for n in ("L0_ffn_gate_up_bias", "L0_ffn_down_bias", "L1_ffn_b1", "L1_ffn_b2"):
        out[n] = a[n].reshape(1, -1)
    for n in ("ln_x_g", "ln_x_b", "ln_l_g", "ln_l_b"):
        out[f"L1_xattn_{n}"] = a[f"L1_xattn_{n}"].reshape(EC, P).T
    for n in ("qn_g", "kn_g"):
        out[f"L1_xattn_{n}"] = np.tile(a[f"L1_xattn_{n}"], 2)[:, None]
    out["mask"] = a["mask_BxS2_bf1"].reshape(1, -1).view(np.uint8)
    out["maskT"] = a["mask_BxS2_bf1"].T.view(np.uint8)
    out["ctx"] = a["ctx_1024"]
    for n in ("Wq", "Wkv", "Wout"):
        out[f"L1_xattn_{n}"] = a[f"L1_xattn_{n}"]
    out["L1_xattn_bout"] = a["L1_xattn_bout"][None, :]
    return {n: np.ascontiguousarray(v) for n, v in out.items()}


def program(nc, I, out):
    with ExitStack() as ctx:
        xres = ctx.enter_context(nc.sbuf_tensor("xres", [P, TILES, E], F32))
        ident = ctx.enter_context(nc.sbuf_tensor("ident", [P, P], F32))
        load_residual(nc, I["x"], I["ident"], xres, ident)
        layer0_attention(nc, I, xres, ident)
        layer0_mixture(nc, I, xres, ident)
        layer1_attention(nc, I, xres, ident)
        layer1_mixture(nc, I, xres, ident, out)


def kernel(**inputs):
    import concourse.bacc as bacc
    from concourse.bass_utils import run_bass_kernel_spmd

    nc = bacc.Bacc("TRN2", target_bir_lowering=False, num_devices=1)
    arrays = {f"in_{n}_dram": v for n, v in lay_out(inputs).items()}
    aps = {n[3:-5]: nc.dram_tensor(n, v.shape, mybir.dt.from_np(v.dtype), kind="ExternalInput").ap()
           for n, v in arrays.items()}
    out = nc.dram_tensor("out_0_dram", (BATCH, SEQ, E), F32, kind="ExternalOutput").ap()
    program(nc, aps, out)
    r = run_bass_kernel_spmd(nc, [arrays], core_ids=[0])
    return r.results[0]["out_0_dram"]
```
